# Optimizing a Trainium2 kernel written in Bass

```python
import numpy as np
import jax
import jax.numpy as jnp

def _softmax(x, axis=-1):
    return jax.nn.softmax(x, axis=axis)

def _gelu(x):
    return jax.nn.gelu(x, approximate=True)

def _silu(x):
    return jax.nn.silu(x)

def _sigmoid(x):
    return jax.nn.sigmoid(x)

def _layernorm(x, axis=-1, eps=1e-05):
    m = jnp.mean(x, axis=axis, keepdims=True)
    v = jnp.var(x, axis=axis, keepdims=True)
    return (x - m) / jnp.sqrt(v + eps)

def _scatter_add(tgt, idx, src, axis=0):
    return tgt.at[idx].add(src)

def _segment_sum(src, seg, n):
    return jax.ops.segment_sum(src, seg, n)
kernel_name = 'mk_prb_d1_jaxref_r4_9c056c'

def setup_inputs(seed: int=0):
    np.random.seed(seed)
    _w = jnp.asarray

    def _L0_attn_setup():
        import jax, jax.numpy as jnp
        import numpy as np
        from jax import lax
        D_MODEL = 256
        D_STATE = 16
        D_CONV = 4
        EXPAND = 2
        D_INNER = EXPAND * D_MODEL
        DT_RANK = (D_MODEL + 15) // 16
        D_FF = 4 * D_MODEL
        B, L = (4, 512)

        def _layer_norm(x, g, b, eps=1e-05):
            mu = jnp.mean(x, axis=-1, keepdims=True)
            var = jnp.mean(jnp.square(x - mu), axis=-1, keepdims=True)
            return (x - mu) * lax.rsqrt(var + eps) * g + b

        def _silu(x):
            return x * jax.nn.sigmoid(x)

        def _mamba(x, in_proj_w, conv_w, conv_b, x_proj_w, dt_proj_w, dt_proj_b, A_log, D, out_proj_w):
            xz = x @ in_proj_w
            xi, z = jnp.split(xz, 2, axis=-1)
            xc = lax.conv_general_dilated(xi.transpose(0, 2, 1), conv_w, window_strides=(1,), padding=[(D_CONV - 1, 0)], feature_group_count=D_INNER, dimension_numbers=('NCH', 'OIH', 'NCH'))
            xc = _silu(xc + conv_b[None, :, None]).transpose(0, 2, 1)
            x_dbl = xc @ x_proj_w
            dt, Bm, Cm = jnp.split(x_dbl, [DT_RANK, DT_RANK + D_STATE], axis=-1)
            dt = jax.nn.softplus(dt @ dt_proj_w + dt_proj_b)
            A = -jnp.exp(A_log)

            def step(h, inp):
                dt_t, B_t, C_t, x_t = inp
                dA = jnp.exp(dt_t[..., None] * A)
                h = dA * h + dt_t[..., None] * B_t[:, None, :] * x_t[..., None]
                y = jnp.sum(h * C_t[:, None, :], axis=-1)
                return (h, y)
            h0 = jnp.zeros((x.shape[0], D_INNER, D_STATE), x.dtype)
            xs = (dt.transpose(1, 0, 2), Bm.transpose(1, 0, 2), Cm.transpose(1, 0, 2), xc.transpose(1, 0, 2))
            _, ys = lax.scan(step, h0, xs)
            y = ys.transpose(1, 0, 2) + D * xc
            y = y * _silu(z)
            return y @ out_proj_w
        key = jax.random.key(seed)
        ks = jax.random.split(key, 16)
        s = 0.02
        inp = {'x': jax.random.normal(ks[0], (B, L, D_MODEL), dtype=jnp.float32), 'ln1_g': jnp.ones((D_MODEL,), jnp.float32), 'ln1_b': jnp.zeros((D_MODEL,), jnp.float32), 'in_proj_w': jax.random.normal(ks[1], (D_MODEL, 2 * D_INNER), jnp.float32) * s, 'conv_w': jax.random.normal(ks[2], (D_INNER, 1, D_CONV), jnp.float32) * s, 'conv_b': jnp.zeros((D_INNER,), jnp.float32), 'x_proj_w': jax.random.normal(ks[3], (D_INNER, DT_RANK + 2 * D_STATE), jnp.float32) * s, 'dt_proj_w': jax.random.normal(ks[4], (DT_RANK, D_INNER), jnp.float32) * s, 'dt_proj_b': jax.random.uniform(ks[5], (D_INNER,), jnp.float32, -4.0, -2.0), 'A_log': jnp.log(jnp.broadcast_to(jnp.arange(1, D_STATE + 1, dtype=jnp.float32), (D_INNER, D_STATE))), 'D': jnp.ones((D_INNER,), jnp.float32), 'out_proj_w': jax.random.normal(ks[6], (D_INNER, D_MODEL), jnp.float32) * s, 'ln2_g': jnp.ones((D_MODEL,), jnp.float32), 'ln2_b': jnp.zeros((D_MODEL,), jnp.float32), 'ffn_w1': jax.random.normal(ks[7], (D_MODEL, D_FF), jnp.float32) * s, 'ffn_b1': jnp.zeros((D_FF,), jnp.float32), 'ffn_w2': jax.random.normal(ks[8], (D_FF, D_MODEL), jnp.float32) * s, 'ffn_b2': jnp.zeros((D_MODEL,), jnp.float32)}
        return inp
    _L0_attn_in = _L0_attn_setup()

    def _L0_ffn_setup():
        import jax, jax.numpy as jnp
        import numpy as np
        S, B, D = (256, 2, 256)
        E, TOPK = (15, 3)
        F = 256
        FS = 512

        def _uinit(k, shape, out_dim):
            std = out_dim ** (-0.5)
            return jax.random.uniform(k, shape, jnp.float32, -std, std)
        key = jax.random.key(seed)
        ks = jax.random.split(key, 10)
        return {'x': jax.random.normal(ks[0], (S, B, D), jnp.float32), 'gate_w': jax.random.normal(ks[1], (E, D), jnp.float32) * D ** (-0.5), 'fc1_w': _uinit(ks[2], (E, 2 * F, D), 2 * F), 'fc1_b': _uinit(ks[3], (E, 2 * F), 2 * F), 'geglu_mult': jnp.ones((E, F), jnp.float32), 'fc2_w': _uinit(ks[4], (E, D, F), D), 'fc2_b': _uinit(ks[5], (E, D), D), 's_fc1_w': _uinit(ks[6], (2 * FS, D), 2 * FS), 's_fc1_b': _uinit(ks[7], (2 * FS,), 2 * FS), 's_geglu_mult': jnp.ones((FS,), jnp.float32), 's_fc2_w': _uinit(ks[8], (D, FS), D), 's_fc2_b': _uinit(ks[9], (D,), D)}
    _L0_ffn_in = _L0_ffn_setup()
    _d = {'L0_attn_x': _L0_attn_in['x'], 'L0_attn_ln1_g': _L0_attn_in['ln1_g'], 'L0_attn_ln1_b': _L0_attn_in['ln1_b'], 'L0_attn_in_proj_w': _L0_attn_in['in_proj_w'], 'L0_attn_conv_w': _L0_attn_in['conv_w'], 'L0_attn_conv_b': _L0_attn_in['conv_b'], 'L0_attn_x_proj_w': _L0_attn_in['x_proj_w'], 'L0_attn_dt_proj_w': _L0_attn_in['dt_proj_w'], 'L0_attn_dt_proj_b': _L0_attn_in['dt_proj_b'], 'L0_attn_A_log': _L0_attn_in['A_log'], 'L0_attn_D': _L0_attn_in['D'], 'L0_attn_out_proj_w': _L0_attn_in['out_proj_w'], 'L0_attn_ln2_g': _L0_attn_in['ln2_g'], 'L0_attn_ln2_b': _L0_attn_in['ln2_b'], 'L0_attn_ffn_w1': _L0_attn_in['ffn_w1'], 'L0_attn_ffn_b1': _L0_attn_in['ffn_b1'], 'L0_attn_ffn_w2': _L0_attn_in['ffn_w2'], 'L0_attn_ffn_b2': _L0_attn_in['ffn_b2'], 'L0_ffn_gate_w': _L0_ffn_in['gate_w'], 'L0_ffn_fc1_w': _L0_ffn_in['fc1_w'], 'L0_ffn_fc1_b': _L0_ffn_in['fc1_b'], 'L0_ffn_geglu_mult': _L0_ffn_in['geglu_mult'], 'L0_ffn_fc2_w': _L0_ffn_in['fc2_w'], 'L0_ffn_fc2_b': _L0_ffn_in['fc2_b'], 'L0_ffn_s_fc1_w': _L0_ffn_in['s_fc1_w'], 'L0_ffn_s_fc1_b': _L0_ffn_in['s_fc1_b'], 'L0_ffn_s_geglu_mult': _L0_ffn_in['s_geglu_mult'], 'L0_ffn_s_fc2_w': _L0_ffn_in['s_fc2_w'], 'L0_ffn_s_fc2_b': _L0_ffn_in['s_fc2_b']}
    _x0 = _d['L0_attn_x']
    _d['L0_attn_x'] = jax.random.normal(jax.random.fold_in(jax.random.key(seed), 1), (2, 2048, 256), dtype=_x0.dtype)
    del _x0
    return _d

def reference(L0_attn_x, L0_attn_ln1_g, L0_attn_ln1_b, L0_attn_in_proj_w, L0_attn_conv_w, L0_attn_conv_b, L0_attn_x_proj_w, L0_attn_dt_proj_w, L0_attn_dt_proj_b, L0_attn_A_log, L0_attn_D, L0_attn_out_proj_w, L0_attn_ln2_g, L0_attn_ln2_b, L0_attn_ffn_w1, L0_attn_ffn_b1, L0_attn_ffn_w2, L0_attn_ffn_b2, L0_ffn_gate_w, L0_ffn_fc1_w, L0_ffn_fc1_b, L0_ffn_geglu_mult, L0_ffn_fc2_w, L0_ffn_fc2_b, L0_ffn_s_fc1_w, L0_ffn_s_fc1_b, L0_ffn_s_geglu_mult, L0_ffn_s_fc2_w, L0_ffn_s_fc2_b):

    def _L0_attn_ref(x, ln1_g, ln1_b, in_proj_w, conv_w, conv_b, x_proj_w, dt_proj_w, dt_proj_b, A_log, D, out_proj_w, ln2_g, ln2_b, ffn_w1, ffn_b1, ffn_w2, ffn_b2):
        import jax, jax.numpy as jnp
        import numpy as np
        from jax import lax
        D_MODEL = 256
        D_STATE = 16
        D_CONV = 4
        EXPAND = 2
        D_INNER = EXPAND * D_MODEL
        DT_RANK = (D_MODEL + 15) // 16
        D_FF = 4 * D_MODEL
        B, L = (4, 512)

        def _layer_norm(x, g, b, eps=1e-05):
            mu = jnp.mean(x, axis=-1, keepdims=True)
            var = jnp.mean(jnp.square(x - mu), axis=-1, keepdims=True)
            return (x - mu) * lax.rsqrt(var + eps) * g + b

        def _silu(x):
            return x * jax.nn.sigmoid(x)

        def _mamba(x, in_proj_w, conv_w, conv_b, x_proj_w, dt_proj_w, dt_proj_b, A_log, D, out_proj_w):
            xz = x @ in_proj_w
            xi, z = jnp.split(xz, 2, axis=-1)
            xc = lax.conv_general_dilated(xi.transpose(0, 2, 1), conv_w, window_strides=(1,), padding=[(D_CONV - 1, 0)], feature_group_count=D_INNER, dimension_numbers=('NCH', 'OIH', 'NCH'))
            xc = _silu(xc + conv_b[None, :, None]).transpose(0, 2, 1)
            x_dbl = xc @ x_proj_w
            dt, Bm, Cm = jnp.split(x_dbl, [DT_RANK, DT_RANK + D_STATE], axis=-1)
            dt = jax.nn.softplus(dt @ dt_proj_w + dt_proj_b)
            A = -jnp.exp(A_log)

            def step(h, inp):
                dt_t, B_t, C_t, x_t = inp
                dA = jnp.exp(dt_t[..., None] * A)
                h = dA * h + dt_t[..., None] * B_t[:, None, :] * x_t[..., None]
                y = jnp.sum(h * C_t[:, None, :], axis=-1)
                return (h, y)
            h0 = jnp.zeros((x.shape[0], D_INNER, D_STATE), x.dtype)
            xs = (dt.transpose(1, 0, 2), Bm.transpose(1, 0, 2), Cm.transpose(1, 0, 2), xc.transpose(1, 0, 2))
            _, ys = lax.scan(step, h0, xs)
            y = ys.transpose(1, 0, 2) + D * xc
            y = y * _silu(z)
            return y @ out_proj_w
        x = x + _mamba(_layer_norm(x, ln1_g, ln1_b), in_proj_w, conv_w, conv_b, x_proj_w, dt_proj_w, dt_proj_b, A_log, D, out_proj_w)
        h = _layer_norm(x, ln2_g, ln2_b)
        h = jax.nn.gelu(h @ ffn_w1 + ffn_b1) @ ffn_w2 + ffn_b2
        return x + h

    def _L0_ffn_ref(x, gate_w, fc1_w, fc1_b, geglu_mult, fc2_w, fc2_b, s_fc1_w, s_fc1_b, s_geglu_mult, s_fc2_w, s_fc2_b):
        import jax, jax.numpy as jnp
        import numpy as np
        S, B, D = (256, 2, 256)
        E, TOPK = (15, 3)
        F = 256
        FS = 512

        def _uinit(k, shape, out_dim):
            std = out_dim ** (-0.5)
            return jax.random.uniform(k, shape, jnp.float32, -std, std)
        s, b, d = x.shape
        xt = x.reshape(-1, d)
        T = xt.shape[0]
        logits = xt @ gate_w.T
        scores = jax.nn.softmax(logits, axis=-1)
        topk_w, topk_idx = jax.lax.top_k(scores, TOPK)
        topk_w = topk_w / (jnp.sum(topk_w, axis=-1, keepdims=True) + 1e-20)
        comb = jnp.zeros((T, E), xt.dtype).at[jnp.arange(T)[:, None], topk_idx].add(topk_w)
        h = jnp.einsum('td,efd->etf', xt, fc1_w) + fc1_b[:, None, :]
        xh, g = (h[..., :F], h[..., F:])
        a = jax.nn.gelu(g, approximate=False) * xh * geglu_mult[:, None, :]
        yexp = jnp.einsum('etf,edf->etd', a, fc2_w) + fc2_b[:, None, :]
        y = jnp.einsum('etd,te->td', yexp, comb)
        hs = xt @ s_fc1_w.T + s_fc1_b
        xs, gs = (hs[..., :FS], hs[..., FS:])
        as_ = jax.nn.gelu(gs, approximate=False) * xs * s_geglu_mult
        ys = as_ @ s_fc2_w.T + s_fc2_b
        return (y + ys).reshape(s, b, d)
    x = L0_attn_x
    xn = _layernorm(x, axis=-1)
    x = x + _L0_attn_ref(xn, L0_attn_ln1_g, L0_attn_ln1_b, L0_attn_in_proj_w, L0_attn_conv_w, L0_attn_conv_b, L0_attn_x_proj_w, L0_attn_dt_proj_w, L0_attn_dt_proj_b, L0_attn_A_log, L0_attn_D, L0_attn_out_proj_w, L0_attn_ln2_g, L0_attn_ln2_b, L0_attn_ffn_w1, L0_attn_ffn_b1, L0_attn_ffn_w2, L0_attn_ffn_b2) + _L0_ffn_ref(xn, L0_ffn_gate_w, L0_ffn_fc1_w, L0_ffn_fc1_b, L0_ffn_geglu_mult, L0_ffn_fc2_w, L0_ffn_fc2_b, L0_ffn_s_fc1_w, L0_ffn_s_fc1_b, L0_ffn_s_geglu_mult, L0_ffn_s_fc2_w, L0_ffn_s_fc2_b)
    return x

_drawn_inputs = setup_inputs


def setup_inputs(seed=0):
    import zlib

    import numpy as np

    out = dict(_drawn_inputs(seed))
    spreads = {'L0_attn_ln1_g': (1.0, 0.6),
     'L0_attn_ln1_b': (0.0, 0.8),
     'L0_attn_conv_b': (0.0, 0.8),
     'L0_attn_D': (1.0, 0.6),
     'L0_attn_ln2_g': (1.0, 0.6),
     'L0_attn_ln2_b': (0.0, 2.0),
     'L0_attn_ffn_b1': (0.0, 2.0),
     'L0_attn_ffn_b2': (0.0, 0.8),
     'L0_ffn_geglu_mult': (1.0, 0.6),
     'L0_ffn_s_geglu_mult': (1.0, 0.6)}
    factors = {'L0_attn_in_proj_w': 8.0,
     'L0_attn_conv_w': 8.0,
     'L0_attn_x_proj_w': 8.0,
     'L0_attn_dt_proj_w': 8.0,
     'L0_attn_dt_proj_b': 8.0,
     'L0_attn_A_log': 8.0,
     'L0_attn_out_proj_w': 8.0,
     'L0_ffn_gate_w': 2.975,
     'L0_ffn_fc1_w': 3.214,
     'L0_ffn_fc1_b': 8.0,
     'L0_ffn_fc2_w': 3.204,
     'L0_ffn_fc2_b': 28.647,
     'L0_ffn_s_fc1_w': 3.014,
     'L0_ffn_s_fc1_b': 8.0,
     'L0_ffn_s_fc2_w': 3.011,
     'L0_ffn_s_fc2_b': 21.426,
     'L0_attn_ffn_w1': 3.963,
     'L0_attn_ffn_w2': 3.127}
    for name, (base, spread) in spreads.items():
        noise = np.random.default_rng([zlib.crc32(name.encode()), seed]).standard_normal(out[name].shape)
        drawn = base * np.exp(spread * noise) if base else spread * noise
        out[name] = jnp.asarray(drawn.astype(out[name].dtype))
    for name, factor in factors.items():
        out[name] = (out[name] * factor).astype(out[name].dtype)
    return out
```

```python
from contextlib import ExitStack

import numpy as np

import concourse.bass as bass
from concourse import mybir

F32 = mybir.dt.float32
BF16 = mybir.dt.bfloat16
I32 = mybir.dt.int32
U32 = mybir.dt.uint32
ALU = mybir.AluOpType
ACT = mybir.ActivationFunctionType
AX = mybir.AxisListType

P = 128
B, L, D = 2, 2048, 256
T = B * L
CH = 512
NCH = T // CH
CPB = L // CH
TPC = CH // P
NT = T // P
KD = D // P
DI = 512
G = DI // P
NS = 16
RK = 16
XP = RK + 2 * NS
CONV = 4
DF = 1024
KF = DF // P
E, TOPK = 15, 3
EP = 16
F = 256
FS = 512
KS = FS // P
BPI = 4
NBLK = -(-((T * TOPK + E * (P - 1)) // P) // BPI) * BPI
NSLOT = NBLK * P
MOE_CHUNKS = -(-NBLK // (BPI * G))
EPS = 1e-5


class Count:

    def __init__(self, sem, per, start=2):
        self.sem, self.per, self.start = sem, per, start

    def at(self, c, k, back=0):
        return c * self.per + ((self.start - back) * self.per + k)


class Phase:

    def __init__(self, nc, ctx, tag):
        self.nc, self.ctx, self.tag, self.counts = nc, ctx, tag, []

    def sb(self, name, shape, dt=F32):
        return self.ctx.enter_context(self.nc.sbuf_tensor(f"{self.tag}_{name}", shape, dt))

    def bank(self, name):
        return self.ctx.enter_context(self.nc.psum_tensor(f"{self.tag}_{name}", [P, 512], F32))

    def sem(self, name):
        return self.ctx.enter_context(self.nc.semaphore(f"{self.tag}_{name}"))

    def count(self, name, per, start=2):
        c = Count(self.sem(name), per, start)
        self.counts.append(c)
        return c

    def credit(self, sp):
        for c in self.counts:
            if c.start:
                sp.sem_inc(c.sem, c.start * c.per)


def norm_steps(nc, v, dve, c, n, src, dst, stats, mv, sd, rs, fence, sd_ready, half, done):
    def settle():
        v.wait_ge(dve.sem, dve.at(c, n[0]))

    for t in range(TPC):
        n[0] += 1
        nc.vector.bn_stats(stats[:, t, :], src[:, t, :]).then_inc(dve.sem, 1)
    settle()
    nc.vector.tensor_copy(fence[:, 0:1], fence[:, 1:2])
    for t in range(TPC):
        n[0] += 1
        nc.vector.bn_aggr(mv[:, t, :], stats[:, t, :]).then_inc(dve.sem, 1)
    v.wait_ge(sd_ready.sem, sd_ready.at(c, half + 1))
    n[0] += 1
    nc.vector.reciprocal(rs[:], sd[:]).then_inc(dve.sem, 1)
    settle()
    for t in range(TPC):
        nc.vector.tensor_scalar(dst[:, t, :], src[:, t, :], mv[:, t, 0:1], rs[:, t:t + 1],
                                ALU.subtract, ALU.mult).then_inc(done.sem, 1)


NORM = 2 * TPC + 1


def head_phase(nc, ctx, d, logits):
    ph = Phase(nc, ctx, "hd")
    sb, bank, sem, count = ph.sb, ph.bank, ph.sem, ph.count
    win = sb("win", [P, KD, 2 * DI])
    wxp = sb("wxp", [P, G, XP])
    wdt = sb("wdt", [RK, DI])
    wgate = sb("wgate", [P, KD, E])
    ident = sb("ident", [P, P])
    convw = sb("convw", [P, G, CONV])
    bias = sb("bias", [P, 2, G])
    ln1 = sb("ln1", [P, 2, KD])
    zeros = sb("zeros", [P, 4 * D])
    eps = sb("eps", [P, 1])
    fence = sb("fence", [P, 2])

    x = [sb(f"x{p}", [P, TPC, D]) for p in range(2)]
    xn = [sb(f"xn{p}", [P, TPC, D]) for p in range(2)]
    xh = sb("xh", [P, TPC, D])
    stats = sb("stats", [P, TPC, 6])
    mv = sb("mv", [P, TPC, 2])
    sd = sb("sd", [P, TPC])
    rs = sb("rs", [P, TPC])
    xnT = [sb(f"xnT{p}", [P, KD, CH]) for p in range(2)]
    xhT = sb("xhT", [P, KD, CH])
    xi = sb("xi", [P, G, CONV - 1 + CH])
    cv = sb("cv", [P, G, CH])
    xc = [sb(f"xc{p}", [P, G, CH]) for p in range(2)]
    sz = sb("sz", [P, G, CH])
    xd = sb("xd", [XP, CH])
    u = sb("u", [P, G, CH])
    rel = sb("rel", [P, G, CH])
    lnw = sb("lnw", [P, G, CH])
    rnd = sb("rnd", [P, G, CH])
    dt = sb("dt", [P, G, CH])
    dtx = sb("dtx", [P, G, CH])

    pT = [bank(f"pT{k}") for k in range(KD)]
    pL, pXI, pZ, pX = bank("pL"), bank("pXI"), bank("pZ"), bank("pX")
    pD = [bank(f"pD{k}") for k in range(2)]

    w_in, const_set, slots_zeroed = sem("w_in"), sem("const_set"), sem("slots_zeroed")
    x_in = [count(f"x_in{p}", 16, start=0) for p in range(2)]
    dve = count("dve", 2 * NORM + G * (CONV - 1) + 4)
    sd_ready = count("sd_ready", 2)
    xn_done, xh_done = count("xn_done", TPC), count("xh_done", TPC)
    tr_done, tr_out = count("tr_done", 2 * KD), count("tr_out", 2 * KD)
    lg_done, lg_out = count("lg_done", 1), count("lg_out", 1)
    xi_done, xi_out = count("xi_done", G), count("xi_out", G)
    z_done, z_out = count("z_done", G), count("z_out", G)
    conv_done, carried, xc_done = count("conv_done", G), count("carried", G), count("xc_done", G)
    xp_done, xp_out = count("xp_done", 1), count("xp_out", 1)
    dtp_done, abs_done, rel_done = count("dtp_done", G), count("abs_done", G), count("rel_done", G)
    u_done, lnw_done, dt_done, dtx_done = (count(n, 1) for n in ("u_done", "lnw_done", "dt_done", "dtx_done"))
    st = {n: count(f"st_{n}", 16) for n in ("xn", "xnT", "sz", "xc", "bc", "dt", "dtx")}

    with nc.Block() as block:
        @block.sync
        def _(sp):
            ph.credit(sp)
    with nc.Block() as block:
        @block.sync
        def _(sp):
            for dst, name in ((win, "in_proj_w"), (wxp, "x_proj_w"), (wdt, "dt_proj_w"), (wgate, "gate_w"),
                              (ident, "ident"), (convw, "conv_w"), (ln1, "ln1"), (bias, "inner_bias")):
                sp.dma_start(dst[:], d[name]).then_inc(w_in, 16)
            sp.wait_ge(const_set, 2)
            slots = d["slot_x"].rearrange("(n p a) w -> n p (a w)", p=P, a=4)
            with sp.Fori(0, NSLOT // (4 * P)) as n:
                sp.dma_start(slots[n], zeros[:]).then_inc(slots_zeroed, 16)
            with sp.Fori(0, NCH // 2) as i:
                for p in range(2):
                    c = 2 * i + p
                    sp.wait_ge(xn_done.sem, xn_done.at(c, TPC))
                    sp.dma_start(d["xn"].rearrange("(i q t p) w -> i q p t w", q=2, t=TPC, p=P)[i, p],
                                 xn[p][:]).then_inc(st["xn"].sem, 16)
                    sp.wait_ge(tr_out.sem, tr_out.at(c, KD))
                    sp.dma_start(d["xnT"].rearrange("(i q) p k t -> i q p k t", q=2)[i, p],
                                 xnT[p][:]).then_inc(st["xnT"].sem, 16)
                    sp.wait_ge(z_out.sem, z_out.at(c, G))
                    sp.dma_start(d["sz"].rearrange("(i q) g p t -> i q p g t", q=2)[i, p],
                                 sz[:]).then_inc(st["sz"].sem, 16)
                    sp.wait_ge(xc_done.sem, xc_done.at(c, G))
                    sp.dma_start(d["xc"].rearrange("(i q) g p t -> i q p g t", q=2)[i, p],
                                 xc[p][:]).then_inc(st["xc"].sem, 16)
                    sp.wait_ge(xp_out.sem, xp_out.at(c, 1))
                    sp.dma_start(d["bc"].rearrange("(i q) n t -> i q n t", q=2)[i, p],
                                 xd[RK:, :]).then_inc(st["bc"].sem, 16)
                    sp.wait_ge(dt_done.sem, dt_done.at(c, 1))
                    sp.dma_start(d["dt"].rearrange("(i q) g p t -> i q p g t", q=2)[i, p],
                                 dt[:]).then_inc(st["dt"].sem, 16)
                    sp.wait_ge(dtx_done.sem, dtx_done.at(c, 1))
                    sp.dma_start(d["dtx"].rearrange("(i q) g p t -> i q p g t", q=2)[i, p],
                                 dtx[:]).then_inc(st["dtx"].sem, 16)
            for s in st.values():
                sp.wait_ge(s.sem, s.at(NCH, 0))
            sp.wait_ge(slots_zeroed, 16 * (NSLOT // (4 * P)))

        @block.gpsimd
        def _(pool):
            nc.gpsimd.memset(zeros[:], 0.0).then_inc(const_set, 1)
            nc.gpsimd.memset(eps[:], EPS).then_inc(const_set, 1)
            with pool.Fori(0, NCH // 2) as i:
                for p in range(2):
                    pool.wait_ge(xn_done.sem, xn_done.at(2 * i + p, TPC, back=2))
                    pool.dma_start(x[p][:], d["x"].rearrange("(i q t p) w -> i q p t w", q=2, t=TPC, p=P)[i, p])\
                        .then_inc(x_in[p].sem, 16)

        @block.vector
        def _(v):
            nc.vector.memset(fence[:], 0.0)
            nc.vector.memset(logits[:], -1e30)
            v.wait_ge(w_in, 16 * 8)

            def chunk(i, p, c):
                n = [0]

                def step(ins):
                    n[0] += 1
                    ins.then_inc(dve.sem, 1)

                def settle():
                    v.wait_ge(dve.sem, dve.at(c, n[0]))

                ln = (stats, mv, sd, rs, fence, sd_ready)
                v.wait_ge(x_in[p].sem, x_in[p].at(i, 16))
                v.wait_ge(st["xn"].sem, st["xn"].at(c, 16, back=2))
                v.wait_ge(tr_done.sem, tr_done.at(c, KD, back=2))
                norm_steps(nc, v, dve, c, n, x[p], xn[p], *ln, 0, xn_done)
                v.wait_ge(xn_done.sem, xn_done.at(c, TPC))
                v.wait_ge(tr_done.sem, tr_done.at(c, 2 * KD, back=1))
                norm_steps(nc, v, dve, c, n, xn[p], xh, *ln, 1, xh_done)
                v.wait_ge(lg_done.sem, lg_done.at(c, 1))
                nc.vector.tensor_scalar(logits[:, bass.ds(c * TPC, TPC), 0:E],
                                        pL[:, 0:TPC * E].rearrange("p (t e) -> p t e", e=E), 1.0, None,
                                        ALU.mult).then_inc(lg_out.sem, 1)
                for k in reversed(range(CONV)):
                    for g in range(G):
                        if k == CONV - 1:
                            v.wait_ge(xi_out.sem, xi_out.at(c, g + 1))
                            v.wait_ge(xc_done.sem, xc_done.at(c, g + 1, back=1))
                            step(nc.vector.tensor_scalar(cv[:, g, :], xi[:, g, k:k + CH], convw[:, g, k:k + 1],
                                                         None, ALU.mult))
                            continue
                        if g == 0:
                            settle()
                        ins = nc.vector.scalar_tensor_tensor(cv[:, g, :], xi[:, g, k:k + CH], convw[:, g, k:k + 1],
                                                             cv[:, g, :], ALU.mult, ALU.add)
                        if k:
                            step(ins)
                        else:
                            ins.then_inc(conv_done.sem, 1)
                for g in range(G):
                    v.wait_ge(conv_done.sem, conv_done.at(c, g + 1))
                    nc.vector.tensor_copy(xi[:, g, 0:CONV - 1], xi[:, g, CH:]).then_inc(carried.sem, 1)
                v.wait_ge(u_done.sem, u_done.at(c, 1))
                step(nc.vector.tensor_scalar(rnd[:], u[:], 1.0, -1.0, ALU.add, ALU.add))
                settle()
                step(nc.vector.tensor_tensor(rnd[:], u[:], rnd[:], ALU.subtract))
                settle()
                v.wait_ge(lnw_done.sem, lnw_done.at(c, 1))
                step(nc.vector.tensor_tensor(rnd[:], rnd[:], lnw[:], ALU.add))
                settle()
                step(nc.vector.tensor_tensor(rnd[:], rnd[:], u[:], ALU.min))
                settle()
                v.wait_ge(st["dt"].sem, st["dt"].at(c, 16, back=1))
                nc.vector.tensor_tensor(dt[:], rnd[:], rel[:], ALU.add).then_inc(dt_done.sem, 1)
                v.wait_ge(dt_done.sem, dt_done.at(c, 1))
                v.wait_ge(st["dtx"].sem, st["dtx"].at(c, 16, back=1))
                nc.vector.tensor_tensor(dtx[:], dt[:], xc[p][:], ALU.mult).then_inc(dtx_done.sem, 1)
                assert n[0] == dve.per

            for b in range(B):
                if b:
                    v.wait_ge(carried.sem, carried.at(b * CPB, 0))
                for g in range(G):
                    nc.vector.memset(xi[:, g, 0:CONV - 1], 0.0)
                with v.Fori(b * CPB // 2, (b + 1) * CPB // 2) as i:
                    for p in range(2):
                        chunk(i, p, 2 * i + p)

        @block.scalar
        def _(a):
            a.wait_ge(const_set, 2)
            a.wait_ge(w_in, 16 * 8)
            act = nc.scalar.activation
            with a.Fori(0, NCH // 2) as i:
                for p in range(2):
                    c = 2 * i + p
                    a.wait_ge(dve.sem, dve.at(c, 2 * TPC))
                    act(sd[:], mv[:, :, 1], ACT.Sqrt, bias=eps[:, 0:1]).then_inc(sd_ready.sem, 1)
                    a.wait_ge(dve.sem, dve.at(c, NORM + 2 * TPC))
                    act(sd[:], mv[:, :, 1], ACT.Sqrt, bias=eps[:, 0:1]).then_inc(sd_ready.sem, 1)
                    a.wait_ge(st["xnT"].sem, st["xnT"].at(c, 16, back=2))
                    for k in range(KD):
                        a.wait_ge(tr_done.sem, tr_done.at(c, k + 1))
                        act(xnT[p][:, k, :], pT[k][:], ACT.Copy).then_inc(tr_out.sem, 1)
                    a.wait_ge(z_done.sem, z_done.at(c, G, back=1))
                    for k in range(KD):
                        a.wait_ge(tr_done.sem, tr_done.at(c, KD + k + 1))
                        act(xhT[:, k, :], pT[k][:], ACT.Identity, bias=ln1[:, 1, k:k + 1],
                            scale=ln1[:, 0, k:k + 1]).then_inc(tr_out.sem, 1)
                    a.wait_ge(st["sz"].sem, st["sz"].at(c, 16, back=1))
                    for g in range(G):
                        a.wait_ge(carried.sem, carried.at(c, g + 1, back=1))
                        a.wait_ge(xi_done.sem, xi_done.at(c, g + 1))
                        act(xi[:, g, CONV - 1:], pXI[:], ACT.Copy).then_inc(xi_out.sem, 1)
                        a.wait_ge(z_done.sem, z_done.at(c, g + 1))
                        act(sz[:, g, :], pZ[:], ACT.Silu).then_inc(z_out.sem, 1)
                    a.wait_ge(st["xc"].sem, st["xc"].at(c, 16, back=2))
                    a.wait_ge(dtx_done.sem, dtx_done.at(c, 1, back=2))
                    for g in range(G):
                        a.wait_ge(conv_done.sem, conv_done.at(c, g + 1))
                        act(xc[p][:, g, :], cv[:, g, :], ACT.Silu, bias=bias[:, 0, g:g + 1]).then_inc(xc_done.sem, 1)
                    a.wait_ge(st["bc"].sem, st["bc"].at(c, 16, back=1))
                    a.wait_ge(dtp_done.sem, dtp_done.at(c, G, back=1))
                    a.wait_ge(xp_done.sem, xp_done.at(c, 1))
                    act(xd[:], pX[0:XP, :], ACT.Copy).then_inc(xp_out.sem, 1)
                    a.wait_ge(dt_done.sem, dt_done.at(c, 1, back=1))
                    for g in range(G):
                        a.wait_ge(dtp_done.sem, dtp_done.at(c, g + 1))
                        act(u[:, g, :], pD[g % 2][:], ACT.Abs, bias=bias[:, 1, g:g + 1]).then_inc(abs_done.sem, 1)
                        act(rel[:, g, :], pD[g % 2][:], ACT.Relu, bias=bias[:, 1, g:g + 1]).then_inc(rel_done.sem, 1)
                    a.wait_ge(abs_done.sem, abs_done.at(c, G))
                    act(u[:], u[:], ACT.Exp, scale=-1.0).then_inc(u_done.sem, 1)
                    a.wait_ge(u_done.sem, u_done.at(c, 1))
                    act(lnw[:], u[:], ACT.Ln, bias=1.0).then_inc(lnw_done.sem, 1)

        @block.tensor
        def _(t):
            t.wait_ge(w_in, 16 * 8)
            mm = nc.tensor.matmul
            with t.Fori(0, NCH // 2) as i:
                for p in range(2):
                    c = 2 * i + p
                    for half, (src, ready) in enumerate(((xn[p], xn_done), (xh, xh_done))):
                        t.wait_ge(ready.sem, ready.at(c, TPC))
                        for k in range(KD):
                            if half:
                                t.wait_ge(tr_out.sem, tr_out.at(c, k + 1))
                            else:
                                t.wait_ge(tr_out.sem, tr_out.at(c, KD + k + 1, back=1))
                            for j in range(TPC):
                                ins = nc.tensor.transpose(pT[k][:, j * P:(j + 1) * P],
                                                          src[:, j, k * P:(k + 1) * P], ident[:])
                            ins.then_inc(tr_done.sem, 1)
                    t.wait_ge(tr_out.sem, tr_out.at(c, KD))
                    t.wait_ge(lg_out.sem, lg_out.at(c, 1, back=1))
                    for j in range(TPC):
                        for k in range(KD):
                            ins = mm(pL[:, j * E:(j + 1) * E], xnT[p][:, k, j * P:(j + 1) * P], wgate[:, k, :],
                                     start=(k == 0), stop=(k == KD - 1))
                    ins.then_inc(lg_done.sem, 1)
                    t.wait_ge(tr_out.sem, tr_out.at(c, 2 * KD))
                    for g in range(G):
                        for col, dst, ready, out in ((g * P, pXI, xi_done, xi_out), (DI + g * P, pZ, z_done, z_out)):
                            if g:
                                t.wait_ge(out.sem, out.at(c, g))
                            else:
                                t.wait_ge(out.sem, out.at(c, G, back=1))
                            for k in range(KD):
                                ins = mm(dst[:], win[:, k, col:col + P], xhT[:, k, :],
                                         start=(k == 0), stop=(k == KD - 1))
                            ins.then_inc(ready.sem, 1)
                    t.wait_ge(xp_out.sem, xp_out.at(c, 1, back=1))
                    for g in range(G):
                        t.wait_ge(xc_done.sem, xc_done.at(c, g + 1))
                        ins = mm(pX[0:XP, :], wxp[:, g, :], xc[p][:, g, :], start=(g == 0), stop=(g == G - 1))
                    ins.then_inc(xp_done.sem, 1)
                    t.wait_ge(xp_out.sem, xp_out.at(c, 1))
                    for g in range(G):
                        if g < 2:
                            t.wait_ge(rel_done.sem, rel_done.at(c, G - 1 + g, back=1))
                        else:
                            t.wait_ge(rel_done.sem, rel_done.at(c, g - 1))
                        mm(pD[g % 2][:], wdt[:, g * P:(g + 1) * P], xd[0:RK, :], start=True, stop=True)\
                            .then_inc(dtp_done.sem, 1)





def route_phase(nc, ctx, d, logits, wts, block_e, slotf, w1, w2):
    ph = Phase(nc, ctx, "rt")
    sb, sem = ph.sb, ph.sem
    tri = sb("tri", [P, P])
    ones = sb("ones", [P, P])
    rev = sb("rev", [P, NT, EP])
    blk = sb("blk", [1, NBLK, EP])
    sc = sb("sc", [P, NT, EP])
    work = sb("work", [P, NT, EP])
    one = sb("one", [P, TOPK, NT, EP])
    mask = sb("mask", [P, NT, EP])
    m = sb("m", [P, TOPK, NT])
    red = sb("red", [P, NT])
    pick = sb("pick", [P, NT])
    pos = sb("pos", [P, NT, EP])
    tot = sb("tot", [P, EP, NT])
    cum = sb("cum", [P, EP, NT])
    before = sb("before", [P, EP])
    cnt = sb("cnt", [P, EP])
    cnt_i = sb("cnt_i", [P, EP], I32)
    nb = sb("nb", [P, EP])
    nb_cum = sb("nb_cum", [P, EP])
    onesr = sb("onesr", [P, EP * NT])
    le = sb("le", [1, NBLK, EP])
    be = sb("be", [1, NBLK])
    mult = sb("mult", [P, E * KD])
    bf = sb("bf", [E, 2 * F + D])
    bparts = [sb(f"b{n}", [E, 2 * F + D], BF16) for n in range(3)]
    xs = [sb(f"xs{p}", [P, TPC, D]) for p in range(2)]
    idx = [sb(f"idx{p}", [P, TOPK * TPC], U32) for p in range(2)]
    pR, pS = ph.bank("pR"), ph.bank("pS")

    c_in, w_in, dve, exp_done, pe_done = sem("c_in"), sem("w_in"), sem("dve"), sem("exp_done"), sem("pe_done")
    b_in, b_out, rounds = sem("b_in"), sem("b_out"), sem("rounds")
    xs_in = [ph.count(f"xs_in{p}", 16) for p in range(2)]
    idx_set = ph.count("idx_set", TOPK)
    freed = [ph.count(f"freed{p}", 1) for p in range(2)]
    sent = [[ph.count(f"sent{p}{j}", 16, start=0) for j in range(TOPK * TPC)] for p in range(2)]
    xn_tiles = d["xn"].rearrange("(i q t p) w -> i q p t w", q=2, t=TPC, p=P)
    SPLIT, SHIFTED, MASKED = 5, 9, 34

    with nc.Block() as block:
        @block.sync
        def _(sp):
            ph.credit(sp)
            for dst, name in ((tri, "tri"), (ones, "ones"), (rev, "rev"), (blk, "blk")):
                sp.dma_start(dst[:], d[name]).then_inc(c_in, 16)
            sp.dma_start(bf[:, 0:2 * F], d["fc1_b"]).then_inc(b_in, 16)
            sp.dma_start(bf[:, 2 * F:], d["fc2_b"]).then_inc(b_in, 16)
            sp.dma_start(mult[:], d["geglu_mult"]).then_inc(w_in, 16)
            sp.dma_start(w2[:], d["fc2_w"]).then_inc(w_in, 16)
            sp.dma_start(w1[:], d["fc1_w"]).then_inc(w_in, 16)
            sp.wait_ge(w_in, 48)

    with nc.Block() as block:
        @block.sync
        def _(sp):
            with sp.Fori(0, NCH // 2) as i:
                for p in range(2):
                    sp.wait_ge(freed[p].sem, freed[p].at(i, 0))
                    sp.dma_start(xs[p][:], xn_tiles[i, p]).then_inc(xs_in[p].sem, 16)
            sp.wait_ge(dve, SPLIT)
            for n in range(3):
                sp.dma_start(d["moe_b"][:, n, :], bparts[n][:]).then_inc(b_out, 16)
            sp.wait_ge(b_out, 48)

        @block.vector
        def _(v):
            chain = [0]
            vec = nc.vector

            def step(ins):
                chain[0] += 1
                ins.then_inc(dve, 1)
                v.wait_ge(dve, chain[0])

            def over_e(ap):
                return ap.rearrange("p (t o) -> p t o", o=1).to_broadcast([P, NT, EP])

            v.wait_ge(c_in, 64)
            v.wait_ge(b_in, 32)
            for n in range(3):
                step(vec.tensor_copy(bparts[n][:], bf[:]))
                if n < 2:
                    step(vec.tensor_tensor(bf[:], bf[:], bparts[n][:], ALU.subtract))
            assert chain[0] == SPLIT
            step(vec.tensor_tensor(w2[:], w2[:], mult[:].rearrange("p (n o) -> p n o", o=1)
                                   .to_broadcast([P, E * KD, D]), ALU.mult))
            step(vec.memset(onesr[:], 1.0))
            step(vec.tensor_reduce(red[:], logits[:], AX.X, ALU.max))
            step(vec.tensor_tensor(work[:], logits[:], over_e(red[:]), ALU.subtract))
            assert chain[0] == SHIFTED
            v.wait_ge(exp_done, 1)
            step(vec.memset(sc[:, :, E:EP], 0.0))
            step(vec.tensor_reduce(red[:], sc[:], AX.X, ALU.add))
            step(vec.reciprocal(pick[:], red[:]))
            step(vec.tensor_tensor(sc[:], sc[:], over_e(pick[:]), ALU.mult))
            step(vec.memset(sc[:, :, E:EP], -1.0))
            for k in range(TOPK):
                step(vec.tensor_reduce(m[:, k, :], sc[:], AX.X, ALU.max))
                step(vec.tensor_tensor(work[:], sc[:], over_e(m[:, k, :]), ALU.is_equal))
                step(vec.tensor_tensor(work[:], work[:], rev[:], ALU.mult))
                step(vec.tensor_reduce(pick[:], work[:], AX.X, ALU.max))
                step(vec.tensor_tensor(one[:, k], rev[:], over_e(pick[:]), ALU.is_equal))
                step(vec.scalar_tensor_tensor(sc[:], one[:, k], -4.0, sc[:], ALU.mult, ALU.add))
            step(vec.tensor_tensor(mask[:], one[:, 0], one[:, 1], ALU.add))
            step(vec.tensor_tensor(mask[:], mask[:], one[:, 2], ALU.add))
            assert chain[0] == MASKED
            step(vec.tensor_tensor(red[:], m[:, 0, :], m[:, 1, :], ALU.add))
            step(vec.tensor_tensor(red[:], red[:], m[:, 2, :], ALU.add))
            step(vec.tensor_scalar(red[:], red[:], 1e-20, None, ALU.add))
            step(vec.reciprocal(pick[:], red[:]))
            for k in range(TOPK):
                step(vec.tensor_tensor(wts[:, k, :], m[:, k, :], pick[:], ALU.mult))
            v.wait_ge(pe_done, 2)
            step(vec.tensor_copy(tot[:], pS[:].rearrange("p (t e) -> p e t", e=EP)))
            step(vec.tensor_tensor_scan(cum[:].rearrange("p e t -> p (e t)"), onesr[:],
                                        tot[:].rearrange("p e t -> p (e t)"), 0.0, ALU.mult, ALU.add))
            step(vec.memset(before[:, 0:1], 0.0))
            step(vec.tensor_copy(before[:, 1:EP], cum[:, 0:EP - 1, NT - 1]))
            step(vec.tensor_tensor(cnt[:], cum[:, :, NT - 1], before[:], ALU.subtract))
            step(vec.tensor_scalar(cnt[:], cnt[:], float(P - 1), None, ALU.add))
            step(vec.tensor_copy(cnt_i[:], cnt[:]))
            step(vec.tensor_scalar(cnt_i[:], cnt_i[:], 7, None, ALU.logical_shift_right))
            step(vec.tensor_copy(nb[:], cnt_i[:]))
            step(vec.tensor_tensor_scan(nb_cum[:], onesr[:, 0:EP], nb[:], 0.0, ALU.mult, ALU.add))
            step(vec.tensor_tensor(nb[:], nb_cum[:], nb[:], ALU.subtract))
            step(vec.scalar_tensor_tensor(before[:], nb[:], float(P), before[:], ALU.mult, ALU.subtract))
            step(vec.tensor_tensor(cum[:], cum[:], tot[:], ALU.subtract))
            step(vec.tensor_tensor(cum[:], cum[:], before[:].rearrange("p (e o) -> p e o", o=1)
                                   .to_broadcast([P, EP, NT]), ALU.add))
            step(vec.tensor_tensor(pos[:], pR[:].rearrange("p (t e) -> p t e", e=EP),
                                   cum[:].rearrange("p e t -> p t e"), ALU.add))
            for k in range(TOPK):
                step(vec.tensor_tensor(work[:], pos[:], one[:, k], ALU.mult))
                step(vec.tensor_reduce(slotf[:, k, :], work[:], AX.X, ALU.add))
            step(vec.tensor_tensor(le[:], nb_cum[0:1, :].rearrange("p (o e) -> p o e", o=1)
                                   .to_broadcast([1, NBLK, EP]), blk[:], ALU.is_le))
            step(vec.tensor_reduce(be[:], le[:, :, 0:E], AX.X, ALU.add))
            step(vec.tensor_scalar(be[:], be[:], float(E - 1), None, ALU.min))
            step(vec.tensor_copy(block_e[:], be[:]))
            with v.Fori(0, NCH // 2) as i:
                for p in range(2):
                    c = 2 * i + p
                    v.wait_ge(freed[p].sem, freed[p].at(i, 0))
                    for k in range(TOPK):
                        vec.tensor_scalar(idx[p][:, k * TPC:(k + 1) * TPC], slotf[:, k, bass.ds(c * TPC, TPC)],
                                          1.0, None, ALU.mult).then_inc(idx_set.sem, 1)

        @block.scalar
        def _(a):
            a.wait_ge(dve, SHIFTED)
            nc.scalar.activation(sc[:], work[:], ACT.Exp).then_inc(exp_done, 1)

        @block.tensor
        def _(t):
            t.wait_ge(dve, MASKED)
            for dst, lhs in ((pR, tri), (pS, ones)):
                nc.tensor.matmul(dst[:], lhs[:], mask[:].rearrange("p t e -> p (t e)"), start=True, stop=True)\
                    .then_inc(pe_done, 1)

        @block.gpsimd
        def _(pool):
            with pool.Fori(0, NCH // 2) as i:
                for p in range(2):
                    pool.wait_ge(xs_in[p].sem, xs_in[p].at(i, 16))
                    pool.wait_ge(idx_set.sem, idx_set.at(2 * i + p, TOPK))
                    pool.sem_inc(rounds, 1)
                    for j in range(TOPK * TPC):
                        pool.indirect_dma_start(
                            d["slot_x"], bass.IndirectOffsetOnAxis(idx[p][:, j:j + 1], 0), xs[p][:, j % TPC, :], None,
                        ).then_inc(sent[p][j].sem, 16)
                for p in range(2):
                    for j in range(TOPK * TPC):
                        pool.wait_ge(sent[p][j].sem, sent[p][j].at(i, 16))
                    pool.sem_inc(freed[p].sem, 1)


def scan_phase(nc, ctx, d, block_e, w1, w2):
    ph = Phase(nc, ctx, "sc")
    sb, bank, sem, count = ph.sb, ph.bank, ph.sem, ph.count
    ident = sb("ident", [P, P])
    A = sb("A", [P, G, NS])
    Dw = sb("Dw", [P, G])
    state = sb("state", [P, G, NS])
    sel = sb("sel", [3 * BPI, BPI, P], BF16)
    bc = sb("bc", [P, NS // 2, 2, 2, CH])
    dt = [sb(f"dt{p}", [P, CH]) for p in range(2)]
    dtx = [sb(f"dtx{p}", [P, CH]) for p in range(2)]
    xc = sb("xc", [P, CH])
    sz = sb("sz", [P, CH])
    dbx = [sb(f"dbx{p}", [P, 2, CH]) for p in range(2)]
    h = [sb(f"h{p}", [P, 2, CH]) for p in range(2)]
    yo = sb("yo", [P, CH])
    sel_f = yo[0:3 * BPI, 0:BPI * P]
    xg = sb("xg", [P, BPI, D])
    bb = [sb(f"bb{p}", [3 * BPI, 2 * F + D], BF16) for p in range(2)]
    xT = sb("xT", [P, 2, KD, P])
    hid = sb("hid", [P, BPI, 2 * F])
    ye = sb("ye", [P, 2, D])

    pA = [bank(f"pA{n}") for n in range(4)]
    pY, pT = bank("pY"), bank("pT")
    pH = [bank(f"pH{q}") for q in range(2)]

    w_in, const_set, reset = sem("w_in"), sem("const_set"), sem("reset")
    in_ld = [count(f"in_ld{p}", 32 * G // 2) for p in range(2)]
    gate_ld = count("gate_ld", 32 * G)
    bc_ld = [count(f"bc_ld{k}", 32) for k in range(NS // 2)]
    xg_ld = count("xg_ld", 16 * G)
    bb_ld = [count(f"bb_ld{p}", 16 * BPI * G // 2) for p in range(2)]
    exp_done, scan_done = count("exp_done", G * NS), count("scan_done", G * NS)
    dbx_done, prod_done, sum_done = (count(n, G * NS // 2) for n in ("dbx_done", "prod_done", "sum_done"))
    saved = count("saved", G * NS // 2)
    skip_done, y_done = count("skip_done", G), count("y_done", G)
    y_st = count("y_st", 16 * G)
    tr_done, tr_out = count("tr_done", 4 * G), count("tr_out", 4 * G)
    f1_done, f1_out = count("f1_done", BPI * G), count("f1_out", BPI * G)
    gelu_done, act_done = count("gelu_done", G), count("act_done", G)
    f2_done, f2_out = count("f2_done", 2 * G), count("f2_out", 2 * G)
    ye_st = count("ye_st", 32 * G)
    NP = NS // 2

    def chunks(eng, body):
        with eng.Fori(0, CPB) as c:
            body(c, True)
        yield
        with eng.Fori(CPB, MOE_CHUNKS) as c:
            body(c, True)
        for c in range(MOE_CHUNKS, NCH):
            body(c, False)

    with nc.Block() as block:
        @block.sync
        def _(sp):
            ph.credit(sp)
            for dst, name in ((ident[:], "ident"), (A[:], "A_log"), (Dw[:], "D"), (sel_f, "sel")):
                sp.dma_start(dst, d[name]).then_inc(w_in, 16)

        @block.vector
        def _(v):
            v.wait_ge(w_in, 64)
            nc.vector.tensor_copy(sel[:].rearrange("k b p -> k (b p)"), sel_f).then_inc(const_set, 1)
            nc.vector.memset(state[:], 0.0)
            v.wait_ge(const_set, 2)
            nc.vector.tensor_scalar(A[:], A[:], -1.0, None, ALU.mult)

        @block.scalar
        def _(a):
            a.wait_ge(w_in, 64)
            nc.scalar.activation(A[:], A[:], ACT.Exp).then_inc(const_set, 1)

    with nc.Block() as block:
        @block.sync
        def _(sp):
            def load_inputs(c, g):
                p = g % 2
                sp.wait_ge(y_done.sem, y_done.at(c, g - 1))
                for dst, name in ((dt, "dt"), (dtx, "dtx")):
                    sp.dma_start(dst[p][:], d[name][c, g]).then_inc(in_ld[p].sem, 16)

            def load_gates(c, g):
                sp.wait_ge(y_done.sem, y_done.at(c, g))
                for dst, name in ((xc, "xc"), (sz, "sz")):
                    sp.dma_start(dst[:], d[name][c, g]).then_inc(gate_ld.sem, 16)

            def load_bc(c):
                for k in range(NP):
                    sp.wait_ge(prod_done.sem, prod_done.at(c, k + 1 - NP))
                    for n in range(2):
                        row = n * NS + 2 * k
                        src = d["bc"][c, row:row + 2, :].rearrange("(o n) t -> o (n t)", o=1)
                        sp.dma_start(bc[:, k, n].rearrange("p n t -> p (n t)"), src.to_broadcast([P, 2 * CH]))\
                            .then_inc(bc_ld[k].sem, 16)

            def load_blocks(c, g):
                p = g % 2
                sp.wait_ge(tr_done.sem, tr_done.at(c, 4 * g - 2))
                sp.dma_start(xg[:], d["slot_x"].rearrange("(c g b p) w -> c g p b w", g=G, b=BPI, p=P)[c, g])\
                    .then_inc(xg_ld.sem, 16)
                sp.wait_ge(f2_done.sem, f2_done.at(c, 2 * g - 2))
                for b in range(BPI):
                    e = sp.value_load(block_e[0:1, bass.ds(c * (G * BPI) + (g * BPI + b), 1)], min_val=0, max_val=E - 1)
                    sp.dma_start(bb[p][3 * b:3 * b + 3, :], d["moe_b"][bass.ds(e, 1)].rearrange("o k n -> (o k) n"))\
                        .then_inc(bb_ld[p].sem, 16)

            def store(c, g, moe):
                sp.wait_ge(y_done.sem, y_done.at(c, g + 1))
                sp.dma_start(d["y"][c, g], yo[:]).then_inc(y_st.sem, 16)
                if moe:
                    for q in range(2):
                        sp.wait_ge(f2_out.sem, f2_out.at(c, 2 * g + q + 1))
                        dst = d["slot_y"].rearrange("(c g q b p) w -> c g q p b w", g=G, q=2, b=2, p=P)
                        sp.dma_start(dst[c, g, q], ye[:]).then_inc(ye_st.sem, 16)

            def chunk(c, moe, first=False):
                for g in range(G):
                    load_inputs(c, g)
                    if moe:
                        load_blocks(c, g)
                    if g == 0:
                        load_bc(c)
                    load_gates(c, g)
                    if g:
                        store(c, g - 1, moe)
                    elif not first:
                        store(c - 1, G - 1, True)

            chunk(0, True, first=True)
            with sp.Fori(1, MOE_CHUNKS) as c:
                chunk(c, True)
            for c in range(MOE_CHUNKS, NCH):
                chunk(c, False)
            store(NCH - 1, G - 1, MOE_CHUNKS == NCH)
            sp.wait_ge(y_st.sem, y_st.at(NCH, 0))
            sp.wait_ge(ye_st.sem, ye_st.at(MOE_CHUNKS, 0))

        @block.gpsimd
        def _(pool):
            def chunk(c, moe):
                for g in range(G):
                    p = g % 2
                    pool.wait_ge(in_ld[p].sem, in_ld[p].at(c, 32 * (g // 2 + 1)))
                    for k in range(NP):
                        if moe and k == NP - 2:
                            pool.wait_ge(gelu_done.sem, gelu_done.at(c, g + 1))
                            nc.gpsimd.tensor_tensor(hid[:, :, 0:F], hid[:, :, 0:F], hid[:, :, F:], ALU.mult)\
                                .then_inc(act_done.sem, 1)
                        pool.wait_ge(bc_ld[k].sem, bc_ld[k].at(c, 32))
                        pool.wait_ge(scan_done.sem, scan_done.at(c, NS * g + 2 * k - 2))
                        nc.gpsimd.tensor_tensor(dbx[k % 2][:], dtx[p][:].rearrange("p (o t) -> p o t", o=1)
                                                .to_broadcast([P, 2, CH]), bc[:, k, 0], ALU.mult)\
                            .then_inc(dbx_done.sem, 1)
            for _ in chunks(pool, chunk):
                pass

        @block.scalar
        def _(a):
            act = nc.scalar.activation

            def chunk(c, moe):
                for g in range(G):
                    p = g % 2

                    def decays(k):
                        for n in (2 * k, 2 * k + 1):
                            a.wait_ge(scan_done.sem, scan_done.at(c, NS * g + n - 3))
                            act(pA[n % 4][:], dt[p][:], ACT.Exp, scale=A[:, g, n:n + 1]).then_inc(exp_done.sem, 1)

                    def transposed(n):
                        if n in (0, 3):
                            a.wait_ge(f2_done.sem, f2_done.at(c, 2 * g + (1 if n else 0)))
                        else:
                            a.wait_ge(f1_done.sem, f1_done.at(c, BPI * g + 2 * n))
                        a.wait_ge(tr_done.sem, tr_done.at(c, 4 * g + n + 1))
                        act(xT[:].rearrange("p b k t -> p (b k t)"), pT[:], ACT.Copy).then_inc(tr_out.sem, 1)

                    def out(q):
                        a.wait_ge(ye_st.sem, ye_st.at(c, 32 * g + 16 * q))
                        a.wait_ge(f2_done.sem, f2_done.at(c, 2 * g + q + 1))
                        act(ye[:].rearrange("p b w -> p (b w)"), pH[q][:], ACT.Copy).then_inc(f2_out.sem, 1)

                    a.wait_ge(in_ld[p].sem, in_ld[p].at(c, 32 * (g // 2 + 1)))
                    if not moe:
                        for k in range(NP):
                            decays(k)
                        continue
                    decays(0)
                    decays(1)
                    transposed(0)
                    decays(2)
                    transposed(1)
                    decays(3)
                    decays(4)
                    a.wait_ge(f1_out.sem, f1_out.at(c, BPI * (g + 1)))
                    act(hid[:, :, F:], hid[:, :, F:], ACT.Gelu).then_inc(gelu_done.sem, 1)
                    decays(5)
                    transposed(2)
                    decays(6)
                    transposed(3)
                    out(0)
                    decays(7)
                    out(1)
            for _ in chunks(a, chunk):
                pass

        @block.vector
        def _(v):
            vec = nc.vector

            def chunk(c, moe):
                for g in range(G):
                    p = g % 2

                    def scans(k):
                        v.wait_ge(sum_done.sem, sum_done.at(c, NP * g + k - 1))
                        v.wait_ge(dbx_done.sem, dbx_done.at(c, NP * g + k + 1))
                        for j in range(2):
                            n = 2 * k + j
                            v.wait_ge(exp_done.sem, exp_done.at(c, NS * g + n + 1))
                            vec.tensor_tensor_scan(h[k % 2][:, j, :], pA[n % 4][:], dbx[k % 2][:, j, :],
                                                   state[:, g, n:n + 1], ALU.mult, ALU.add).then_inc(scan_done.sem, 1)
                        v.wait_ge(scan_done.sem, scan_done.at(c, NS * g + 2 * k + 2))
                        vec.tensor_copy(state[:, g, 2 * k:2 * k + 2], h[k % 2][:, :, CH - 1]).then_inc(saved.sem, 1)
                        v.wait_ge(saved.sem, saved.at(c, NP * g + k + 1))
                        v.wait_ge(bc_ld[k].sem, bc_ld[k].at(c, 32))
                        vec.tensor_tensor(h[k % 2][:], h[k % 2][:], bc[:, k, 1], ALU.mult).then_inc(prod_done.sem, 1)

                    def hidden(b):
                        v.wait_ge(tr_done.sem, tr_done.at(c, 4 * g))
                        v.wait_ge(f1_done.sem, f1_done.at(c, BPI * g + b + 1))
                        vec.tensor_copy(hid[:, b, :], pH[b % 2][:]).then_inc(f1_out.sem, 1)

                    for k in range(NP):
                        scans(k)
                        if moe and k in (1, 2):
                            hidden(2 * k - 2)
                            hidden(2 * k - 1)
                    v.wait_ge(sum_done.sem, sum_done.at(c, NP * (g + 1)))
                    v.wait_ge(gate_ld.sem, gate_ld.at(c, 32 * (g + 1)))
                    v.wait_ge(y_st.sem, y_st.at(c, 16 * g))
                    vec.scalar_tensor_tensor(yo[:], xc[:], Dw[:, g:g + 1], pY[:], ALU.mult, ALU.add)\
                        .then_inc(skip_done.sem, 1)
                    v.wait_ge(skip_done.sem, skip_done.at(c, g + 1))
                    vec.tensor_tensor(yo[:], yo[:], sz[:], ALU.mult).then_inc(y_done.sem, 1)

            for _ in chunks(v, chunk):
                v.wait_ge(prod_done.sem, prod_done.at(CPB, 0))
                vec.memset(state[:], 0.0).then_inc(reset, 1)
                v.wait_ge(reset, 1)

        @block.tensor
        def _(t):
            mm = nc.tensor.matmul

            def chunk(c, moe):
                for g in range(G):
                    p = g % 2

                    def sums(k):
                        if k == 0:
                            t.wait_ge(skip_done.sem, skip_done.at(c, g))
                        t.wait_ge(prod_done.sem, prod_done.at(c, NP * g + k + 1))
                        for j in range(2):
                            ins = mm(pY[:], ident[:], h[k % 2][:, j, :], start=(k + j == 0),
                                     stop=(2 * k + j == NS - 1))
                        ins.then_inc(sum_done.sem, 1)

                    def turn(n):
                        t.wait_ge(tr_out.sem, tr_out.at(c, 4 * g + n))
                        if n == 0:
                            t.wait_ge(xg_ld.sem, xg_ld.at(c, 16 * (g + 1)))
                        if n == 2:
                            t.wait_ge(act_done.sem, act_done.at(c, g + 1))
                        src = xg if n < 2 else hid
                        for b in range(2):
                            for k in range(KD):
                                at = (KD * b + k) * P
                                ins = nc.tensor.transpose(pT[:, at:at + P],
                                                          src[:, 2 * (n % 2) + b, k * P:(k + 1) * P], ident[:])
                        ins.then_inc(tr_done.sem, 1)

                    def first(b):
                        if b % 2 == 0:
                            t.wait_ge(tr_out.sem, tr_out.at(c, 4 * g + b // 2 + 1))
                        if b < 2:
                            t.wait_ge(f2_out.sem, f2_out.at(c, 2 * g - 1 + b))
                        else:
                            t.wait_ge(f1_out.sem, f1_out.at(c, BPI * g + b - 1))
                        if b == 0:
                            t.wait_ge(bb_ld[p].sem, bb_ld[p].at(c, 16 * BPI * (g // 2 + 1)))
                        for k in range(KD):
                            mm(pH[b % 2][:], xT[:, b % 2, k, :], w1[:, bass.ds(e[b] * KD + k, 1), :]
                               .rearrange("p o n -> p (o n)"), start=(k == 0), stop=False)
                        mm(pH[b % 2][:], sel[:, b, :], bb[p][:, 0:2 * F], start=False, stop=True)\
                            .then_inc(f1_done.sem, 1)

                    def second(q):
                        t.wait_ge(tr_out.sem, tr_out.at(c, 4 * g + 2 + q + 1))
                        t.wait_ge(f1_out.sem, f1_out.at(c, BPI * g + 3 + q))
                        for j in range(2):
                            dst = pH[q][:, j * D:(j + 1) * D]
                            for k in range(KD):
                                mm(dst, xT[:, j, k, :], w2[:, bass.ds(e[2 * q + j] * KD + k, 1), :]
                                   .rearrange("p o n -> p (o n)"), start=(k == 0), stop=False)
                            ins = mm(dst, sel[:, 2 * q + j, :], bb[p][:, 2 * F:], start=False, stop=True)
                        ins.then_inc(f2_done.sem, 1)

                    if not moe:
                        for k in range(NP):
                            sums(k)
                        continue
                    e = [t.value_load(block_e[0:1, bass.ds(c * (G * BPI) + (g * BPI + b), 1)], min_val=0,
                                      max_val=E - 1) for b in range(BPI)]
                    turn(0)
                    sums(0)
                    first(0)
                    first(1)
                    turn(1)
                    sums(1)
                    first(2)
                    first(3)
                    sums(2)
                    sums(3)
                    sums(4)
                    turn(2)
                    sums(5)
                    second(0)
                    turn(3)
                    sums(6)
                    second(1)
                    sums(7)
            for _ in chunks(t, chunk):
                pass

def tail_phase(nc, ctx, d, wts, slotf):
    ph = Phase(nc, ctx, "tl")
    sb, bank, sem, count = ph.sb, ph.bank, ph.sem, ph.count
    wo = sb("wo", [P, G, D])
    wf1 = sb("wf1", [P, KD, DF])
    wf2 = sb("wf2", [P, KF, D])
    ws1 = sb("ws1", [P, KD, 2 * FS])
    ws2 = sb("ws2", [P, KS, D])
    mult = sb("mult", [P, KS])
    ident = sb("ident", [P, P])
    bf1 = sb("bf1", [P, KF])
    bs1 = sb("bs1", [P, 2 * KS])
    ln2 = sb("ln2", [P, 2, KD])
    brow = [sb(f"brow{n}", [P, D]) for n in range(2)]
    eps = sb("eps", [P, 1])
    fence = sb("fence", [P, 2])
    idx_all = sb("idx_all", [P, NCH, TOPK, TPC], U32)

    y = [sb(f"y{p}", [P, G, CH]) for p in range(2)]
    xn = [sb(f"xn{p}", [P, TPC, D]) for p in range(2)]
    xnT = [sb(f"xnT{p}", [P, KD, CH]) for p in range(2)]
    x = [sb(f"x{p}", [P, TPC, D]) for p in range(2)]
    idx = [sb(f"idx{p}", [P, TOPK * TPC], U32) for p in range(2)]
    rows = [sb(f"rows{p}", [P, TOPK, TPC, D]) for p in range(2)]
    x1 = sb("res", [P, TPC, D])
    xh = sb("xh", [P, TPC, D])
    xhT = sb("xhT", [P, KD, CH])
    stats = sb("stats", [P, TPC, 6])
    mv = sb("mv", [P, TPC, 2])
    sd = sb("sd", [P, TPC])
    rs = sb("rs", [P, TPC])
    ff = sb("ff", [P, KF, CH])
    gate = sb("gate", [P, 2, CH])
    sh = sb("sh", [P, KS, CH])
    acc = sb("acc", [P, TPC, D])
    out = [sb(f"out{p}", [P, TPC, D]) for p in range(2)]

    pO = [bank(f"pO{q}") for q in range(2)]
    pT = [bank(f"pT{k}") for k in range(KD)]
    pF = [bank(f"pF{n}") for n in range(2)]
    pR = [bank(f"pR{q}") for q in range(2)]

    w_in, const_set, rounds = sem("w_in"), sem("const_set"), sem("rounds")
    ld = [count(f"ld{p}", 64, start=0) for p in range(2)]
    got = [count(f"got{p}", 16 * TOPK * TPC, start=0) for p in range(2)]
    idx_set = count("idx_set", 1)
    o_done, x1_done = count("o_done", 2), count("x1_done", 2)
    dve = count("dve", NORM)
    sd_ready, xh_done = count("sd_ready", 1), count("xh_done", TPC)
    tr_done, tr_out = count("tr_done", KD), count("tr_out", KD)
    s1_done, s1_out = count("s1_done", 2 * KS), count("s1_out", KS)
    sh_done = count("sh_done", KS)
    f1_done, f1_out = count("f1_done", KF), count("f1_out", KF)
    r_done = count("r_done", 2)
    acc_step = count("acc_step", 2 + TOPK)
    out_done = count("out_done", 2)
    out_st = [count(f"out_st{p}", 16) for p in range(2)]
    pair = lambda ap, q: ap[:, 2 * q:2 * q + 2, :]

    names = (("out_proj_w", wo), ("ffn_w1", wf1), ("ffn_w2", wf2), ("s_fc1_w", ws1), ("s_fc2_w", ws2),
             ("s_mult", mult), ("ident", ident), ("ffn_b1", bf1), ("s_fc1_b", bs1), ("ln2", ln2))
    NW = 16 * (len(names) + 2)
    with nc.Block() as block:
        @block.sync
        def _(sp):
            ph.credit(sp)
            for name, dst in names:
                sp.dma_start(dst[:], d[name]).then_inc(w_in, 16)
            for n, name in enumerate(("ffn_b2", "s_fc2_b")):
                sp.dma_start(brow[n][:], d[name].to_broadcast([P, D])).then_inc(w_in, 16)

        @block.vector
        def _(v):
            nc.vector.memset(fence[:], 0.0)
            nc.vector.memset(eps[:], EPS)
            nc.vector.tensor_copy(idx_all[:], slotf[:].rearrange("p k (c t) -> p c k t", t=TPC))
            v.wait_ge(w_in, NW)
            nc.vector.tensor_tensor(brow[0][:], brow[0][:], brow[1][:], ALU.add)
            nc.vector.tensor_tensor(ws2[:], ws2[:], mult[:].rearrange("p (k o) -> p k o", o=1)
                                    .to_broadcast([P, KS, D]), ALU.mult)

    tiles = lambda name: d[name].rearrange("(i q t p) w -> i q p t w", q=2, t=TPC, p=P)
    with nc.Block() as block:
        @block.sync
        def _(sp):
            with sp.Fori(0, NCH // 2) as i:
                for p in range(2):
                    sp.wait_ge(out_done.sem, out_done.at(2 * i + p, 2))
                    sp.dma_start(tiles("out")[i, p], out[p][:]).then_inc(out_st[p].sem, 16)
            for p in range(2):
                sp.wait_ge(out_st[p].sem, out_st[p].at(NCH // 2, 0))

        @block.gpsimd
        def _(pool):
            with pool.Fori(0, NCH // 2) as i:
                for p in range(2):
                    c = 2 * i + p
                    pool.wait_ge(out_done.sem, out_done.at(c, 2, back=2))
                    pool.sem_inc(rounds, 1)
                    for dst, src in ((y, d["y"].rearrange("(i q) g p t -> i q p g t", q=2)[i, p]),
                                     (xn, tiles("xn")[i, p]),
                                     (xnT, d["xnT"].rearrange("(i q) p k t -> i q p k t", q=2)[i, p]),
                                     (x, tiles("x")[i, p])):
                        pool.dma_start(dst[p][:], src).then_inc(ld[p].sem, 16)
                    nc.gpsimd.tensor_copy(idx[p][:], idx_all[:].rearrange("p c k t -> p (c k t)")[
                        :, bass.ds(c * (TOPK * TPC), TOPK * TPC)]).then_inc(idx_set.sem, 1)
                    pool.wait_ge(idx_set.sem, idx_set.at(c, 1))
                    pool.sem_inc(rounds, 1)
                    for k in range(TOPK):
                        for j in range(TPC):
                            n = k * TPC + j
                            pool.indirect_dma_start(rows[p][:, k, j, :], None, d["slot_y"],
                                                    bass.IndirectOffsetOnAxis(idx[p][:, n:n + 1], 0))\
                                .then_inc(got[p].sem, 16)

        @block.vector
        def _(v):
            vec = nc.vector
            with v.Fori(0, NCH // 2) as i:
                for p in range(2):
                    c = 2 * i + p
                    n = [0]
                    v.wait_ge(ld[p].sem, ld[p].at(i, 64))
                    v.wait_ge(acc_step.sem, acc_step.at(c, 1, back=1))
                    for q in range(2):
                        v.wait_ge(o_done.sem, o_done.at(c, q + 1))
                        vec.tensor_tensor(pair(x1, q), pair(xn[p], q), pO[q][:].rearrange("p (t w) -> p t w", t=2),
                                          ALU.add).then_inc(x1_done.sem, 1)
                    v.wait_ge(x1_done.sem, x1_done.at(c, 2))
                    v.wait_ge(tr_done.sem, tr_done.at(c, KD, back=1))
                    norm_steps(nc, v, dve, c, n, x1, xh, stats, mv, sd, rs, fence, sd_ready, 0, xh_done)
                    assert n[0] == NORM
                    v.wait_ge(r_done.sem, r_done.at(c, 2, back=1))
                    for k in range(KS):
                        v.wait_ge(s1_out.sem, s1_out.at(c, k + 1))
                        v.wait_ge(s1_done.sem, s1_done.at(c, 2 * k + 2))
                        vec.scalar_tensor_tensor(sh[:, k, :], pF[1][:], bs1[:, k:k + 1], gate[:, k % 2, :],
                                                 ALU.add, ALU.mult).then_inc(sh_done.sem, 1)
                    vec.tensor_tensor(acc[:], x1[:], x[p][:], ALU.add).then_inc(acc_step.sem, 1)
                    v.wait_ge(acc_step.sem, acc_step.at(c, 1))
                    vec.tensor_tensor(acc[:], acc[:], brow[0][:].rearrange("p (o w) -> p o w", o=1)
                                      .to_broadcast([P, TPC, D]), ALU.add).then_inc(acc_step.sem, 1)
                    v.wait_ge(acc_step.sem, acc_step.at(c, 2))
                    v.wait_ge(got[p].sem, got[p].at(i, got[p].per))
                    for k in range(TOPK):
                        for j in range(TPC):
                            ins = vec.scalar_tensor_tensor(acc[:, j, :], rows[p][:, k, j, :],
                                                           wts[:, k, bass.ds(c * TPC + j, 1)], acc[:, j, :],
                                                           ALU.mult, ALU.add)
                        ins.then_inc(acc_step.sem, 1)
                        v.wait_ge(acc_step.sem, acc_step.at(c, k + 3))
                    v.wait_ge(out_st[p].sem, out_st[p].at(i, 16, back=1))
                    for q in range(2):
                        v.wait_ge(r_done.sem, r_done.at(c, q + 1))
                        vec.tensor_tensor(pair(out[p], q), pair(acc, q), pR[q][:].rearrange("p (t w) -> p t w", t=2),
                                          ALU.add).then_inc(out_done.sem, 1)

        @block.scalar
        def _(a):
            act = nc.scalar.activation
            with a.Fori(0, NCH // 2) as i:
                for p in range(2):
                    c = 2 * i + p
                    a.wait_ge(dve.sem, dve.at(c, 2 * TPC))
                    act(sd[:], mv[:, :, 1], ACT.Sqrt, bias=eps[:, 0:1]).then_inc(sd_ready.sem, 1)
                    for k in range(KS):
                        a.wait_ge(sh_done.sem, sh_done.at(c, k - 1))
                        a.wait_ge(s1_done.sem, s1_done.at(c, 2 * k + 1))
                        act(gate[:, k % 2, :], pF[0][:], ACT.Gelu, bias=bs1[:, KS + k:KS + k + 1])\
                            .then_inc(s1_out.sem, 1)
                    a.wait_ge(f1_done.sem, f1_done.at(c, KF, back=1))
                    for k in range(KD):
                        a.wait_ge(tr_done.sem, tr_done.at(c, k + 1))
                        act(xhT[:, k, :], pT[k][:], ACT.Identity, bias=ln2[:, 1, k:k + 1],
                            scale=ln2[:, 0, k:k + 1]).then_inc(tr_out.sem, 1)
                    a.wait_ge(r_done.sem, r_done.at(c, 2, back=1))
                    for k in range(KF):
                        a.wait_ge(f1_done.sem, f1_done.at(c, k + 1))
                        act(ff[:, k, :], pF[k % 2][:], ACT.Gelu_apprx_tanh, bias=bf1[:, k:k + 1]).then_inc(f1_out.sem, 1)

        @block.tensor
        def _(t):
            mm = nc.tensor.matmul
            with t.Fori(0, NCH // 2) as i:
                for p in range(2):
                    c = 2 * i + p
                    t.wait_ge(ld[p].sem, ld[p].at(i, 64))
                    for q in range(2):
                        t.wait_ge(x1_done.sem, x1_done.at(c, q + 1, back=1))
                        for j in range(2):
                            for g in range(G):
                                ins = mm(pO[q][:, j * D:(j + 1) * D], y[p][:, g, (2 * q + j) * P:(2 * q + j + 1) * P],
                                         wo[:, g, :], start=(g == 0), stop=(g == G - 1))
                        ins.then_inc(o_done.sem, 1)
                    for k in range(KS):
                        for n, col in ((0, FS + k * P), (1, k * P)):
                            if k:
                                if n:
                                    t.wait_ge(sh_done.sem, sh_done.at(c, k))
                                else:
                                    t.wait_ge(s1_out.sem, s1_out.at(c, k))
                            elif n == 0:
                                t.wait_ge(f1_out.sem, f1_out.at(c, KF, back=1))
                            for kk in range(KD):
                                ins = mm(pF[n][:], ws1[:, kk, col:col + P], xnT[p][:, kk, :],
                                         start=(kk == 0), stop=(kk == KD - 1))
                            ins.then_inc(s1_done.sem, 1)
                    t.wait_ge(xh_done.sem, xh_done.at(c, TPC))
                    for k in range(KD):
                        t.wait_ge(tr_out.sem, tr_out.at(c, k + 1, back=1))
                        for j in range(TPC):
                            ins = nc.tensor.transpose(pT[k][:, j * P:(j + 1) * P], xh[:, j, k * P:(k + 1) * P],
                                                      ident[:])
                        ins.then_inc(tr_done.sem, 1)
                    t.wait_ge(tr_out.sem, tr_out.at(c, KD))
                    for k in range(KF):
                        if k < 2:
                            t.wait_ge(sh_done.sem, sh_done.at(c, KS))
                        else:
                            t.wait_ge(f1_out.sem, f1_out.at(c, k - 1))
                        for kk in range(KD):
                            ins = mm(pF[k % 2][:], wf1[:, kk, k * P:(k + 1) * P], xhT[:, kk, :],
                                     start=(kk == 0), stop=(kk == KD - 1))
                        ins.then_inc(f1_done.sem, 1)
                    t.wait_ge(f1_out.sem, f1_out.at(c, KF))
                    for q in range(2):
                        t.wait_ge(out_done.sem, out_done.at(c, q + 1, back=1))
                        for j in range(2):
                            dst, col = pR[q][:, j * D:(j + 1) * D], (2 * q + j) * P
                            for k in range(KF):
                                mm(dst, ff[:, k, col:col + P], wf2[:, k, :], start=(k == 0), stop=False)
                            for k in range(KS):
                                ins = mm(dst, sh[:, k, col:col + P], ws2[:, k, :], start=False, stop=(k == KS - 1))
                        ins.then_inc(r_done.sem, 1)


SCRATCH = {
    "xn": (T, D), "xnT": (NCH, P, KD, CH), "sz": (NCH, G, P, CH), "xc": (NCH, G, P, CH),
    "bc": (NCH, 2 * NS, CH), "dt": (NCH, G, P, CH), "dtx": (NCH, G, P, CH),
    "slot_x": (NSLOT, D), "slot_y": (NSLOT, D), "y": (NCH, G, P, CH),
}
DEBUG = False


def build(nc, d):
    for name, shape in SCRATCH.items():
        d[name] = nc.dram_tensor(f"{name}_dram", shape, F32, kind="ExternalOutput" if DEBUG else "Internal").ap()
    d["moe_b"] = nc.dram_tensor("moe_b_dram", (E, 3, 2 * F + D), BF16, kind="Internal").ap()
    with ExitStack() as ctx:
        def sb(name, shape, dt=F32):
            return ctx.enter_context(nc.sbuf_tensor(name, shape, dt))

        wts = sb("wts", [P, TOPK, NT])
        slotf = sb("slotf", [P, TOPK, NT])
        block_e = sb("block_e", [1, NBLK], I32)
        scores = ExitStack()
        logits = scores.enter_context(nc.sbuf_tensor("logits", [P, NT, EP], F32, side="right"))
        with ExitStack() as inner:
            head_phase(nc, inner, d, logits)
        with ExitStack() as experts:
            w1 = experts.enter_context(nc.sbuf_tensor("w1", [P, E * KD, 2 * F], F32))
            w2 = experts.enter_context(nc.sbuf_tensor("w2", [P, E * KD, D], F32))
            with ExitStack() as inner:
                route_phase(nc, inner, d, logits, wts, block_e, slotf, w1, w2)
            scores.close()
            with ExitStack() as inner:
                scan_phase(nc, inner, d, block_e, w1, w2)
        with ExitStack() as inner:
            tail_phase(nc, inner, d, wts, slotf)


def arrange(inputs):
    a = {k: np.asarray(v) for k, v in inputs.items()}
    m, f = (lambda n: a["L0_attn_" + n]), (lambda n: a["L0_ffn_" + n])
    rows = lambda w: w.reshape(-1, P, w.shape[-1]).transpose(1, 0, 2)
    cols = lambda v: v.reshape(-1, P).T
    out = {
        "x": m("x").reshape(T, D),
        "in_proj_w": rows(m("in_proj_w")), "x_proj_w": rows(m("x_proj_w")), "dt_proj_w": m("dt_proj_w"),
        "gate_w": rows(f("gate_w").T), "conv_w": m("conv_w").reshape(G, P, CONV).transpose(1, 0, 2),
        "ln1": np.stack([cols(m("ln1_g")), cols(m("ln1_b"))], 1),
        "inner_bias": np.stack([cols(m("conv_b")), cols(m("dt_proj_b"))], 1),
        "ident": np.eye(P, dtype=np.float32),
        "tri": np.triu(np.ones((P, P), np.float32), 1), "ones": np.ones((P, P), np.float32),
        "rev": np.broadcast_to(np.float32(EP) - np.arange(EP, dtype=np.float32), (P, NT, EP)),
        "blk": np.broadcast_to(np.arange(NBLK, dtype=np.float32)[:, None], (1, NBLK, EP)),
        "sel": np.kron(np.eye(BPI, dtype=np.float32), np.ones((3, P), np.float32)),
        "fc1_w": f("fc1_w").reshape(E, 2 * F, KD, P).transpose(3, 0, 2, 1).reshape(P, E * KD, 2 * F),
        "fc2_w": f("fc2_w").reshape(E, D, F // P, P).transpose(3, 0, 2, 1).reshape(P, E * KD, D),
        "fc1_b": f("fc1_b"), "fc2_b": f("fc2_b"),
        "geglu_mult": f("geglu_mult").reshape(E * KD, P).T,
        "out_proj_w": rows(m("out_proj_w")), "ffn_w1": rows(m("ffn_w1")), "ffn_w2": rows(m("ffn_w2")),
        "s_fc1_w": rows(f("s_fc1_w").T), "s_fc2_w": rows(f("s_fc2_w").T), "s_mult": cols(f("s_geglu_mult")),
        "ffn_b1": cols(m("ffn_b1")), "s_fc1_b": cols(f("s_fc1_b")),
        "ffn_b2": m("ffn_b2").reshape(1, D), "s_fc2_b": f("s_fc2_b").reshape(1, D),
        "ln2": np.stack([cols(m("ln2_g")), cols(m("ln2_b"))], 1),
        "A_log": m("A_log").reshape(G, P, NS).transpose(1, 0, 2), "D": cols(m("D")),
    }
    return {k: np.ascontiguousarray(v) for k, v in out.items()}


def kernel(**inputs):
    import concourse.bacc as bacc
    from concourse.bass_utils import run_bass_kernel_spmd

    nc = bacc.Bacc("TRN2", target_bir_lowering=False, num_devices=1)
    arrays = arrange(inputs)
    d = {n: nc.dram_tensor(n + "_in", a.shape, mybir.dt.from_np(a.dtype), kind="ExternalInput").ap()
         for n, a in arrays.items()}
    d["out"] = nc.dram_tensor("out", (T, D), F32, kind="ExternalOutput").ap()
    build(nc, d)
    r = run_bass_kernel_spmd(nc, [{n + "_in": a for n, a in arrays.items()}], core_ids=[0])
    return r.results[0]["out"].reshape(B, L, D)
```

```python
from contextlib import ExitStack

import numpy as np

import concourse.bass as bass
from concourse import mybir

F32 = mybir.dt.float32
BF16 = mybir.dt.bfloat16
I32 = mybir.dt.int32
U32 = mybir.dt.uint32
ALU = mybir.AluOpType
ACT = mybir.ActivationFunctionType
AX = mybir.AxisListType

P = 128
B, L, D = 2, 2048, 256
T = B * L
CH = 512
NCH = T // CH
CPB = L // CH
TPC = CH // P
NT = T // P
KD = D // P
DI = 512
G = DI // P
NS = 16
RK = 16
XP = RK + 2 * NS
CONV = 4
DF = 1024
KF = DF // P
E, TOPK = 15, 3
EP = 16
F = 256
FS = 512
KS = FS // P
BPI = 4
NBLK = -(-((T * TOPK + E * (P - 1)) // P) // BPI) * BPI
NSLOT = NBLK * P
MOE_CHUNKS = -(-NBLK // (BPI * G))
EPS = 1e-5


class Count:

    def __init__(self, sem, per, start=2):
        self.sem, self.per, self.start = sem, per, start

    def at(self, c, k, back=0):
        return c * self.per + ((self.start - back) * self.per + k)


class Phase:

    def __init__(self, nc, ctx, tag):
        self.nc, self.ctx, self.tag, self.counts = nc, ctx, tag, []

    def sb(self, name, shape, dt=F32):
        return self.ctx.enter_context(self.nc.sbuf_tensor(f"{self.tag}_{name}", shape, dt))

    def bank(self, name):
        return self.ctx.enter_context(self.nc.psum_tensor(f"{self.tag}_{name}", [P, 512], F32))

    def sem(self, name):
        return self.ctx.enter_context(self.nc.semaphore(f"{self.tag}_{name}"))

    def count(self, name, per, start=2):
        c = Count(self.sem(name), per, start)
        self.counts.append(c)
        return c

    def credit(self, sp):
        for c in self.counts:
            if c.start:
                sp.sem_inc(c.sem, c.start * c.per)


def norm_steps(nc, v, dve, c, n, src, dst, stats, mv, sd, rs, fence, sd_ready, half, done):
    def settle():
        v.wait_ge(dve.sem, dve.at(c, n[0]))

    for t in range(TPC):
        n[0] += 1
        nc.vector.bn_stats(stats[:, t, :], src[:, t, :]).then_inc(dve.sem, 1)
    settle()
    nc.vector.tensor_copy(fence[:, 0:1], fence[:, 1:2])
    for t in range(TPC):
        n[0] += 1
        nc.vector.bn_aggr(mv[:, t, :], stats[:, t, :]).then_inc(dve.sem, 1)
    v.wait_ge(sd_ready.sem, sd_ready.at(c, half + 1))
    n[0] += 1
    nc.vector.reciprocal(rs[:], sd[:]).then_inc(dve.sem, 1)
    settle()
    for t in range(TPC):
        nc.vector.tensor_scalar(dst[:, t, :], src[:, t, :], mv[:, t, 0:1], rs[:, t:t + 1],
                                ALU.subtract, ALU.mult).then_inc(done.sem, 1)


NORM = 2 * TPC + 1


def gate_phase(nc, ctx, d, logits, consts):
    ph = Phase(nc, ctx, "gt")
    sb, bank, sem, count = ph.sb, ph.bank, ph.sem, ph.count
    wgate = sb("wgate", [P, KD, E])
    ident = sb("ident", [P, P])
    ln1 = sb("ln1", [P, 2, KD])
    zeros = sb("zeros", [P, 4 * D])
    eps = sb("eps", [P, 1])
    fence = sb("fence", [P, 2])
    bf = sb("bf", [E, 2 * F + D])
    bparts = [sb(f"b{n}", [E, 2 * F + D], BF16) for n in range(3)]
    x = [sb(f"x{p}", [P, TPC, D]) for p in range(2)]
    xn = [sb(f"xn{p}", [P, TPC, D]) for p in range(2)]
    xh = [sb(f"xh{p}", [P, TPC, D]) for p in range(2)]
    stats = sb("stats", [P, TPC, 6])
    mv = sb("mv", [P, TPC, 2])
    sd = sb("sd", [P, TPC])
    rs = sb("rs", [P, TPC])
    xnT = [sb(f"xnT{p}", [P, KD, CH]) for p in range(2)]
    xhT = [sb(f"xhT{p}", [P, KD, CH]) for p in range(2)]

    pN = [bank(f"pN{k}") for k in range(KD)]
    pH = [bank(f"pH{k}") for k in range(KD)]
    pL = bank("pL")

    w_in, c_in, const_set, slots_zeroed = sem("w_in"), sem("c_in"), sem("const_set"), sem("slots_zeroed")
    b_in, split, b_out, rounds = sem("b_in"), sem("split"), sem("b_out"), sem("rounds")
    x_in = [count(f"x_in{p}", 16) for p in range(2)]
    dve = count("dve", 2 * NORM)
    sd_ready = count("sd_ready", 2)
    xn_done, xh_done = count("xn_done", TPC), count("xh_done", TPC)
    n_done, n_out = count("n_done", KD), count("n_out", KD)
    h_done, h_out = count("h_done", KD), count("h_out", KD)
    lg_done, lg_out = count("lg_done", 1), count("lg_out", 1)
    st = {n: [count(f"st_{n}{p}", 16) for p in range(2)] for n in ("xn", "xnT", "xhT")}
    ZEROED = NSLOT // (4 * P)
    assert ZEROED % 4 == 0

    with nc.Block() as block:
        @block.sync
        def _(sp):
            ph.credit(sp)
    with nc.Block() as block:
        @block.sync
        def _(sp):
            halves = lambda name: d[name].rearrange("(i q t p) w -> i q p t w", q=2, t=TPC, p=P)
            turned = lambda name: d[name].rearrange("(i q) p k t -> i q p k t", q=2)
            slots = d["slot_x"].rearrange("(n p a) w -> n p (a w)", p=P, a=4)

            def load_x(i, p):
                sp.dma_start(x[p][:], halves("x")[i, p]).then_inc(x_in[p].sem, 16)

            load_x(0, 0)
            for dst, name in ((wgate, "gate_w"), (ident, "ident"), (ln1, "ln1")):
                sp.dma_start(dst[:], d[name]).then_inc(w_in, 16)
            load_x(0, 1)
            sp.dma_start(bf[:, 0:2 * F], d["fc1_b"]).then_inc(b_in, 16)
            sp.dma_start(bf[:, 2 * F:], d["fc2_b"]).then_inc(b_in, 16)
            for dst, name in consts:
                sp.dma_start(dst[:], d[name]).then_inc(c_in, 16)
            sp.wait_ge(const_set, 2)

            def pair(i, load):
                for p in range(2):
                    c = 2 * i + p
                    sp.wait_ge(xn_done.sem, xn_done.at(c, TPC))
                    sp.sem_inc(rounds, 1)
                    sp.dma_start(halves("xn")[i, p], xn[p][:]).then_inc(st["xn"][p].sem, 16)
                    if load:
                        load_x(i + 1, p)
                    sp.wait_ge(n_out.sem, n_out.at(c, KD))
                    sp.sem_inc(rounds, 1)
                    sp.dma_start(turned("xnT")[i, p], xnT[p][:]).then_inc(st["xnT"][p].sem, 16)
                    sp.wait_ge(h_out.sem, h_out.at(c, KD))
                    sp.sem_inc(rounds, 1)
                    sp.dma_start(turned("xhT")[i, p], xhT[p][:]).then_inc(st["xhT"][p].sem, 16)
                for n in range(ZEROED // 4):
                    sp.dma_start(slots[i * (ZEROED // 4) + n], zeros[:]).then_inc(slots_zeroed, 16)

            with sp.Fori(0, NCH // 2 - 1) as i:
                pair(i, True)
            pair(NCH // 2 - 1, False)
            sp.wait_ge(split, 5)
            for n in range(3):
                sp.dma_start(d["moe_b"][:, n, :], bparts[n][:]).then_inc(b_out, 16)
            sp.wait_ge(b_out, 48)
            for s in st["xn"] + st["xnT"] + st["xhT"]:
                sp.wait_ge(s.sem, s.at(NCH // 2, 0))
            sp.wait_ge(slots_zeroed, 16 * ZEROED)
            sp.wait_ge(c_in, 16 * len(consts))

        @block.gpsimd
        def _(pool):
            nc.gpsimd.memset(zeros[:], 0.0).then_inc(const_set, 1)
            nc.gpsimd.memset(eps[:], EPS).then_inc(const_set, 1)
            pool.wait_ge(b_in, 32)
            for n in range(3):
                nc.gpsimd.tensor_copy(bparts[n][:], bf[:]).then_inc(split, 1)
                if n < 2:
                    pool.wait_ge(split, 2 * n + 1)
                    nc.gpsimd.tensor_tensor(bf[:], bf[:], bparts[n][:], ALU.subtract).then_inc(split, 1)
                    pool.wait_ge(split, 2 * n + 2)

        @block.vector
        def _(v):
            nc.vector.memset(fence[:], 0.0)
            nc.vector.memset(logits[:], -1e30)

            def take_logits(c):
                v.wait_ge(lg_done.sem, lg_done.at(c, 1))
                nc.vector.tensor_scalar(logits[:, bass.ds(c * TPC, TPC), 0:E],
                                        pL[:, 0:TPC * E].rearrange("p (t e) -> p t e", e=E), 1.0, None,
                                        ALU.mult).then_inc(lg_out.sem, 1)

            def chunk(i, p, first=False):
                c = 2 * i + p
                n = [0]
                ln = (stats, mv, sd, rs, fence, sd_ready)
                v.wait_ge(x_in[p].sem, x_in[p].at(i, 16))
                v.wait_ge(xh_done.sem, xh_done.at(c, 0))
                v.wait_ge(st["xn"][p].sem, st["xn"][p].at(i, 16, back=1))
                v.wait_ge(n_done.sem, n_done.at(c, KD, back=2))
                norm_steps(nc, v, dve, c, n, x[p], xn[p], *ln, 0, xn_done)
                if not first:
                    take_logits(c - 1)
                v.wait_ge(xn_done.sem, xn_done.at(c, TPC))
                v.wait_ge(h_done.sem, h_done.at(c, KD, back=2))
                norm_steps(nc, v, dve, c, n, xn[p], xh[p], *ln, 1, xh_done)
                assert n[0] == dve.per

            chunk(0, 0, first=True)
            chunk(0, 1)
            with v.Fori(1, NCH // 2) as i:
                for p in range(2):
                    chunk(i, p)
            take_logits(NCH - 1)

        @block.scalar
        def _(a):
            a.wait_ge(const_set, 2)
            a.wait_ge(w_in, 16 * 3)
            act = nc.scalar.activation

            def turned_h(i, p):
                c = 2 * i + p
                a.wait_ge(st["xhT"][p].sem, st["xhT"][p].at(i, 16, back=1))
                for k in range(KD):
                    a.wait_ge(h_done.sem, h_done.at(c, k + 1))
                    act(xhT[p][:, k, :], pH[k][:], ACT.Identity, bias=ln1[:, 1, k:k + 1],
                        scale=ln1[:, 0, k:k + 1]).then_inc(h_out.sem, 1)

            def chunk(i, p, first=False):
                c = 2 * i + p
                a.wait_ge(dve.sem, dve.at(c, 2 * TPC))
                act(sd[:], mv[:, :, 1], ACT.Sqrt, bias=eps[:, 0:1]).then_inc(sd_ready.sem, 1)
                if not first:
                    turned_h(i - (1 - p), 1 - p)
                a.wait_ge(dve.sem, dve.at(c, NORM + 2 * TPC))
                act(sd[:], mv[:, :, 1], ACT.Sqrt, bias=eps[:, 0:1]).then_inc(sd_ready.sem, 1)
                a.wait_ge(st["xnT"][p].sem, st["xnT"][p].at(i, 16, back=1))
                for k in range(KD):
                    a.wait_ge(n_done.sem, n_done.at(c, k + 1))
                    act(xnT[p][:, k, :], pN[k][:], ACT.Copy).then_inc(n_out.sem, 1)

            chunk(0, 0, first=True)
            chunk(0, 1)
            with a.Fori(1, NCH // 2) as i:
                for p in range(2):
                    chunk(i, p)
            turned_h(NCH // 2 - 1, 1)

        @block.tensor
        def _(t):
            t.wait_ge(w_in, 16 * 3)
            with t.Fori(0, NCH // 2) as i:
                for p in range(2):
                    c = 2 * i + p
                    for src, ready, banks, done, out in ((xn[p], xn_done, pN, n_done, n_out),
                                                         (xh[p], xh_done, pH, h_done, h_out)):
                        if src is xh[p]:
                            t.wait_ge(n_out.sem, n_out.at(c, KD))
                            t.wait_ge(lg_out.sem, lg_out.at(c, 1, back=1))
                            for j in range(TPC):
                                for k in range(KD):
                                    ins = nc.tensor.matmul(pL[:, j * E:(j + 1) * E], xnT[p][:, k, j * P:(j + 1) * P],
                                                           wgate[:, k, :], start=(k == 0), stop=(k == KD - 1))
                            ins.then_inc(lg_done.sem, 1)
                        t.wait_ge(ready.sem, ready.at(c, TPC))
                        for k in range(KD):
                            t.wait_ge(out.sem, out.at(c, k + 1, back=1))
                            for j in range(TPC):
                                ins = nc.tensor.transpose(banks[k][:, j * P:(j + 1) * P],
                                                          src[:, j, k * P:(k + 1) * P], ident[:])
                            ins.then_inc(done.sem, 1)


def head_phase(nc, ctx, d, hw, logits, wts, block_e, slotf, idx_all, w1, w2):
    ph = Phase(nc, ctx, "hd")
    sb, bank, sem, count = ph.sb, ph.bank, ph.sem, ph.count
    win, wxp, wdt, convw, bias, tri, ones, rev, mult = hw

    xhT = [sb(f"xhT{p}", [P, KD, CH]) for p in range(2)]
    xi = sb("xi", [P, G, CONV - 1 + CH])
    cv = sb("cv", [P, G, CH])
    xc = [sb(f"xc{p}", [P, G, CH]) for p in range(2)]
    sz = sb("sz", [P, G, CH])
    xd = sb("xd", [XP, CH])
    u = sb("u", [P, G, CH])
    rel = sb("rel", [P, G, CH])
    dt = sb("dt", [P, G, CH])
    dtx = sb("dtx", [P, G, CH])
    keep = sb("keep", [P, NCH])

    assert NT * EP == CH and TOPK < G and NBLK * EP <= G * CH
    sc, work, mask, tot, cum = (w.rearrange("p (t e) -> p t e", e=EP) for w in (
        rel[:, 0, :], u[:, TOPK, :], rel[:, 1, :], rel[:, 2, :], rel[:, 3, :]))
    tot, cum = (w.rearrange("p t e -> p (t e)").rearrange("p (e t) -> p e t", t=NT) for w in (tot, cum))
    one = [u[:, k, :].rearrange("p (t e) -> p t e", e=EP) for k in range(TOPK)]
    blk, le = (w[0:1].rearrange("p g t -> p (g t)")[:, 0:NBLK * EP].rearrange("p (n e) -> p n e", e=EP)
               for w in (dt, dtx))
    m = sb("m", [P, TOPK, NT])
    red = sb("red", [P, NT])
    pick = sb("pick", [P, NT])
    pos = sc
    before = sb("before", [P, EP])
    cnt = sb("cnt", [P, EP])
    cnt_i = sb("cnt_i", [P, EP], I32)
    nb = sb("nb", [P, EP])
    nb_cum = sb("nb_cum", [P, EP])
    onesr = mask
    be = sb("be", [1, NBLK])
    xs = [sb(f"xs{p}", [P, TPC, D]) for p in range(2)]
    idx = [sb(f"idx{p}", [P, TOPK * TPC], U32) for p in range(2)]

    pXI, pZ, pD = ([bank(f"{name}{k}") for k in range(2)] for name in ("pXI", "pZ", "pD"))
    pX, pR = bank("pX"), bank("pR")
    pS = pD[1]

    h_in = [count(f"h_in{p}", 16) for p in range(2)]
    w1_in, w2_in, blk_in, rounds = sem("w1_in"), sem("w2_in"), sem("blk_in"), sem("rounds")
    cstep, sstep = count("cstep", G * (CONV - 1)), count("sstep", 3)
    xi_done, xi_out = count("xi_done", G), count("xi_out", G)
    z_done, z_out = count("z_done", G), count("z_out", G)
    conv_done, carried, xc_done = count("conv_done", G), count("carried", G), count("xc_done", G)
    xp_done, xp_out = count("xp_done", 1), count("xp_out", 1)
    dtp_done, abs_done, rel_done = count("dtp_done", G), count("abs_done", G), count("rel_done", G)
    u_done, lnw_done, dt_done, dtx_done = (count(n, 1) for n in ("u_done", "lnw_done", "dt_done", "dtx_done"))
    min_done = count("min_done", 1)
    st = {n: count(f"st_{n}", 16) for n in ("sz", "xc", "bc", "dt", "dtx")}

    route, exp_done, pe_done, idx_made, scaled = (sem(n) for n in ("route", "exp_done", "pe_done", "idx_made", "scaled"))
    xs_in = [count(f"xs_in{p}", 16, start=0) for p in range(2)]
    idx_set = count("idx_set", 1)
    sent = [[count(f"sent{p}{j}", 16, start=0) for j in range(TOPK * TPC)] for p in range(2)]
    SHIFTED, MASKED = 2, 27

    def steps(eng, step, finish):
        step(0, first=True)
        with eng.Fori(0, NCH // 2 - 1) as i:
            for s in (1, 2):
                step(2 * i + s, p=s % 2)
        step(NCH - 1, p=1, last=True)
        finish(NCH - 1, 1)

    with nc.Block() as block:
        @block.sync
        def _(sp):
            ph.credit(sp)
    with nc.Block() as block:
        @block.sync
        def _(sp):
            def load_h(c, p):
                sp.dma_start(xhT[p][:], d["xhT"][c]).then_inc(h_in[p].sem, 16)

            def store(name, c, src, done, k):
                sp.wait_ge(done.sem, done.at(c, k))
                sp.sem_inc(rounds, 1)
                dst = d[name][c] if name == "bc" else d[name][c].rearrange("g p t -> p g t")
                sp.dma_start(dst, src).then_inc(st[name].sem, 16)

            def rest(c):
                store("dt", c, dt[:], dt_done, 1)
                store("dtx", c, dtx[:], dtx_done, 1)

            def step(s, p=0, first=False, last=False, load=True):
                if load:
                    sp.wait_ge(z_done.sem, z_done.at(s, G))
                    sp.sem_inc(rounds, 1)
                    load_h(s + 2, p)
                if not first:
                    store("bc", s - 1, xd[RK:, :], xp_out, 1)
                store("xc", s, xc[p][:], xc_done, G)
                if not last:
                    store("sz", s + 1, sz[:], z_out, G)
                if not first:
                    rest(s - 1)

            load_h(0, 0)
            sp.dma_start(blk, d["blk"]).then_inc(blk_in, 16)
            load_h(1, 1)
            store("sz", 0, sz[:], z_out, G)
            pieces = NCH - 3
            rows = E * KD // pieces

            def load_w1(n):
                sp.dma_start(w1[:, bass.ds(n * rows, rows), :], d["fc1_w"][:, bass.ds(n * rows, rows), :])\
                    .then_inc(w1_in, 16)

            assert rows * pieces == E * KD
            step(0, first=True)
            sp.dma_start(w2[:], d["fc2_w"]).then_inc(w2_in, 16)
            with sp.Fori(0, NCH // 2 - 2) as i:
                for s in (1, 2):
                    step(2 * i + s, p=s % 2)
                    load_w1(2 * i + (s - 1))
            step(NCH - 3, p=1)
            load_w1(pieces - 1)
            step(NCH - 2, p=0, load=False)
            step(NCH - 1, p=1, load=False, last=True)
            store("bc", NCH - 1, xd[RK:, :], xp_out, 1)
            rest(NCH - 1)
            for s in st.values():
                sp.wait_ge(s.sem, s.at(NCH, 0))
            sp.wait_ge(w1_in, 16 * pieces)

        @block.vector
        def _(v):
            vec = nc.vector
            chain = [0]

            def link(ins):
                chain[0] += 1
                ins.then_inc(route, 1)
                v.wait_ge(route, chain[0])

            def over_e(ap):
                return ap.rearrange("p (t o) -> p t o", o=1).to_broadcast([P, NT, EP])

            vec.memset(keep[:], 1.0)
            link(vec.tensor_reduce(red[:], logits[:], AX.X, ALU.max))
            link(vec.tensor_tensor(work, logits[:], over_e(red[:]), ALU.subtract))
            assert chain[0] == SHIFTED
            v.wait_ge(exp_done, 1)
            link(vec.memset(sc[:, :, E:EP], 0.0))
            link(vec.tensor_reduce(red[:], sc, AX.X, ALU.add))
            link(vec.reciprocal(pick[:], red[:]))
            link(vec.tensor_tensor(sc, sc, over_e(pick[:]), ALU.mult))
            link(vec.memset(sc[:, :, E:EP], -1.0))
            for k in range(TOPK):
                link(vec.tensor_reduce(m[:, k, :], sc, AX.X, ALU.max))
                link(vec.tensor_tensor(work, sc, over_e(m[:, k, :]), ALU.is_equal))
                link(vec.tensor_tensor(work, work, rev[:], ALU.mult))
                link(vec.tensor_reduce(pick[:], work, AX.X, ALU.max))
                link(vec.tensor_tensor(one[k], rev[:], over_e(pick[:]), ALU.is_equal))
                link(vec.scalar_tensor_tensor(sc, one[k], -4.0, sc, ALU.mult, ALU.add))
            link(vec.tensor_tensor(mask, one[0], one[1], ALU.add))
            link(vec.tensor_tensor(mask, mask, one[2], ALU.add))
            assert chain[0] == MASKED, chain[0]
            link(vec.tensor_tensor(red[:], m[:, 0, :], m[:, 1, :], ALU.add))
            link(vec.tensor_tensor(red[:], red[:], m[:, 2, :], ALU.add))
            link(vec.tensor_scalar(red[:], red[:], 1e-20, None, ALU.add))
            link(vec.reciprocal(pick[:], red[:]))
            for k in range(TOPK):
                link(vec.tensor_tensor(wts[:, k, :], m[:, k, :], pick[:], ALU.mult))
            v.wait_ge(pe_done, 2)
            link(vec.memset(onesr, 1.0))
            flat = onesr.rearrange("p t e -> p (t e)")
            link(vec.tensor_copy(tot, pS[:].rearrange("p (t e) -> p e t", e=EP)))
            link(vec.tensor_tensor_scan(cum.rearrange("p e t -> p (e t)"), flat,
                                        tot.rearrange("p e t -> p (e t)"), 0.0, ALU.mult, ALU.add))
            link(vec.memset(before[:, 0:1], 0.0))
            link(vec.tensor_copy(before[:, 1:EP], cum[:, 0:EP - 1, NT - 1]))
            link(vec.tensor_tensor(cnt[:], cum[:, :, NT - 1], before[:], ALU.subtract))
            link(vec.tensor_scalar(cnt[:], cnt[:], float(P - 1), None, ALU.add))
            link(vec.tensor_copy(cnt_i[:], cnt[:]))
            link(vec.tensor_scalar(cnt_i[:], cnt_i[:], 7, None, ALU.logical_shift_right))
            link(vec.tensor_copy(nb[:], cnt_i[:]))
            link(vec.tensor_tensor_scan(nb_cum[:], flat[:, 0:EP], nb[:], 0.0, ALU.mult, ALU.add))
            link(vec.tensor_tensor(nb[:], nb_cum[:], nb[:], ALU.subtract))
            link(vec.scalar_tensor_tensor(before[:], nb[:], float(P), before[:], ALU.mult, ALU.subtract))
            link(vec.tensor_tensor(cum, cum, tot, ALU.subtract))
            link(vec.tensor_tensor(cum, cum, before[:].rearrange("p (e o) -> p e o", o=1)
                                   .to_broadcast([P, EP, NT]), ALU.add))
            link(vec.tensor_tensor(pos, pR[:].rearrange("p (t e) -> p t e", e=EP),
                                   cum.rearrange("p e t -> p t e"), ALU.add))
            for k in range(TOPK):
                link(vec.tensor_tensor(work, pos, one[k], ALU.mult))
                link(vec.tensor_reduce(slotf[:, k, :], work, AX.X, ALU.add))
            vec.tensor_copy(idx_all[:], slotf[:].rearrange("p k (c t) -> p c k t", t=TPC)).then_inc(idx_made, 1)
            v.wait_ge(blk_in, 16)
            link(vec.tensor_tensor(le, nb_cum[0:1, :].rearrange("p (o e) -> p o e", o=1)
                                   .to_broadcast([1, NBLK, EP]), blk, ALU.is_le))
            link(vec.tensor_reduce(be[:], le[:, :, 0:E], AX.X, ALU.add))
            link(vec.tensor_scalar(be[:], be[:], float(E - 1), None, ALU.min))
            link(vec.memset(keep[:, CPB - 1:CPB], 0.0))
            vec.tensor_copy(block_e[:], be[:])
            for g in range(G):
                vec.memset(xi[:, g, 0:CONV - 1], 0.0)

            def conv(s):
                n = 0
                for k in reversed(range(CONV)):
                    for g in range(G):
                        if k == CONV - 1:
                            v.wait_ge(xi_out.sem, xi_out.at(s, g + 1))
                            v.wait_ge(xc_done.sem, xc_done.at(s, g + 1, back=1))
                            vec.tensor_scalar(cv[:, g, :], xi[:, g, k:k + CH], convw[:, g, k:k + 1],
                                              None, ALU.mult).then_inc(cstep.sem, 1)
                            n += 1
                            continue
                        if g == 0:
                            v.wait_ge(cstep.sem, cstep.at(s, n))
                        ins = vec.scalar_tensor_tensor(cv[:, g, :], xi[:, g, k:k + CH], convw[:, g, k:k + 1],
                                                       cv[:, g, :], ALU.mult, ALU.add)
                        if k:
                            ins.then_inc(cstep.sem, 1)
                            n += 1
                        else:
                            ins.then_inc(conv_done.sem, 1)
                for g in range(G):
                    v.wait_ge(conv_done.sem, conv_done.at(s, g + 1))
                    vec.tensor_scalar(xi[:, g, 0:CONV - 1], xi[:, g, CH:], keep[:, bass.ds(s, 1)], None, ALU.mult)\
                        .then_inc(carried.sem, 1)

            def softplus(c, p):
                v.wait_ge(st["dt"].sem, st["dt"].at(c, 16, back=1))
                v.wait_ge(u_done.sem, u_done.at(c, 1))
                v.wait_ge(dtx_done.sem, dtx_done.at(c, 0))
                vec.tensor_scalar(dt[:], u[:], 1.0, -1.0, ALU.add, ALU.add).then_inc(sstep.sem, 1)
                v.wait_ge(sstep.sem, sstep.at(c, 1))
                vec.tensor_tensor(dt[:], u[:], dt[:], ALU.subtract).then_inc(sstep.sem, 1)
                v.wait_ge(sstep.sem, sstep.at(c, 2))
                v.wait_ge(lnw_done.sem, lnw_done.at(c, 1))
                vec.tensor_tensor(dt[:], dt[:], dtx[:], ALU.add).then_inc(sstep.sem, 1)
                v.wait_ge(sstep.sem, sstep.at(c, 3))
                vec.tensor_tensor(dt[:], dt[:], u[:], ALU.min).then_inc(min_done.sem, 1)
                v.wait_ge(min_done.sem, min_done.at(c, 1))
                vec.tensor_tensor(dt[:], dt[:], rel[:], ALU.add).then_inc(dt_done.sem, 1)
                v.wait_ge(dt_done.sem, dt_done.at(c, 1))
                vec.tensor_tensor(dtx[:], dt[:], xc[p][:], ALU.mult).then_inc(dtx_done.sem, 1)

            def step(s, p=0, first=False, last=False):
                conv(s)
                if not first:
                    softplus(s - 1, 1 - p)

            steps(v, step, softplus)

        @block.scalar
        def _(a):
            act = nc.scalar.activation
            a.wait_ge(route, SHIFTED)
            act(sc, work, ACT.Exp).then_inc(exp_done, 1)

            def project_in(c, groups=range(G)):
                a.wait_ge(st["sz"].sem, st["sz"].at(c, 16, back=1))
                for g in groups:
                    a.wait_ge(carried.sem, carried.at(c, g + 1, back=1))
                    a.wait_ge(xi_done.sem, xi_done.at(c, g + 1))
                    act(xi[:, g, CONV - 1:], pXI[g % 2][:], ACT.Copy).then_inc(xi_out.sem, 1)
                    a.wait_ge(z_done.sem, z_done.at(c, g + 1))
                    act(sz[:, g, :], pZ[g % 2][:], ACT.Silu).then_inc(z_out.sem, 1)

            def small(c):
                a.wait_ge(st["bc"].sem, st["bc"].at(c, 16, back=1))
                a.wait_ge(dtp_done.sem, dtp_done.at(c, G, back=1))
                a.wait_ge(xp_done.sem, xp_done.at(c, 1))
                act(xd[:], pX[0:XP, :], ACT.Copy).then_inc(xp_out.sem, 1)

            def finish(c, p):
                a.wait_ge(dt_done.sem, dt_done.at(c, 1, back=1))
                for g in range(G):
                    a.wait_ge(dtp_done.sem, dtp_done.at(c, g + 1))
                    act(u[:, g, :], pD[g % 2][:], ACT.Abs, bias=bias[:, 1, g:g + 1]).then_inc(abs_done.sem, 1)
                    act(rel[:, g, :], pD[g % 2][:], ACT.Relu, bias=bias[:, 1, g:g + 1]).then_inc(rel_done.sem, 1)
                a.wait_ge(abs_done.sem, abs_done.at(c, G))
                act(u[:], u[:], ACT.Exp, scale=-1.0).then_inc(u_done.sem, 1)
                a.wait_ge(u_done.sem, u_done.at(c, 1))
                a.wait_ge(st["dtx"].sem, st["dtx"].at(c, 16, back=1))
                act(dtx[:], u[:], ACT.Ln, bias=1.0).then_inc(lnw_done.sem, 1)

            def step(s, p=0, first=False, last=False):
                if not first:
                    finish(s - 1, 1 - p)
                a.wait_ge(st["xc"].sem, st["xc"].at(s, 16, back=2))
                a.wait_ge(dtx_done.sem, dtx_done.at(s, 1, back=2))
                for g in range(G):
                    a.wait_ge(conv_done.sem, conv_done.at(s, g + 1))
                    act(xc[p][:, g, :], cv[:, g, :], ACT.Silu, bias=bias[:, 0, g:g + 1]).then_inc(xc_done.sem, 1)
                if not last:
                    project_in(s + 1, range(G // 2))
                small(s)
                if not last:
                    project_in(s + 1, range(G // 2, G))

            project_in(0)
            steps(a, step, finish)

        @block.tensor
        def _(t):
            mm = nc.tensor.matmul

            def project_in(c, p, i, groups=range(G)):
                t.wait_ge(h_in[p].sem, h_in[p].at(i, 16))
                for g in groups:
                    for col, dst, ready, out in ((g * P, pXI, xi_done, xi_out), (DI + g * P, pZ, z_done, z_out)):
                        t.wait_ge(out.sem, out.at(c, g - 1))
                        for k in range(KD):
                            ins = mm(dst[g % 2][:], win[:, k, col:col + P], xhT[p][:, k, :],
                                     start=(k == 0), stop=(k == KD - 1))
                        ins.then_inc(ready.sem, 1)

            def x_proj(c, p):
                t.wait_ge(xp_out.sem, xp_out.at(c, 1, back=1))
                for g in range(G):
                    t.wait_ge(xc_done.sem, xc_done.at(c, g + 1))
                    ins = mm(pX[0:XP, :], wxp[:, g, :], xc[p][:, g, :], start=(g == 0), stop=(g == G - 1))
                ins.then_inc(xp_done.sem, 1)

            def dt_proj(c):
                t.wait_ge(xp_out.sem, xp_out.at(c, 1))
                for g in range(G):
                    t.wait_ge(rel_done.sem, rel_done.at(c, g - 1))
                    mm(pD[g % 2][:], wdt[:, g * P:(g + 1) * P], xd[0:RK, :], start=True, stop=True)\
                        .then_inc(dtp_done.sem, 1)

            project_in(0, 0, 0)
            t.wait_ge(route, MASKED)
            for dst, lhs in ((pR, tri), (pS, ones)):
                mm(dst[:], lhs[:], mask.rearrange("p t e -> p (t e)"), start=True, stop=True).then_inc(pe_done, 1)

            def step(s, p, i):
                project_in(s + 1, 1 - p, i, range(G // 2))
                x_proj(s, p)
                project_in(s + 1, 1 - p, i, range(G // 2, G))
                dt_proj(s)

            step(0, 0, 0)
            with t.Fori(0, NCH // 2 - 1) as i:
                for s in (1, 2):
                    step(2 * i + s, s % 2, i + 1)
            x_proj(NCH - 1, 1)
            dt_proj(NCH - 1)

        @block.gpsimd
        def _(pool):
            xn_tiles = d["xn"].rearrange("(i q t p) w -> i q p t w", q=2, t=TPC, p=P)

            def load_rows(i, p):
                pool.dma_start(xs[p][:], xn_tiles[i, p]).then_inc(xs_in[p].sem, 16)

            def pair(i, first=False, last=False):
                for p in range(2):
                    c = 2 * i + p
                    if not (first and p == 0):
                        for j in range(TOPK * TPC):
                            pool.wait_ge(sent[1 - p][j].sem, sent[1 - p][j].at(i, 16 * p))
                        pool.sem_inc(rounds, 1)
                    if not (last and p == 1):
                        load_rows(i + p, 1 - p)
                    nc.gpsimd.tensor_copy(idx[p][:], idx_all[:].rearrange("p c k t -> p (c k t)")[
                        :, bass.ds(c * (TOPK * TPC), TOPK * TPC)]).then_inc(idx_set.sem, 1)
                    pool.wait_ge(xs_in[p].sem, xs_in[p].at(i, 16))
                    pool.wait_ge(idx_set.sem, idx_set.at(c, 1))
                    pool.sem_inc(rounds, 1)
                    for j in range(TOPK * TPC):
                        pool.indirect_dma_start(
                            d["slot_x"], bass.IndirectOffsetOnAxis(idx[p][:, j:j + 1], 0), xs[p][:, j % TPC, :], None,
                        ).then_inc(sent[p][j].sem, 16)

            load_rows(0, 0)
            pool.wait_ge(idx_made, 1)
            pair(0, first=True)
            with pool.Fori(1, NCH // 2 - 1) as i:
                pair(i)
            pair(NCH // 2 - 1, last=True)
            for j in range(TOPK * TPC):
                pool.wait_ge(sent[1][j].sem, sent[1][j].at(NCH // 2, 0))
            pool.wait_ge(w2_in, 16)
            nc.gpsimd.tensor_tensor(w2[:], w2[:], mult[:].rearrange("p (n o) -> p n o", o=1)
                                    .to_broadcast([P, E * KD, D]), ALU.mult).then_inc(scaled, 1)
            pool.wait_ge(scaled, 1)


VE_PLAN = {2: (0,), 3: (1,), 4: (2,), 5: (3,)}
ACT_PLAN = {1: (('turn', 0),), 4: (('turn', 1),), 6: (('gelu', 0),), 7: (('turn', 2), ('out', 0), ('turn', 3))}
PE_PLAN = [('turn', 0), ('first', 0), ('sums', 0), ('first', 1), ('turn', 1), ('sums', 1), ('first', 2), ('sums', 2), ('first', 3), ('sums', 3), ('sums', 4), ('sums', 5), ('turn', 2), ('second', 0), ('turn', 3), ('sums', 6), ('second', 1), ('sums', 7)]
POOL_K = 7


def scan_phase(nc, ctx, d, block_e, w1, w2):
    ph = Phase(nc, ctx, "sc")
    NP = NS // 2
    NH = 3
    hb = lambda g, k: h[(g * NP + k) % NH]
    turns = [(j % NH) for j in range(G * NP)]
    since = lambda g, k: next(n for n in range(1, 2 * NH) if turns[(g * NP + k - n) % (G * NP)] == turns[g * NP + k])
    sb, bank, sem, count = ph.sb, ph.bank, ph.sem, ph.count
    ident = sb("ident", [P, P])
    A = sb("A", [P, G, NS])
    Dw = sb("Dw", [P, G])
    state = sb("state", [P, G, NS])
    sel = sb("sel", [3 * BPI, BPI, P], BF16)
    bc = sb("bc", [P, NS // 2, 2, 2, CH])
    dt = [sb(f"dt{p}", [P, CH]) for p in range(2)]
    dtx = [sb(f"dtx{p}", [P, CH]) for p in range(2)]
    xc = sb("xc", [P, CH])
    sz = sb("sz", [P, CH])
    dbx = [sb(f"dbx{p}", [P, 2, CH]) for p in range(2)]
    h = [sb(f"h{p}", [P, 2, CH]) for p in range(NH)]
    yo = sb("yo", [P, CH])
    sel_f = yo[0:3 * BPI, 0:BPI * P]
    xg = sb("xg", [P, BPI, D])
    bb1 = sb("bb1", [3 * BPI, 2 * F], BF16)
    bb2 = sb("bb2", [3 * BPI, D], BF16)
    xT = sb("xT", [P, 2, KD, P])
    hid = sb("hid", [P, BPI, 2 * F])

    pA = [bank(f"pA{n}") for n in range(4)]
    pY, pT = bank("pY"), bank("pT")
    pH = [bank(f"pH{q}") for q in range(2)]

    w_in, const_set, reset, rounds = sem("w_in"), sem("const_set"), sem("reset"), sem("rounds")
    in_ld = [count(f"in_ld{p}", 32 * G // 2) for p in range(2)]
    gate_ld = count("gate_ld", 32 * G)
    bc_ld = [count(f"bc_ld{k}", 32) for k in range(NS // 2)]
    xg_ld = count("xg_ld", 16 * G)
    bb1_ld, bb2_ld = (count(n, 16 * BPI * G) for n in ("bb1_ld", "bb2_ld"))
    exp_done, scan_done = count("exp_done", G * NS), count("scan_done", G * NS)
    dbx_done, prod_done, sum_done = (count(n, G * NS // 2) for n in ("dbx_done", "prod_done", "sum_done"))
    saved = count("saved", G * NS // 2)
    skip_done, y_done = count("skip_done", G), count("y_done", G)
    y_st = count("y_st", 16 * G)
    tr_done, tr_out = count("tr_done", 4 * G), count("tr_out", 4 * G)
    f1_done, f1_out = count("f1_done", BPI * G), count("f1_out", BPI * G)
    gelu_done, act_done = count("gelu_done", G), count("act_done", G)
    f2_done, f2_out = count("f2_done", 2 * G), count("f2_out", 2 * G)
    ye_st = [count(f"ye_st{q}", 16 * G) for q in range(2)]

    def chunks(eng, body, between=None):
        body(0, True, first=True)
        with eng.Fori(1, CPB) as c:
            body(c, True)
        if between:
            between()
        with eng.Fori(CPB, MOE_CHUNKS) as c:
            body(c, True)
        for c in range(MOE_CHUNKS, NCH):
            body(c, False)

    with nc.Block() as block:
        @block.sync
        def _(sp):
            ph.credit(sp)
            for dst, name in ((ident[:], "ident"), (A[:], "A_log"), (Dw[:], "D"), (sel_f, "sel")):
                sp.dma_start(dst, d[name]).then_inc(w_in, 16)

        @block.vector
        def _(v):
            v.wait_ge(w_in, 64)
            nc.vector.tensor_copy(sel[:].rearrange("k b p -> k (b p)"), sel_f).then_inc(const_set, 1)
            nc.vector.memset(state[:], 0.0)
            v.wait_ge(const_set, 2)
            nc.vector.tensor_scalar(A[:], A[:], -1.0, None, ALU.mult)

        @block.scalar
        def _(a):
            a.wait_ge(w_in, 64)
            nc.scalar.activation(A[:], A[:], ACT.Exp).then_inc(const_set, 1)

    with nc.Block() as block:
        @block.sync
        def _(sp):
            def load_inputs(c, g):
                for dst, name in ((dt, "dt"), (dtx, "dtx")):
                    sp.dma_start(dst[g % 2][:], d[name][c, g]).then_inc(in_ld[g % 2].sem, 16)

            def load_bc(c, k):
                sp.wait_ge(prod_done.sem, prod_done.at(c, k + 1 - NP))
                sp.sem_inc(rounds, 1)
                for n in range(2):
                    row = n * NS + 2 * k
                    src = d["bc"][c, row:row + 2, :].rearrange("(o n) t -> o (n t)", o=1)
                    sp.dma_start(bc[:, k, n].rearrange("p n t -> p (n t)"), src.to_broadcast([P, 2 * CH]))\
                        .then_inc(bc_ld[k].sem, 16)

            def load_blocks(c, g):
                p = g % 2
                sp.wait_ge(tr_done.sem, tr_done.at(c, 4 * g - 2))
                sp.sem_inc(rounds, 1)
                sp.dma_start(xg[:], d["slot_x"].rearrange("(c g b p) w -> c g p b w", g=G, b=BPI, p=P)[c, g])\
                    .then_inc(xg_ld.sem, 16)

            def load_biases(c, g, dst, part, ld):
                for b in range(BPI):
                    e = sp.value_load(block_e[0:1, bass.ds(c * (G * BPI) + (g * BPI + b), 1)], min_val=0, max_val=E - 1)
                    sp.dma_start(dst[3 * b:3 * b + 3, :], d["moe_b"][bass.ds(e, 1)].rearrange("o k n -> (o k) n")[:, part])\
                        .then_inc(ld.sem, 16)

            def load_biases1(c, g):
                sp.wait_ge(f1_done.sem, f1_done.at(c, BPI * g))
                sp.sem_inc(rounds, 1)
                load_biases(c, g, bb1, slice(0, 2 * F), bb1_ld)

            def load_biases2(c, g):
                sp.wait_ge(f2_done.sem, f2_done.at(c, 2 * g))
                sp.sem_inc(rounds, 1)
                load_biases(c, g, bb2, slice(2 * F, 2 * F + D), bb2_ld)

            def store_blocks(c, g, q):
                sp.wait_ge(f2_out.sem, f2_out.at(c, 2 * g + q + 1))
                sp.sem_inc(rounds, 1)
                dst = d["slot_y"].rearrange("(c g q b p) w -> c g q p b w", g=G, q=2, b=2, p=P)
                sp.dma_start(dst[c, g, q], hid[:, 2 * q:2 * q + 2, F:]).then_inc(ye_st[q].sem, 16)

            def chunk(c, moe, moe_next, first=False, last=False):
                for g in range(G):
                    sp.wait_ge(y_done.sem, y_done.at(c, g))
                    sp.sem_inc(rounds, 1)
                    if g:
                        sp.dma_start(d["y"][c, g - 1], yo[:]).then_inc(y_st.sem, 16)
                    elif not first:
                        sp.dma_start(d["y"][c - 1, G - 1], yo[:]).then_inc(y_st.sem, 16)
                    for dst, name in ((xc, "xc"), (sz, "sz")):
                        sp.dma_start(dst[:], d[name][c, g]).then_inc(gate_ld.sem, 16)
                    if g < G - 1:
                        load_inputs(c, g + 1)
                        if moe:
                            load_blocks(c, g + 1)
                            load_biases1(c, g + 1)
                            store_blocks(c, g, 0)
                            load_biases2(c, g + 1)
                            store_blocks(c, g, 1)
                        continue
                    if not last:
                        load_inputs(c + 1, 0)
                        load_bc(c + 1, 0)
                        load_bc(c + 1, 1)
                        if moe_next:
                            load_blocks(c + 1, 0)
                        for k in range(2, NP - 2):
                            load_bc(c + 1, k)
                        if moe_next:
                            load_biases1(c + 1, 0)
                    if moe:
                        store_blocks(c, g, 0)
                    if not last:
                        for k in range(NP - 2, NP):
                            load_bc(c + 1, k)
                        if moe_next:
                            load_biases2(c + 1, 0)
                    if moe:
                        store_blocks(c, g, 1)

            load_inputs(0, 0)
            load_bc(0, 0)
            load_blocks(0, 0)
            load_biases1(0, 0)
            for k in range(1, NP):
                load_bc(0, k)
            load_biases2(0, 0)
            chunk(0, True, True, first=True)
            with sp.Fori(1, MOE_CHUNKS - 1) as c:
                chunk(c, True, True)
            chunk(MOE_CHUNKS - 1, True, False, last=MOE_CHUNKS == NCH)
            for c in range(MOE_CHUNKS, NCH):
                chunk(c, False, False, last=c == NCH - 1)
            sp.wait_ge(y_done.sem, y_done.at(NCH, 0))
            sp.dma_start(d["y"][NCH - 1, G - 1], yo[:]).then_inc(y_st.sem, 16)
            sp.wait_ge(y_st.sem, y_st.at(NCH, 0))
            for s in ye_st:
                sp.wait_ge(s.sem, s.at(MOE_CHUNKS, 0))

        @block.gpsimd
        def _(pool):
            def output(c, g):
                pool.wait_ge(skip_done.sem, skip_done.at(c, g + 1))
                nc.gpsimd.tensor_tensor(yo[:], yo[:], sz[:], ALU.mult).then_inc(y_done.sem, 1)

            def chunk(c, moe, first=False):
                for g in range(G):
                    p = g % 2
                    pool.wait_ge(in_ld[p].sem, in_ld[p].at(c, 32 * (g // 2 + 1)))
                    for k in range(NP):
                        if k == 2 and not (first and g == 0):
                            output(c, g - 1)
                        if moe and k == POOL_K:
                            pool.wait_ge(gelu_done.sem, gelu_done.at(c, g + 1))
                            nc.gpsimd.tensor_tensor(hid[:, :, 0:F], hid[:, :, 0:F], hid[:, :, F:], ALU.mult)\
                                .then_inc(act_done.sem, 1)
                        pool.wait_ge(bc_ld[k].sem, bc_ld[k].at(c, 32))
                        pool.wait_ge(scan_done.sem, scan_done.at(c, NS * g + 2 * k - 2))
                        nc.gpsimd.tensor_tensor(dbx[k % 2][:], dtx[p][:].rearrange("p (o t) -> p o t", o=1)
                                                .to_broadcast([P, 2, CH]), bc[:, k, 0], ALU.mult)\
                            .then_inc(dbx_done.sem, 1)
            chunks(pool, chunk)
            output(NCH - 1, G - 1)

        @block.scalar
        def _(a):
            act = nc.scalar.activation

            def chunk(c, moe, first=False):
                for g in range(G):
                    p = g % 2

                    def decays(k):
                        for n in (2 * k, 2 * k + 1):
                            a.wait_ge(scan_done.sem, scan_done.at(c, NS * g + n - 3))
                            act(pA[n % 4][:], dt[p][:], ACT.Exp, scale=A[:, g, n:n + 1]).then_inc(exp_done.sem, 1)

                    def save(k):
                        a.wait_ge(scan_done.sem, scan_done.at(c, NS * g + 2 * k + 2))
                        act(state[:, g, 2 * k:2 * k + 2], hb(g, k)[:, :, CH - 1], ACT.Copy).then_inc(saved.sem, 1)

                    def transposed(n):
                        if n in (0, 3):
                            a.wait_ge(f2_done.sem, f2_done.at(c, 2 * g + (1 if n else 0)))
                        else:
                            a.wait_ge(f1_done.sem, f1_done.at(c, BPI * g + 2 * n))
                        a.wait_ge(tr_done.sem, tr_done.at(c, 4 * g + n + 1))
                        act(xT[:].rearrange("p b k t -> p (b k t)"), pT[:], ACT.Copy).then_inc(tr_out.sem, 1)

                    def out(q, group):
                        a.wait_ge(f2_done.sem, f2_done.at(c, 2 * group + q + 1))
                        act(hid[:, 2 * q:2 * q + 2, F:], pH[q][:].rearrange("p (b w) -> p b w", b=2), ACT.Copy)\
                            .then_inc(f2_out.sem, 1)

                    a.wait_ge(in_ld[p].sem, in_ld[p].at(c, 32 * (g // 2 + 1)))
                    def gelu():
                        a.wait_ge(f1_out.sem, f1_out.at(c, BPI * (g + 1)))
                        act(hid[:, :, F:], hid[:, :, F:], ACT.Gelu).then_inc(gelu_done.sem, 1)

                    decays(0)
                    if not (first and g == 0):
                        h_last = hb((g - 1) % G, NP - 1)
                        a.wait_ge(scan_done.sem, scan_done.at(c, NS * g))
                        act(state[:, (g - 1) % G, NS - 2:NS], h_last[:, :, CH - 1], ACT.Copy).then_inc(saved.sem, 1)
                        if moe or g == 0:
                            out(1, g - 1)
                    for k in range(1, NP):
                        decays(k)
                        save(k - 1)
                        if moe:
                            for name, n in ACT_PLAN.get(k, ()):
                                if name == "turn":
                                    transposed(n)
                                elif name == "gelu":
                                    gelu()
                                else:
                                    out(n, g)
            chunks(a, chunk)
            a.wait_ge(scan_done.sem, scan_done.at(NCH, 0))
            act(state[:, G - 1, NS - 2:NS], hb(G - 1, NP - 1)[:, :, CH - 1], ACT.Copy).then_inc(saved.sem, 1)

        @block.vector
        def _(v):
            vec = nc.vector

            def chunk(c, moe, first=False):
                for g in range(G):
                    p = g % 2

                    def scans(k):
                        v.wait_ge(sum_done.sem, sum_done.at(c, NP * g + k + 1 - since(g, k)))
                        v.wait_ge(dbx_done.sem, dbx_done.at(c, NP * g + k + 1))
                        for j in range(2):
                            n = 2 * k + j
                            v.wait_ge(exp_done.sem, exp_done.at(c, NS * g + n + 1))
                            vec.tensor_tensor_scan(hb(g, k)[:, j, :], pA[n % 4][:], dbx[k % 2][:, j, :],
                                                   state[:, g, n:n + 1], ALU.mult, ALU.add).then_inc(scan_done.sem, 1)

                    def hidden(b):
                        v.wait_ge(tr_done.sem, tr_done.at(c, 4 * g))
                        v.wait_ge(ye_st[b // 2].sem, ye_st[b // 2].at(c, 16 * g))
                        v.wait_ge(f1_done.sem, f1_done.at(c, BPI * g + b + 1))
                        vec.tensor_copy(hid[:, b, :], pH[b % 2][:]).then_inc(f1_out.sem, 1)

                    for k in range(NP):
                        scans(k)
                        if moe:
                            for b in VE_PLAN.get(k, ()):
                                hidden(b)
                        if k:
                            products(c, g, k - 1)
                        elif not (first and g == 0):
                            products(c if g else c - 1, (g - 1) % G, NP - 1)
                            output(c, g - 1)

            def products(c, g, k):
                v.wait_ge(saved.sem, saved.at(c, NP * g + k + 1))
                v.wait_ge(bc_ld[k].sem, bc_ld[k].at(c, 32))
                vec.tensor_tensor(hb(g, k)[:], hb(g, k)[:], bc[:, k, 1], ALU.mult).then_inc(prod_done.sem, 1)

            def output(c, g):
                v.wait_ge(sum_done.sem, sum_done.at(c, NP * (g + 1)))
                v.wait_ge(gate_ld.sem, gate_ld.at(c, 32 * (g + 1)))
                v.wait_ge(y_st.sem, y_st.at(c, 16 * g))
                vec.scalar_tensor_tensor(yo[:], xc[:], Dw[:, g % G:g % G + 1], pY[:], ALU.mult, ALU.add)\
                    .then_inc(skip_done.sem, 1)

            def new_sequence():
                v.wait_ge(saved.sem, saved.at(CPB, 0))
                vec.memset(state[:], 0.0).then_inc(reset, 1)
                v.wait_ge(reset, 1)

            chunks(v, chunk, between=new_sequence)
            products(NCH - 1, G - 1, NP - 1)
            output(NCH - 1, G - 1)

        @block.tensor
        def _(t):
            mm = nc.tensor.matmul

            def chunk(c, moe, first=False):
                for g in range(G):
                    p = g % 2

                    def sums(k):
                        if k == 0:
                            t.wait_ge(skip_done.sem, skip_done.at(c, g))
                        t.wait_ge(prod_done.sem, prod_done.at(c, NP * g + k + 1))
                        for j in range(2):
                            ins = mm(pY[:], ident[:], hb(g, k)[:, j, :], start=(k + j == 0),
                                     stop=(2 * k + j == NS - 1))
                        ins.then_inc(sum_done.sem, 1)

                    def turn(n):
                        t.wait_ge(tr_out.sem, tr_out.at(c, 4 * g + n))
                        if n == 0:
                            t.wait_ge(xg_ld.sem, xg_ld.at(c, 16 * (g + 1)))
                        if n == 2:
                            t.wait_ge(act_done.sem, act_done.at(c, g + 1))
                        src = xg if n < 2 else hid
                        for b in range(2):
                            for k in range(KD):
                                at = (KD * b + k) * P
                                ins = nc.tensor.transpose(pT[:, at:at + P],
                                                          src[:, 2 * (n % 2) + b, k * P:(k + 1) * P], ident[:])
                        ins.then_inc(tr_done.sem, 1)

                    def first(b):
                        if b % 2 == 0:
                            t.wait_ge(tr_out.sem, tr_out.at(c, 4 * g + b // 2 + 1))
                        if b < 2:
                            t.wait_ge(f2_out.sem, f2_out.at(c, 2 * g - 1 + b))
                        else:
                            t.wait_ge(f1_out.sem, f1_out.at(c, BPI * g + b - 1))
                        for k in range(KD):
                            mm(pH[b % 2][:], xT[:, b % 2, k, :], w1[:, bass.ds(e[b] * KD + k, 1), :]
                               .rearrange("p o n -> p (o n)"), start=(k == 0), stop=False)
                        if b == 0:
                            t.wait_ge(bb1_ld.sem, bb1_ld.at(c, 16 * BPI * (g + 1)))
                        mm(pH[b % 2][:], sel[:, b, :], bb1[:], start=False, stop=True)\
                            .then_inc(f1_done.sem, 1)

                    def second(q):
                        t.wait_ge(tr_out.sem, tr_out.at(c, 4 * g + 2 + q + 1))
                        t.wait_ge(f1_out.sem, f1_out.at(c, BPI * g + 3 + q))
                        for j in range(2):
                            dst = pH[q][:, j * D:(j + 1) * D]
                            for k in range(KD):
                                mm(dst, xT[:, j, k, :], w2[:, bass.ds(e[2 * q + j] * KD + k, 1), :]
                                   .rearrange("p o n -> p (o n)"), start=(k == 0), stop=False)
                            if q + j == 0:
                                t.wait_ge(bb2_ld.sem, bb2_ld.at(c, 16 * BPI * (g + 1)))
                            ins = mm(dst, sel[:, 2 * q + j, :], bb2[:], start=False, stop=True)
                        ins.then_inc(f2_done.sem, 1)

                    if not moe:
                        for k in range(NP):
                            sums(k)
                        continue
                    e = [t.value_load(block_e[0:1, bass.ds(c * (G * BPI) + (g * BPI + b), 1)], min_val=0,
                                      max_val=E - 1) for b in range(BPI)]
                    for name, n in PE_PLAN:
                        {"turn": turn, "sums": sums, "first": first, "second": second}[name](n)
            chunks(t, chunk)

def tail_phase(nc, ctx, d, wts, idx_all):
    ph = Phase(nc, ctx, "tl")
    sb, bank, sem, count = ph.sb, ph.bank, ph.sem, ph.count
    wo = sb("wo", [P, G, D])
    wf1 = sb("wf1", [P, KD, DF])
    wf2 = sb("wf2", [P, KF, D])
    ws1 = sb("ws1", [P, KD, 2 * FS])
    ws2 = sb("ws2", [P, KS, D])
    mult = sb("mult", [P, KS])
    ident = sb("ident", [P, P])
    bf1 = sb("bf1", [P, KF])
    bs1 = sb("bs1", [P, 2 * KS])
    ln2 = sb("ln2", [P, 2, KD])
    brow = [sb(f"brow{n}", [P, D]) for n in range(2)]
    eps = sb("eps", [P, 1])
    fence = sb("fence", [P, 2])

    y = [sb(f"y{p}", [P, G, CH]) for p in range(2)]
    xn = [sb(f"xn{p}", [P, TPC, D]) for p in range(2)]
    xnT = [sb(f"xnT{p}", [P, KD, CH]) for p in range(2)]
    x = [sb(f"x{p}", [P, TPC, D]) for p in range(2)]
    idx = [sb(f"idx{p}", [P, TOPK * TPC], U32) for p in range(2)]
    rows = [sb(f"rows{p}", [P, TOPK, TPC, D]) for p in range(2)]
    x1 = sb("res", [P, TPC, D])
    xh = sb("xh", [P, TPC, D])
    xhT = sb("xhT", [P, KD, CH])
    stats = sb("stats", [P, TPC, 6])
    mv = sb("mv", [P, TPC, 2])
    sd = sb("sd", [P, TPC])
    rs = sb("rs", [P, TPC])
    ff = sb("ff", [P, KF, CH])
    gate = sb("gate", [P, 2, CH])
    sh = sb("sh", [P, KS, CH])
    acc = sb("acc", [P, TPC, D])
    out = [sb(f"out{p}", [P, TPC, D]) for p in range(2)]

    pO = [bank(f"pO{q}") for q in range(2)]
    pT = [bank(f"pT{k}") for k in range(KD)]
    pF = [bank(f"pF{n}") for n in range(2)]
    pR = [bank(f"pR{q}") for q in range(2)]

    w_in, const_set, rounds = sem("w_in"), sem("const_set"), sem("rounds")
    ld = [count(f"ld{p}", 64, start=0) for p in range(2)]
    got = [count(f"got{p}", 16 * TOPK * TPC, start=0) for p in range(2)]
    idx_set = count("idx_set", 1)
    o_done, x1_done = count("o_done", 2), count("x1_done", 2)
    dve = count("dve", NORM)
    sd_ready, xh_done = count("sd_ready", 1), count("xh_done", TPC)
    tr_done, tr_out = count("tr_done", KD), count("tr_out", KD)
    s1_done, s1_out = count("s1_done", 2 * KS), count("s1_out", KS)
    sh_done = count("sh_done", KS)
    f1_done, f1_out = count("f1_done", KF), count("f1_out", KF)
    r_done = count("r_done", 2)
    acc_step = count("acc_step", 2 + TOPK)
    out_done = count("out_done", 2)
    out_st = [count(f"out_st{p}", 16) for p in range(2)]
    pair = lambda ap, q: ap[:, 2 * q:2 * q + 2, :]

    names = (("out_proj_w", wo), ("ffn_w1", wf1), ("ffn_w2", wf2), ("s_fc1_w", ws1), ("s_fc2_w", ws2),
             ("s_mult", mult), ("ident", ident), ("ffn_b1", bf1), ("s_fc1_b", bs1), ("ln2", ln2))
    NW = 16 * (len(names) + 2)
    with nc.Block() as block:
        @block.sync
        def _(sp):
            ph.credit(sp)
            for name, dst in names:
                sp.dma_start(dst[:], d[name]).then_inc(w_in, 16)
            for n, name in enumerate(("ffn_b2", "s_fc2_b")):
                sp.dma_start(brow[n][:], d[name].to_broadcast([P, D])).then_inc(w_in, 16)

        @block.vector
        def _(v):
            nc.vector.memset(fence[:], 0.0)
            nc.vector.memset(eps[:], EPS)
            v.wait_ge(w_in, NW)
            nc.vector.tensor_tensor(brow[0][:], brow[0][:], brow[1][:], ALU.add)
            nc.vector.tensor_tensor(ws2[:], ws2[:], mult[:].rearrange("p (k o) -> p k o", o=1)
                                    .to_broadcast([P, KS, D]), ALU.mult)

    tiles = lambda name: d[name].rearrange("(i q t p) w -> i q p t w", q=2, t=TPC, p=P)
    with nc.Block() as block:
        @block.sync
        def _(sp):
            with sp.Fori(0, NCH // 2) as i:
                for p in range(2):
                    sp.wait_ge(out_done.sem, out_done.at(2 * i + p, 2))
                    sp.dma_start(tiles("out")[i, p], out[p][:]).then_inc(out_st[p].sem, 16)
            for p in range(2):
                sp.wait_ge(out_st[p].sem, out_st[p].at(NCH // 2, 0))

        @block.gpsimd
        def _(pool):
            with pool.Fori(0, NCH // 2) as i:
                for p in range(2):
                    c = 2 * i + p
                    pool.wait_ge(out_done.sem, out_done.at(c, 2, back=2))
                    pool.sem_inc(rounds, 1)
                    for dst, src in ((y, d["y"].rearrange("(i q) g p t -> i q p g t", q=2)[i, p]),
                                     (xn, tiles("xn")[i, p]),
                                     (xnT, d["xnT"].rearrange("(i q) p k t -> i q p k t", q=2)[i, p]),
                                     (x, tiles("x")[i, p])):
                        pool.dma_start(dst[p][:], src).then_inc(ld[p].sem, 16)
                    nc.gpsimd.tensor_copy(idx[p][:], idx_all[:].rearrange("p c k t -> p (c k t)")[
                        :, bass.ds(c * (TOPK * TPC), TOPK * TPC)]).then_inc(idx_set.sem, 1)
                    pool.wait_ge(idx_set.sem, idx_set.at(c, 1))
                    pool.sem_inc(rounds, 1)
                    for k in range(TOPK):
                        for j in range(TPC):
                            n = k * TPC + j
                            pool.indirect_dma_start(rows[p][:, k, j, :], None, d["slot_y"],
                                                    bass.IndirectOffsetOnAxis(idx[p][:, n:n + 1], 0))\
                                .then_inc(got[p].sem, 16)

        @block.vector
        def _(v):
            vec = nc.vector
            with v.Fori(0, NCH // 2) as i:
                for p in range(2):
                    c = 2 * i + p
                    n = [0]
                    v.wait_ge(ld[p].sem, ld[p].at(i, 64))
                    v.wait_ge(acc_step.sem, acc_step.at(c, 1, back=1))
                    for q in range(2):
                        v.wait_ge(o_done.sem, o_done.at(c, q + 1))
                        vec.tensor_tensor(pair(x1, q), pair(xn[p], q), pO[q][:].rearrange("p (t w) -> p t w", t=2),
                                          ALU.add).then_inc(x1_done.sem, 1)
                    v.wait_ge(x1_done.sem, x1_done.at(c, 2))
                    v.wait_ge(tr_done.sem, tr_done.at(c, KD, back=1))
                    norm_steps(nc, v, dve, c, n, x1, xh, stats, mv, sd, rs, fence, sd_ready, 0, xh_done)
                    assert n[0] == NORM
                    v.wait_ge(r_done.sem, r_done.at(c, 2, back=1))
                    for k in range(KS):
                        v.wait_ge(s1_out.sem, s1_out.at(c, k + 1))
                        v.wait_ge(s1_done.sem, s1_done.at(c, 2 * k + 2))
                        vec.scalar_tensor_tensor(sh[:, k, :], pF[1][:], bs1[:, k:k + 1], gate[:, k % 2, :],
                                                 ALU.add, ALU.mult).then_inc(sh_done.sem, 1)
                    vec.tensor_tensor(acc[:], x1[:], x[p][:], ALU.add).then_inc(acc_step.sem, 1)
                    v.wait_ge(acc_step.sem, acc_step.at(c, 1))
                    vec.tensor_tensor(acc[:], acc[:], brow[0][:].rearrange("p (o w) -> p o w", o=1)
                                      .to_broadcast([P, TPC, D]), ALU.add).then_inc(acc_step.sem, 1)
                    v.wait_ge(acc_step.sem, acc_step.at(c, 2))
                    v.wait_ge(got[p].sem, got[p].at(i, got[p].per))
                    for k in range(TOPK):
                        for j in range(TPC):
                            ins = vec.scalar_tensor_tensor(acc[:, j, :], rows[p][:, k, j, :],
                                                           wts[:, k, bass.ds(c * TPC + j, 1)], acc[:, j, :],
                                                           ALU.mult, ALU.add)
                        ins.then_inc(acc_step.sem, 1)
                        v.wait_ge(acc_step.sem, acc_step.at(c, k + 3))
                    v.wait_ge(out_st[p].sem, out_st[p].at(i, 16, back=1))
                    for q in range(2):
                        v.wait_ge(r_done.sem, r_done.at(c, q + 1))
                        vec.tensor_tensor(pair(out[p], q), pair(acc, q), pR[q][:].rearrange("p (t w) -> p t w", t=2),
                                          ALU.add).then_inc(out_done.sem, 1)

        @block.scalar
        def _(a):
            act = nc.scalar.activation
            with a.Fori(0, NCH // 2) as i:
                for p in range(2):
                    c = 2 * i + p
                    a.wait_ge(dve.sem, dve.at(c, 2 * TPC))
                    act(sd[:], mv[:, :, 1], ACT.Sqrt, bias=eps[:, 0:1]).then_inc(sd_ready.sem, 1)
                    for k in range(KS):
                        a.wait_ge(sh_done.sem, sh_done.at(c, k - 1))
                        a.wait_ge(s1_done.sem, s1_done.at(c, 2 * k + 1))
                        act(gate[:, k % 2, :], pF[0][:], ACT.Gelu, bias=bs1[:, KS + k:KS + k + 1])\
                            .then_inc(s1_out.sem, 1)
                    a.wait_ge(f1_done.sem, f1_done.at(c, KF, back=1))
                    for k in range(KD):
                        a.wait_ge(tr_done.sem, tr_done.at(c, k + 1))
                        act(xhT[:, k, :], pT[k][:], ACT.Identity, bias=ln2[:, 1, k:k + 1],
                            scale=ln2[:, 0, k:k + 1]).then_inc(tr_out.sem, 1)
                    a.wait_ge(r_done.sem, r_done.at(c, 2, back=1))
                    for k in range(KF):
                        a.wait_ge(f1_done.sem, f1_done.at(c, k + 1))
                        act(ff[:, k, :], pF[k % 2][:], ACT.Gelu_apprx_tanh, bias=bf1[:, k:k + 1]).then_inc(f1_out.sem, 1)

        @block.tensor
        def _(t):
            mm = nc.tensor.matmul
            with t.Fori(0, NCH // 2) as i:
                for p in range(2):
                    c = 2 * i + p
                    t.wait_ge(ld[p].sem, ld[p].at(i, 64))
                    for q in range(2):
                        t.wait_ge(x1_done.sem, x1_done.at(c, q + 1, back=1))
                        for j in range(2):
                            for g in range(G):
                                ins = mm(pO[q][:, j * D:(j + 1) * D], y[p][:, g, (2 * q + j) * P:(2 * q + j + 1) * P],
                                         wo[:, g, :], start=(g == 0), stop=(g == G - 1))
                        ins.then_inc(o_done.sem, 1)
                    for k in range(KS):
                        for n, col in ((0, FS + k * P), (1, k * P)):
                            if k:
                                if n:
                                    t.wait_ge(sh_done.sem, sh_done.at(c, k))
                                else:
                                    t.wait_ge(s1_out.sem, s1_out.at(c, k))
                            elif n == 0:
                                t.wait_ge(f1_out.sem, f1_out.at(c, KF, back=1))
                            for kk in range(KD):
                                ins = mm(pF[n][:], ws1[:, kk, col:col + P], xnT[p][:, kk, :],
                                         start=(kk == 0), stop=(kk == KD - 1))
                            ins.then_inc(s1_done.sem, 1)
                    t.wait_ge(xh_done.sem, xh_done.at(c, TPC))
                    for k in range(KD):
                        t.wait_ge(tr_out.sem, tr_out.at(c, k + 1, back=1))
                        for j in range(TPC):
                            ins = nc.tensor.transpose(pT[k][:, j * P:(j + 1) * P], xh[:, j, k * P:(k + 1) * P],
                                                      ident[:])
                        ins.then_inc(tr_done.sem, 1)
                    t.wait_ge(tr_out.sem, tr_out.at(c, KD))
                    for k in range(KF):
                        if k < 2:
                            t.wait_ge(sh_done.sem, sh_done.at(c, KS))
                        else:
                            t.wait_ge(f1_out.sem, f1_out.at(c, k - 1))
                        for kk in range(KD):
                            ins = mm(pF[k % 2][:], wf1[:, kk, k * P:(k + 1) * P], xhT[:, kk, :],
                                     start=(kk == 0), stop=(kk == KD - 1))
                        ins.then_inc(f1_done.sem, 1)
                    t.wait_ge(f1_out.sem, f1_out.at(c, KF))
                    for q in range(2):
                        t.wait_ge(out_done.sem, out_done.at(c, q + 1, back=1))
                        for j in range(2):
                            dst, col = pR[q][:, j * D:(j + 1) * D], (2 * q + j) * P
                            for k in range(KF):
                                mm(dst, ff[:, k, col:col + P], wf2[:, k, :], start=(k == 0), stop=False)
                            for k in range(KS):
                                ins = mm(dst, sh[:, k, col:col + P], ws2[:, k, :], start=False, stop=(k == KS - 1))
                        ins.then_inc(r_done.sem, 1)


SCRATCH = {
    "xn": (T, D), "xnT": (NCH, P, KD, CH), "xhT": (NCH, P, KD, CH), "sz": (NCH, G, P, CH), "xc": (NCH, G, P, CH),
    "bc": (NCH, 2 * NS, CH), "dt": (NCH, G, P, CH), "dtx": (NCH, G, P, CH),
    "slot_x": (NSLOT, D), "slot_y": (NSLOT, D), "y": (NCH, G, P, CH),
}
DEBUG = False


def build(nc, d):
    for name, shape in SCRATCH.items():
        d[name] = nc.dram_tensor(f"{name}_dram", shape, F32, kind="ExternalOutput" if DEBUG else "Internal").ap()
    d["moe_b"] = nc.dram_tensor("moe_b_dram", (E, 3, 2 * F + D), BF16, kind="Internal").ap()
    with ExitStack() as ctx:
        def sb(name, shape, dt=F32):
            return ctx.enter_context(nc.sbuf_tensor(name, shape, dt))

        wts = sb("wts", [P, TOPK, NT])
        slotf = sb("slotf", [P, TOPK, NT])
        block_e = sb("block_e", [1, NBLK], I32)
        idx_all = sb("idx_all", [P, NCH, TOPK, TPC], U32)
        scores = ExitStack()
        logits = scores.enter_context(nc.sbuf_tensor("logits", [P, NT, EP], F32, side="right"))
        with ExitStack() as experts:
            w1 = experts.enter_context(nc.sbuf_tensor("w1", [P, E * KD, 2 * F], F32))
            w2 = experts.enter_context(nc.sbuf_tensor("w2", [P, E * KD, D], F32))
            with ExitStack() as head:
                consts = [(head.enter_context(nc.sbuf_tensor(f"hw_{name}", shape, F32)), name) for name, shape in (
                    ("in_proj_w", [P, KD, 2 * DI]), ("x_proj_w", [P, G, XP]), ("dt_proj_w", [RK, DI]),
                    ("conv_w", [P, G, CONV]), ("inner_bias", [P, 2, G]), ("tri", [P, P]), ("ones", [P, P]),
                    ("rev", [P, NT, EP]), ("geglu_mult", [P, E * KD]))]
                with ExitStack() as inner:
                    gate_phase(nc, inner, d, logits, consts)
                with ExitStack() as inner:
                    head_phase(nc, inner, d, [t for t, _ in consts], logits, wts, block_e, slotf, idx_all, w1, w2)
            scores.close()
            with ExitStack() as inner:
                scan_phase(nc, inner, d, block_e, w1, w2)
        with ExitStack() as inner:
            tail_phase(nc, inner, d, wts, idx_all)


def arrange(inputs):
    a = {k: np.asarray(v) for k, v in inputs.items()}
    m, f = (lambda n: a["L0_attn_" + n]), (lambda n: a["L0_ffn_" + n])
    rows = lambda w: w.reshape(-1, P, w.shape[-1]).transpose(1, 0, 2)
    cols = lambda v: v.reshape(-1, P).T
    out = {
        "x": m("x").reshape(T, D),
        "in_proj_w": rows(m("in_proj_w")), "x_proj_w": rows(m("x_proj_w")), "dt_proj_w": m("dt_proj_w"),
        "gate_w": rows(f("gate_w").T), "conv_w": m("conv_w").reshape(G, P, CONV).transpose(1, 0, 2),
        "ln1": np.stack([cols(m("ln1_g")), cols(m("ln1_b"))], 1),
        "inner_bias": np.stack([cols(m("conv_b")), cols(m("dt_proj_b"))], 1),
        "ident": np.eye(P, dtype=np.float32),
        "tri": np.triu(np.ones((P, P), np.float32), 1), "ones": np.ones((P, P), np.float32),
        "rev": np.broadcast_to(np.float32(EP) - np.arange(EP, dtype=np.float32), (P, NT, EP)),
        "blk": np.broadcast_to(np.arange(NBLK, dtype=np.float32)[:, None], (1, NBLK, EP)),
        "sel": np.kron(np.eye(BPI, dtype=np.float32), np.ones((3, P), np.float32)),
        "fc1_w": f("fc1_w").reshape(E, 2 * F, KD, P).transpose(3, 0, 2, 1).reshape(P, E * KD, 2 * F),
        "fc2_w": f("fc2_w").reshape(E, D, F // P, P).transpose(3, 0, 2, 1).reshape(P, E * KD, D),
        "fc1_b": f("fc1_b"), "fc2_b": f("fc2_b"),
        "geglu_mult": f("geglu_mult").reshape(E * KD, P).T,
        "out_proj_w": rows(m("out_proj_w")), "ffn_w1": rows(m("ffn_w1")), "ffn_w2": rows(m("ffn_w2")),
        "s_fc1_w": rows(f("s_fc1_w").T), "s_fc2_w": rows(f("s_fc2_w").T), "s_mult": cols(f("s_geglu_mult")),
        "ffn_b1": cols(m("ffn_b1")), "s_fc1_b": cols(f("s_fc1_b")),
        "ffn_b2": m("ffn_b2").reshape(1, D), "s_fc2_b": f("s_fc2_b").reshape(1, D),
        "ln2": np.stack([cols(m("ln2_g")), cols(m("ln2_b"))], 1),
        "A_log": m("A_log").reshape(G, P, NS).transpose(1, 0, 2), "D": cols(m("D")),
    }
    return {k: np.ascontiguousarray(v) for k, v in out.items()}


def kernel(**inputs):
    import concourse.bacc as bacc
    from concourse.bass_utils import run_bass_kernel_spmd

    nc = bacc.Bacc("TRN2", target_bir_lowering=False, num_devices=1)
    arrays = arrange(inputs)
    d = {n: nc.dram_tensor(n + "_in", a.shape, mybir.dt.from_np(a.dtype), kind="ExternalInput").ap()
         for n, a in arrays.items()}
    d["out"] = nc.dram_tensor("out", (T, D), F32, kind="ExternalOutput").ap()
    build(nc, d)
    r = run_bass_kernel_spmd(nc, [{n + "_in": a for n, a in arrays.items()}], core_ids=[0])
    return r.results[0]["out"].reshape(B, L, D)
```

```python
from contextlib import ExitStack

import numpy as np

import concourse.bass as bass
from concourse import mybir

F32 = mybir.dt.float32
BF16 = mybir.dt.bfloat16
I32 = mybir.dt.int32
U32 = mybir.dt.uint32
ALU = mybir.AluOpType
ACT = mybir.ActivationFunctionType
AX = mybir.AxisListType

P = 128
B, L, D = 2, 2048, 256
T = B * L
CH = 512
NCH = T // CH
CPB = L // CH
TPC = CH // P
NT = T // P
KD = D // P
DI = 512
G = DI // P
NS = 16
RK = 16
XP = RK + 2 * NS
CONV = 4
DF = 1024
KF = DF // P
E, TOPK = 15, 3
EP = 16
F = 256
FS = 512
KS = FS // P
BPI = 4
NBLK = -(-((T * TOPK + E * (P - 1)) // P) // BPI) * BPI
NSLOT = NBLK * P
MOE_CHUNKS = -(-NBLK // (BPI * G))
EPS = 1e-5


class Count:

    def __init__(self, sem, per, start=2):
        self.sem, self.per, self.start = sem, per, start

    def at(self, c, k, back=0):
        return c * self.per + ((self.start - back) * self.per + k)


class Phase:

    def __init__(self, nc, ctx, tag):
        self.nc, self.ctx, self.tag, self.counts = nc, ctx, tag, []

    def sb(self, name, shape, dt=F32):
        return self.ctx.enter_context(self.nc.sbuf_tensor(f"{self.tag}_{name}", shape, dt))

    def bank(self, name):
        return self.ctx.enter_context(self.nc.psum_tensor(f"{self.tag}_{name}", [P, 512], F32))

    def sem(self, name):
        return self.ctx.enter_context(self.nc.semaphore(f"{self.tag}_{name}"))

    def count(self, name, per, start=2):
        c = Count(self.sem(name), per, start)
        self.counts.append(c)
        return c

    def credit(self, sp):
        for c in self.counts:
            if c.start:
                sp.sem_inc(c.sem, c.start * c.per)


def norm_steps(nc, v, dve, c, n, src, dst, stats, mv, sd, rs, fence, sd_ready, half, done):
    def settle():
        v.wait_ge(dve.sem, dve.at(c, n[0]))

    for t in range(TPC):
        n[0] += 1
        nc.vector.bn_stats(stats[:, t, :], src[:, t, :]).then_inc(dve.sem, 1)
    settle()
    nc.vector.tensor_copy(fence[:, 0:1], fence[:, 1:2])
    for t in range(TPC):
        n[0] += 1
        nc.vector.bn_aggr(mv[:, t, :], stats[:, t, :]).then_inc(dve.sem, 1)
    v.wait_ge(sd_ready.sem, sd_ready.at(c, half + 1))
    n[0] += 1
    nc.vector.reciprocal(rs[:], sd[:]).then_inc(dve.sem, 1)
    settle()
    for t in range(TPC):
        nc.vector.tensor_scalar(dst[:, t, :], src[:, t, :], mv[:, t, 0:1], rs[:, t:t + 1],
                                ALU.subtract, ALU.mult).then_inc(done.sem, 1)


NORM = 2 * TPC + 1


def gate_phase(nc, ctx, d, logits, consts):
    ph = Phase(nc, ctx, "gt")
    sb, bank, sem, count = ph.sb, ph.bank, ph.sem, ph.count
    wgate = sb("wgate", [P, KD, E])
    ident = sb("ident", [P, P])
    ln1 = sb("ln1", [P, 2, KD])
    zeros = sb("zeros", [P, 4 * D])
    eps = sb("eps", [P, 1])
    fence = sb("fence", [P, 2])
    bf = sb("bf", [E, 2 * F + D])
    bparts = [sb(f"b{n}", [E, 2 * F + D], BF16) for n in range(3)]
    x = [sb(f"x{p}", [P, TPC, D]) for p in range(2)]
    xn = [sb(f"xn{p}", [P, TPC, D]) for p in range(2)]
    xh = [sb(f"xh{p}", [P, TPC, D]) for p in range(2)]
    stats = sb("stats", [P, TPC, 6])
    mv = sb("mv", [P, TPC, 2])
    sd = sb("sd", [P, TPC])
    rs = sb("rs", [P, TPC])
    xnT = [sb(f"xnT{p}", [P, KD, CH]) for p in range(2)]
    xhT = [sb(f"xhT{p}", [P, KD, CH]) for p in range(2)]
    ws1 = sb("ws1", [P, KD, 2 * FS])
    ws2 = sb("ws2", [P, KS, D])
    mult = sb("mult", [P, KS])
    bs1 = sb("bs1", [P, 2 * KS])
    gate = sb("gate", [P, 2, CH])
    sh = sb("sh", [P, KS, CH])
    ys = sb("ys", [P, TPC, D])

    pN = [bank(f"pN{k}") for k in range(KD)]
    pH = [bank(f"pH{k}") for k in range(KD)]
    pL = bank("pL")
    pF = [bank(f"pF{n}") for n in range(2)]
    pR = [bank("pR"), pL]

    w_in, c_in, const_set, slots_zeroed = sem("w_in"), sem("c_in"), sem("const_set"), sem("slots_zeroed")
    s_in = sem("s_in")
    b_in, split, b_out, rounds = sem("b_in"), sem("split"), sem("b_out"), sem("rounds")
    x_in = [count(f"x_in{p}", 16) for p in range(2)]
    dve = count("dve", 2 * NORM)
    sd_ready = count("sd_ready", 2)
    xn_done, xh_done = count("xn_done", TPC), count("xh_done", TPC)
    n_done, n_out = count("n_done", KD), count("n_out", KD)
    h_done, h_out = count("h_done", KD), count("h_out", KD)
    lg_done, lg_out = count("lg_done", 1), count("lg_out", 1)
    scaled = sem("scaled")
    s1_done, s1_out = count("s1_done", 2 * KS), count("s1_out", KS)
    sh_done, r_done, r_out, ys_st = count("sh_done", KS), count("r_done", 2), count("r_out", 2), count("ys_st", 16)
    st = {n: [count(f"st_{n}{p}", 16) for p in range(2)] for n in ("xn", "xnT", "xhT")}
    ZEROED = NSLOT // (4 * P)
    assert ZEROED % 4 == 0

    with nc.Block() as block:
        @block.sync
        def _(sp):
            ph.credit(sp)
    with nc.Block() as block:
        @block.sync
        def _(sp):
            halves = lambda name: d[name].rearrange("(i q t p) w -> i q p t w", q=2, t=TPC, p=P)
            turned = lambda name: d[name].rearrange("(i q) p k t -> i q p k t", q=2)
            slots = d["slot_x"].rearrange("(n p a) w -> n p (a w)", p=P, a=4)

            def load_x(i, p):
                sp.dma_start(x[p][:], halves("x")[i, p]).then_inc(x_in[p].sem, 16)

            load_x(0, 0)
            for dst, name in ((wgate, "gate_w"), (ident, "ident"), (ln1, "ln1")):
                sp.dma_start(dst[:], d[name]).then_inc(w_in, 16)
            load_x(0, 1)
            sp.dma_start(bf[:, 0:2 * F], d["fc1_b"]).then_inc(b_in, 16)
            sp.dma_start(bf[:, 2 * F:], d["fc2_b"]).then_inc(b_in, 16)
            for dst, name in ((ws1, "s_fc1_w"), (ws2, "s_fc2_w"), (mult, "s_mult"), (bs1, "s_fc1_b")):
                sp.dma_start(dst[:], d[name]).then_inc(s_in, 16)
            for dst, name in consts:
                sp.dma_start(dst[:], d[name]).then_inc(c_in, 16)
            sp.wait_ge(const_set, 2)

            def rows_out(i, p, load=True):
                c = 2 * i + p
                sp.wait_ge(xn_done.sem, xn_done.at(c, TPC))
                sp.sem_inc(rounds, 1)
                sp.dma_start(halves("xn")[i, p], xn[p][:]).then_inc(st["xn"][p].sem, 16)
                if load:
                    load_x(i + 1, p)

            def pair(i, to_last=False, last=False):
                for p in range(2):
                    c = 2 * i + p
                    if not (last and p):
                        rows_out(i + p, 1 - p, load=not last and not (to_last and p))
                    sp.wait_ge(n_out.sem, n_out.at(c, KD))
                    sp.sem_inc(rounds, 1)
                    sp.dma_start(turned("xnT")[i, p], xnT[p][:]).then_inc(st["xnT"][p].sem, 16)
                    sp.wait_ge(h_out.sem, h_out.at(c, KD))
                    sp.sem_inc(rounds, 1)
                    sp.dma_start(turned("xhT")[i, p], xhT[p][:]).then_inc(st["xhT"][p].sem, 16)
                    sp.wait_ge(r_out.sem, r_out.at(c, 2))
                    sp.sem_inc(rounds, 1)
                    sp.dma_start(halves("ys")[i, p], ys[:]).then_inc(ys_st.sem, 16)
                for n in range(ZEROED // 4):
                    sp.dma_start(slots[i * (ZEROED // 4) + n], zeros[:]).then_inc(slots_zeroed, 16)

            rows_out(0, 0)
            with sp.Fori(0, NCH // 2 - 2) as i:
                pair(i)
            pair(NCH // 2 - 2, to_last=True)
            pair(NCH // 2 - 1, last=True)
            sp.wait_ge(ys_st.sem, ys_st.at(NCH, 0))
            sp.wait_ge(split, 5)
            for n in range(3):
                sp.dma_start(d["moe_b"][:, n, :], bparts[n][:]).then_inc(b_out, 16)
            sp.wait_ge(b_out, 48)
            for s in st["xn"] + st["xnT"] + st["xhT"]:
                sp.wait_ge(s.sem, s.at(NCH // 2, 0))
            sp.wait_ge(slots_zeroed, 16 * ZEROED)
            sp.wait_ge(c_in, 16 * len(consts))

        @block.gpsimd
        def _(pool):
            nc.gpsimd.memset(zeros[:], 0.0).then_inc(const_set, 1)
            nc.gpsimd.memset(eps[:], EPS).then_inc(const_set, 1)
            pool.wait_ge(b_in, 32)
            for n in range(3):
                nc.gpsimd.tensor_copy(bparts[n][:], bf[:]).then_inc(split, 1)
                if n < 2:
                    pool.wait_ge(split, 2 * n + 1)
                    nc.gpsimd.tensor_tensor(bf[:], bf[:], bparts[n][:], ALU.subtract).then_inc(split, 1)
                    pool.wait_ge(split, 2 * n + 2)

        @block.vector
        def _(v):
            nc.vector.memset(fence[:], 0.0)
            nc.vector.memset(logits[:], -1e30)

            def take_logits(c):
                v.wait_ge(lg_done.sem, lg_done.at(c, 1))
                nc.vector.tensor_scalar(logits[:, bass.ds(c * TPC, TPC), 0:E],
                                        pL[:, 0:TPC * E].rearrange("p (t e) -> p t e", e=E), 1.0, None,
                                        ALU.mult).then_inc(lg_out.sem, 1)

            def norms(i, p):
                c = 2 * i + p
                n = [0]
                ln = (stats, mv, sd, rs, fence, sd_ready)
                v.wait_ge(x_in[p].sem, x_in[p].at(i, 16))
                v.wait_ge(xh_done.sem, xh_done.at(c, 0))
                v.wait_ge(st["xn"][p].sem, st["xn"][p].at(i, 16, back=1))
                v.wait_ge(n_done.sem, n_done.at(c, KD, back=2))
                norm_steps(nc, v, dve, c, n, x[p], xn[p], *ln, 0, xn_done)
                v.wait_ge(xn_done.sem, xn_done.at(c, TPC))
                v.wait_ge(h_done.sem, h_done.at(c, KD, back=2))
                norm_steps(nc, v, dve, c, n, xn[p], xh[p], *ln, 1, xh_done)
                assert n[0] == dve.per

            def pair(i, last=False):
                for p in range(2):
                    c = 2 * i + p
                    if not (last and p):
                        norms(i + p, 1 - p)
                    take_logits(c)
                    v.wait_ge(r_done.sem, r_done.at(c, 2, back=1))
                    for k in range(KS):
                        v.wait_ge(s1_out.sem, s1_out.at(c, k + 1))
                        v.wait_ge(s1_done.sem, s1_done.at(c, 2 * k + 2))
                        nc.vector.scalar_tensor_tensor(sh[:, k, :], pF[1][:], bs1[:, k:k + 1], gate[:, k % 2, :],
                                                       ALU.add, ALU.mult).then_inc(sh_done.sem, 1)

            norms(0, 0)
            v.wait_ge(s_in, 16 * 4)
            nc.vector.tensor_tensor(ws2[:], ws2[:], mult[:].rearrange("p (k o) -> p k o", o=1)
                                    .to_broadcast([P, KS, D]), ALU.mult).then_inc(scaled, 1)
            with v.Fori(0, NCH // 2 - 1) as i:
                pair(i)
            pair(NCH // 2 - 1, last=True)

        @block.scalar
        def _(a):
            a.wait_ge(const_set, 2)
            a.wait_ge(w_in, 16 * 3)
            act = nc.scalar.activation

            def root(c, half):
                a.wait_ge(dve.sem, dve.at(c, half * NORM + 2 * TPC))
                act(sd[:], mv[:, :, 1], ACT.Sqrt, bias=eps[:, 0:1]).then_inc(sd_ready.sem, 1)

            def pair(i, last=False):
                for p in range(2):
                    c = 2 * i + p
                    a.wait_ge(st["xnT"][p].sem, st["xnT"][p].at(i, 16, back=1))
                    a.wait_ge(s1_done.sem, s1_done.at(c, 0, back=1))
                    for k in range(KD):
                        a.wait_ge(n_done.sem, n_done.at(c, k + 1))
                        act(xnT[p][:, k, :], pN[k][:], ACT.Copy).then_inc(n_out.sem, 1)
                    a.wait_ge(st["xhT"][p].sem, st["xhT"][p].at(i, 16, back=1))
                    for k in range(KD):
                        a.wait_ge(h_done.sem, h_done.at(c, k + 1))
                        act(xhT[p][:, k, :], pH[k][:], ACT.Identity, bias=ln1[:, 1, k:k + 1],
                            scale=ln1[:, 0, k:k + 1]).then_inc(h_out.sem, 1)
                    for k in range(KS):
                        a.wait_ge(sh_done.sem, sh_done.at(c, k - 1))
                        a.wait_ge(s1_done.sem, s1_done.at(c, 2 * k + 1))
                        act(gate[:, k % 2, :], pF[0][:], ACT.Gelu, bias=bs1[:, KS + k:KS + k + 1])\
                            .then_inc(s1_out.sem, 1)
                    if not last:
                        root(c + 2, 0)
                        root(c + 2, 1)
                    a.wait_ge(ys_st.sem, ys_st.at(c, 16, back=1))
                    for q in range(2):
                        a.wait_ge(r_done.sem, r_done.at(c, q + 1))
                        act(ys[:, 2 * q:2 * q + 2, :], pR[q][:].rearrange("p (t w) -> p t w", t=2), ACT.Copy)\
                            .then_inc(r_out.sem, 1)

            a.wait_ge(s_in, 16 * 4)
            for c in range(2):
                root(c, 0)
                root(c, 1)
            with a.Fori(0, NCH // 2 - 1) as i:
                pair(i)
            pair(NCH // 2 - 1, last=True)

        @block.tensor
        def _(t):
            t.wait_ge(w_in, 16 * 3)
            t.wait_ge(s_in, 16 * 4)
            t.wait_ge(scaled, 1)
            with t.Fori(0, NCH // 2) as i:
                for p in range(2):
                    c = 2 * i + p
                    for src, ready, banks, done, out in ((xn[p], xn_done, pN, n_done, n_out),
                                                         (xh[p], xh_done, pH, h_done, h_out)):
                        if src is xh[p]:
                            t.wait_ge(n_out.sem, n_out.at(c, KD))
                            t.wait_ge(lg_out.sem, lg_out.at(c, 1, back=1))
                            t.wait_ge(r_out.sem, r_out.at(c, 0))
                            for j in range(TPC):
                                for k in range(KD):
                                    ins = nc.tensor.matmul(pL[:, j * E:(j + 1) * E], xnT[p][:, k, j * P:(j + 1) * P],
                                                           wgate[:, k, :], start=(k == 0), stop=(k == KD - 1))
                            ins.then_inc(lg_done.sem, 1)
                        t.wait_ge(ready.sem, ready.at(c, TPC))
                        for k in range(KD):
                            t.wait_ge(out.sem, out.at(c, k + 1, back=1))
                            for j in range(TPC):
                                ins = nc.tensor.transpose(banks[k][:, j * P:(j + 1) * P],
                                                          src[:, j, k * P:(k + 1) * P], ident[:])
                            ins.then_inc(done.sem, 1)
                    for k in range(KS):
                        for n, col in ((0, FS + k * P), (1, k * P)):
                            if n:
                                t.wait_ge(sh_done.sem, sh_done.at(c, k))
                            else:
                                t.wait_ge(s1_out.sem, s1_out.at(c, k))
                            for kk in range(KD):
                                ins = nc.tensor.matmul(pF[n][:], ws1[:, kk, col:col + P], xnT[p][:, kk, :],
                                                       start=(kk == 0), stop=(kk == KD - 1))
                            ins.then_inc(s1_done.sem, 1)
                    t.wait_ge(sh_done.sem, sh_done.at(c, KS))
                    t.wait_ge(lg_out.sem, lg_out.at(c, 1))
                    for q in range(2):
                        t.wait_ge(r_out.sem, r_out.at(c, q - 1))
                        for j in range(2):
                            dst, col = pR[q][:, j * D:(j + 1) * D], (2 * q + j) * P
                            for k in range(KS):
                                ins = nc.tensor.matmul(dst, sh[:, k, col:col + P], ws2[:, k, :],
                                                       start=(k == 0), stop=(k == KS - 1))
                        ins.then_inc(r_done.sem, 1)


def head_phase(nc, ctx, d, hw, logits, wts, block_e, slotf, idx_all, w1, w2):
    ph = Phase(nc, ctx, "hd")
    sb, bank, sem, count = ph.sb, ph.bank, ph.sem, ph.count
    win, wxp, wdt, convw, bias, tri, ones, rev, mult = hw

    xhT = [sb(f"xhT{p}", [P, KD, CH]) for p in range(2)]
    xi = sb("xi", [P, G, CONV - 1 + CH])
    cv = sb("cv", [P, G, CH])
    xc = [sb(f"xc{p}", [P, G, CH]) for p in range(2)]
    sz = sb("sz", [P, G, CH])
    xd = sb("xd", [XP, CH])
    u = sb("u", [P, G, CH])
    rel = sb("rel", [P, G, CH])
    dt = sb("dt", [P, G, CH])
    dtx = sb("dtx", [P, G, CH])
    keep = sb("keep", [P, NCH])

    assert NT * EP == CH and TOPK < G and NBLK * EP <= G * CH
    sc, work, mask, tot, cum = (w.rearrange("p (t e) -> p t e", e=EP) for w in (
        rel[:, 0, :], u[:, TOPK, :], rel[:, 1, :], rel[:, 2, :], rel[:, 3, :]))
    tot, cum = (w.rearrange("p t e -> p (t e)").rearrange("p (e t) -> p e t", t=NT) for w in (tot, cum))
    one = [u[:, k, :].rearrange("p (t e) -> p t e", e=EP) for k in range(TOPK)]
    blk, le = (w[0:1].rearrange("p g t -> p (g t)")[:, 0:NBLK * EP].rearrange("p (n e) -> p n e", e=EP)
               for w in (dt, dtx))
    m = sb("m", [P, TOPK, NT])
    red = sb("red", [P, NT])
    pick = sb("pick", [P, NT])
    pos = sc
    before = sb("before", [P, EP])
    cnt = sb("cnt", [P, EP])
    cnt_i = sb("cnt_i", [P, EP], I32)
    nb = sb("nb", [P, EP])
    nb_cum = sb("nb_cum", [P, EP])
    onesr = mask
    be = sb("be", [1, NBLK])
    xs = [sb(f"xs{p}", [P, TPC, D]) for p in range(2)]
    idx = [sb(f"idx{p}", [P, TOPK * TPC], U32) for p in range(2)]

    pXI, pZ, pD = ([bank(f"{name}{k}") for k in range(2)] for name in ("pXI", "pZ", "pD"))
    pX, pR = bank("pX"), bank("pR")
    pS = pD[1]

    h_in = [count(f"h_in{p}", 16) for p in range(2)]
    w1_in, w2_in, blk_in, rounds = sem("w1_in"), sem("w2_in"), sem("blk_in"), sem("rounds")
    cstep, sstep = count("cstep", G * (CONV - 1)), count("sstep", 3)
    xi_done, xi_out = count("xi_done", G), count("xi_out", G)
    z_done, z_out = count("z_done", G), count("z_out", G)
    conv_done, carried, xc_done = count("conv_done", G), count("carried", G), count("xc_done", G)
    xp_done, xp_out = count("xp_done", 1), count("xp_out", 1)
    dtp_done, abs_done, rel_done = count("dtp_done", G), count("abs_done", G), count("rel_done", G)
    u_done, lnw_done, dt_done, dtx_done = (count(n, 1) for n in ("u_done", "lnw_done", "dt_done", "dtx_done"))
    min_done = count("min_done", 1)
    st = {n: count(f"st_{n}", 16) for n in ("sz", "xc", "bc", "dt", "dtx")}

    route, exp_done, pe_done, idx_made, scaled = (sem(n) for n in ("route", "exp_done", "pe_done", "idx_made", "scaled"))
    xs_in = [count(f"xs_in{p}", 16, start=0) for p in range(2)]
    idx_set = count("idx_set", 1)
    sent = [[count(f"sent{p}{j}", 16, start=0) for j in range(TOPK * TPC)] for p in range(2)]
    SHIFTED, MASKED = 2, 27

    def steps(eng, step, finish):
        step(0, first=True)
        with eng.Fori(0, NCH // 2 - 1) as i:
            for s in (1, 2):
                step(2 * i + s, p=s % 2)
        step(NCH - 1, p=1, last=True)
        finish(NCH - 1, 1)

    with nc.Block() as block:
        @block.sync
        def _(sp):
            ph.credit(sp)
    with nc.Block() as block:
        @block.sync
        def _(sp):
            def load_h(c, p):
                sp.dma_start(xhT[p][:], d["xhT"][c]).then_inc(h_in[p].sem, 16)

            def store(name, c, src, done, k):
                sp.wait_ge(done.sem, done.at(c, k))
                sp.sem_inc(rounds, 1)
                dst = d[name][c] if name == "bc" else d[name][c].rearrange("g p t -> p g t")
                sp.dma_start(dst, src).then_inc(st[name].sem, 16)

            def rest(c):
                store("dt", c, dt[:], dt_done, 1)
                store("dtx", c, dtx[:], dtx_done, 1)

            def step(s, p=0, first=False, last=False, load=True):
                if load:
                    sp.wait_ge(z_done.sem, z_done.at(s, G))
                    sp.sem_inc(rounds, 1)
                    load_h(s + 2, p)
                if not first:
                    store("bc", s - 1, xd[RK:, :], xp_out, 1)
                store("xc", s, xc[p][:], xc_done, G)
                if not last:
                    store("sz", s + 1, sz[:], z_out, G)
                if not first:
                    rest(s - 1)

            load_h(0, 0)
            sp.dma_start(blk, d["blk"]).then_inc(blk_in, 16)
            load_h(1, 1)
            sp.dma_start(w2[:], d["fc2_w"]).then_inc(w2_in, 16)
            store("sz", 0, sz[:], z_out, G)
            pieces = NCH - 3
            rows = E * KD // pieces

            def load_w1(n):
                sp.dma_start(w1[:, bass.ds(n * rows, rows), :], d["fc1_w"][:, bass.ds(n * rows, rows), :])\
                    .then_inc(w1_in, 16)

            assert rows * pieces == E * KD
            step(0, first=True)
            with sp.Fori(0, NCH // 2 - 2) as i:
                for s in (1, 2):
                    step(2 * i + s, p=s % 2)
                    load_w1(2 * i + (s - 1))
            step(NCH - 3, p=1)
            load_w1(pieces - 1)
            step(NCH - 2, p=0, load=False)
            step(NCH - 1, p=1, load=False, last=True)
            store("bc", NCH - 1, xd[RK:, :], xp_out, 1)
            rest(NCH - 1)
            for s in st.values():
                sp.wait_ge(s.sem, s.at(NCH, 0))
            sp.wait_ge(w1_in, 16 * pieces)

        @block.vector
        def _(v):
            vec = nc.vector
            chain = [0]

            def link(ins):
                chain[0] += 1
                ins.then_inc(route, 1)
                v.wait_ge(route, chain[0])

            def over_e(ap):
                return ap.rearrange("p (t o) -> p t o", o=1).to_broadcast([P, NT, EP])

            vec.memset(keep[:], 1.0)
            link(vec.tensor_reduce(red[:], logits[:], AX.X, ALU.max))
            link(vec.tensor_tensor(work, logits[:], over_e(red[:]), ALU.subtract))
            assert chain[0] == SHIFTED
            v.wait_ge(exp_done, 1)
            link(vec.memset(sc[:, :, E:EP], 0.0))
            link(vec.tensor_reduce(red[:], sc, AX.X, ALU.add))
            link(vec.reciprocal(pick[:], red[:]))
            link(vec.tensor_tensor(sc, sc, over_e(pick[:]), ALU.mult))
            link(vec.memset(sc[:, :, E:EP], -1.0))
            for k in range(TOPK):
                link(vec.tensor_reduce(m[:, k, :], sc, AX.X, ALU.max))
                link(vec.tensor_tensor(work, sc, over_e(m[:, k, :]), ALU.is_equal))
                link(vec.tensor_tensor(work, work, rev[:], ALU.mult))
                link(vec.tensor_reduce(pick[:], work, AX.X, ALU.max))
                link(vec.tensor_tensor(one[k], rev[:], over_e(pick[:]), ALU.is_equal))
                link(vec.scalar_tensor_tensor(sc, one[k], -4.0, sc, ALU.mult, ALU.add))
            link(vec.tensor_tensor(mask, one[0], one[1], ALU.add))
            link(vec.tensor_tensor(mask, mask, one[2], ALU.add))
            assert chain[0] == MASKED, chain[0]
            link(vec.tensor_tensor(red[:], m[:, 0, :], m[:, 1, :], ALU.add))
            link(vec.tensor_tensor(red[:], red[:], m[:, 2, :], ALU.add))
            link(vec.tensor_scalar(red[:], red[:], 1e-20, None, ALU.add))
            link(vec.reciprocal(pick[:], red[:]))
            for k in range(TOPK):
                link(vec.tensor_tensor(wts[:, k, :], m[:, k, :], pick[:], ALU.mult))
            v.wait_ge(pe_done, 2)
            link(vec.memset(onesr, 1.0))
            flat = onesr.rearrange("p t e -> p (t e)")
            link(vec.tensor_copy(tot, pS[:].rearrange("p (t e) -> p e t", e=EP)))
            link(vec.tensor_tensor_scan(cum.rearrange("p e t -> p (e t)"), flat,
                                        tot.rearrange("p e t -> p (e t)"), 0.0, ALU.mult, ALU.add))
            link(vec.memset(before[:, 0:1], 0.0))
            link(vec.tensor_copy(before[:, 1:EP], cum[:, 0:EP - 1, NT - 1]))
            link(vec.tensor_tensor(cnt[:], cum[:, :, NT - 1], before[:], ALU.subtract))
            link(vec.tensor_scalar(cnt[:], cnt[:], float(P - 1), None, ALU.add))
            link(vec.tensor_copy(cnt_i[:], cnt[:]))
            link(vec.tensor_scalar(cnt_i[:], cnt_i[:], 7, None, ALU.logical_shift_right))
            link(vec.tensor_copy(nb[:], cnt_i[:]))
            link(vec.tensor_tensor_scan(nb_cum[:], flat[:, 0:EP], nb[:], 0.0, ALU.mult, ALU.add))
            link(vec.tensor_tensor(nb[:], nb_cum[:], nb[:], ALU.subtract))
            link(vec.scalar_tensor_tensor(before[:], nb[:], float(P), before[:], ALU.mult, ALU.subtract))
            link(vec.tensor_tensor(cum, cum, tot, ALU.subtract))
            link(vec.tensor_tensor(cum, cum, before[:].rearrange("p (e o) -> p e o", o=1)
                                   .to_broadcast([P, EP, NT]), ALU.add))
            link(vec.tensor_tensor(pos, pR[:].rearrange("p (t e) -> p t e", e=EP),
                                   cum.rearrange("p e t -> p t e"), ALU.add))
            for k in range(TOPK):
                link(vec.tensor_tensor(work, pos, one[k], ALU.mult))
                link(vec.tensor_reduce(slotf[:, k, :], work, AX.X, ALU.add))
            vec.tensor_copy(idx_all[:], slotf[:].rearrange("p k (c t) -> p c k t", t=TPC)).then_inc(idx_made, 1)
            v.wait_ge(blk_in, 16)
            link(vec.tensor_tensor(le, nb_cum[0:1, :].rearrange("p (o e) -> p o e", o=1)
                                   .to_broadcast([1, NBLK, EP]), blk, ALU.is_le))
            link(vec.tensor_reduce(be[:], le[:, :, 0:E], AX.X, ALU.add))
            link(vec.tensor_scalar(be[:], be[:], float(E - 1), None, ALU.min))
            link(vec.memset(keep[:, CPB - 1:CPB], 0.0))
            vec.tensor_copy(block_e[:], be[:])
            for g in range(G):
                vec.memset(xi[:, g, 0:CONV - 1], 0.0)

            def conv(s):
                n = 0
                for k in reversed(range(CONV)):
                    for g in range(G):
                        if k == CONV - 1:
                            v.wait_ge(xi_out.sem, xi_out.at(s, g + 1))
                            v.wait_ge(xc_done.sem, xc_done.at(s, g + 1, back=1))
                            vec.tensor_scalar(cv[:, g, :], xi[:, g, k:k + CH], convw[:, g, k:k + 1],
                                              None, ALU.mult).then_inc(cstep.sem, 1)
                            n += 1
                            continue
                        if g == 0:
                            v.wait_ge(cstep.sem, cstep.at(s, n))
                        ins = vec.scalar_tensor_tensor(cv[:, g, :], xi[:, g, k:k + CH], convw[:, g, k:k + 1],
                                                       cv[:, g, :], ALU.mult, ALU.add)
                        if k:
                            ins.then_inc(cstep.sem, 1)
                            n += 1
                        else:
                            ins.then_inc(conv_done.sem, 1)
                for g in range(G):
                    v.wait_ge(conv_done.sem, conv_done.at(s, g + 1))
                    vec.tensor_scalar(xi[:, g, 0:CONV - 1], xi[:, g, CH:], keep[:, bass.ds(s, 1)], None, ALU.mult)\
                        .then_inc(carried.sem, 1)

            def softplus(c, p):
                v.wait_ge(st["dt"].sem, st["dt"].at(c, 16, back=1))
                v.wait_ge(u_done.sem, u_done.at(c, 1))
                v.wait_ge(dtx_done.sem, dtx_done.at(c, 0))
                vec.tensor_scalar(dt[:], u[:], 1.0, -1.0, ALU.add, ALU.add).then_inc(sstep.sem, 1)
                v.wait_ge(sstep.sem, sstep.at(c, 1))
                vec.tensor_tensor(dt[:], u[:], dt[:], ALU.subtract).then_inc(sstep.sem, 1)
                v.wait_ge(sstep.sem, sstep.at(c, 2))
                v.wait_ge(lnw_done.sem, lnw_done.at(c, 1))
                vec.tensor_tensor(dt[:], dt[:], dtx[:], ALU.add).then_inc(sstep.sem, 1)
                v.wait_ge(sstep.sem, sstep.at(c, 3))
                vec.tensor_tensor(dt[:], dt[:], u[:], ALU.min).then_inc(min_done.sem, 1)
                v.wait_ge(min_done.sem, min_done.at(c, 1))
                vec.tensor_tensor(dt[:], dt[:], rel[:], ALU.add).then_inc(dt_done.sem, 1)
                v.wait_ge(dt_done.sem, dt_done.at(c, 1))
                vec.tensor_tensor(dtx[:], dt[:], xc[p][:], ALU.mult).then_inc(dtx_done.sem, 1)

            def step(s, p=0, first=False, last=False):
                conv(s)
                if not first:
                    softplus(s - 1, 1 - p)

            steps(v, step, softplus)

        @block.scalar
        def _(a):
            act = nc.scalar.activation
            a.wait_ge(route, SHIFTED)
            act(sc, work, ACT.Exp).then_inc(exp_done, 1)

            def project_in(c, groups=range(G)):
                a.wait_ge(st["sz"].sem, st["sz"].at(c, 16, back=1))
                for g in groups:
                    a.wait_ge(carried.sem, carried.at(c, g + 1, back=1))
                    a.wait_ge(xi_done.sem, xi_done.at(c, g + 1))
                    act(xi[:, g, CONV - 1:], pXI[g % 2][:], ACT.Copy).then_inc(xi_out.sem, 1)
                    a.wait_ge(z_done.sem, z_done.at(c, g + 1))
                    act(sz[:, g, :], pZ[g % 2][:], ACT.Silu).then_inc(z_out.sem, 1)

            def small(c):
                a.wait_ge(st["bc"].sem, st["bc"].at(c, 16, back=1))
                a.wait_ge(dtp_done.sem, dtp_done.at(c, G, back=1))
                a.wait_ge(xp_done.sem, xp_done.at(c, 1))
                act(xd[:], pX[0:XP, :], ACT.Copy).then_inc(xp_out.sem, 1)

            def finish(c, p):
                a.wait_ge(dt_done.sem, dt_done.at(c, 1, back=1))
                for g in range(G):
                    a.wait_ge(dtp_done.sem, dtp_done.at(c, g + 1))
                    act(u[:, g, :], pD[g % 2][:], ACT.Abs, bias=bias[:, 1, g:g + 1]).then_inc(abs_done.sem, 1)
                    act(rel[:, g, :], pD[g % 2][:], ACT.Relu, bias=bias[:, 1, g:g + 1]).then_inc(rel_done.sem, 1)
                a.wait_ge(abs_done.sem, abs_done.at(c, G))
                act(u[:], u[:], ACT.Exp, scale=-1.0).then_inc(u_done.sem, 1)
                a.wait_ge(u_done.sem, u_done.at(c, 1))
                a.wait_ge(st["dtx"].sem, st["dtx"].at(c, 16, back=1))
                act(dtx[:], u[:], ACT.Ln, bias=1.0).then_inc(lnw_done.sem, 1)

            def step(s, p=0, first=False, last=False):
                if not first:
                    finish(s - 1, 1 - p)
                a.wait_ge(st["xc"].sem, st["xc"].at(s, 16, back=2))
                a.wait_ge(dtx_done.sem, dtx_done.at(s, 1, back=2))
                for g in range(G):
                    a.wait_ge(conv_done.sem, conv_done.at(s, g + 1))
                    act(xc[p][:, g, :], cv[:, g, :], ACT.Silu, bias=bias[:, 0, g:g + 1]).then_inc(xc_done.sem, 1)
                if not last:
                    project_in(s + 1, range(G // 2))
                small(s)
                if not last:
                    project_in(s + 1, range(G // 2, G))

            project_in(0)
            steps(a, step, finish)

        @block.tensor
        def _(t):
            mm = nc.tensor.matmul

            def project_in(c, p, i, groups=range(G)):
                t.wait_ge(h_in[p].sem, h_in[p].at(i, 16))
                for g in groups:
                    for col, dst, ready, out in ((g * P, pXI, xi_done, xi_out), (DI + g * P, pZ, z_done, z_out)):
                        t.wait_ge(out.sem, out.at(c, g - 1))
                        for k in range(KD):
                            ins = mm(dst[g % 2][:], win[:, k, col:col + P], xhT[p][:, k, :],
                                     start=(k == 0), stop=(k == KD - 1))
                        ins.then_inc(ready.sem, 1)

            def x_proj(c, p):
                t.wait_ge(xp_out.sem, xp_out.at(c, 1, back=1))
                for g in range(G):
                    t.wait_ge(xc_done.sem, xc_done.at(c, g + 1))
                    ins = mm(pX[0:XP, :], wxp[:, g, :], xc[p][:, g, :], start=(g == 0), stop=(g == G - 1))
                ins.then_inc(xp_done.sem, 1)

            def dt_proj(c):
                t.wait_ge(xp_out.sem, xp_out.at(c, 1))
                for g in range(G):
                    t.wait_ge(rel_done.sem, rel_done.at(c, g - 1))
                    mm(pD[g % 2][:], wdt[:, g * P:(g + 1) * P], xd[0:RK, :], start=True, stop=True)\
                        .then_inc(dtp_done.sem, 1)

            project_in(0, 0, 0)
            t.wait_ge(route, MASKED)
            for dst, lhs in ((pR, tri), (pS, ones)):
                mm(dst[:], lhs[:], mask.rearrange("p t e -> p (t e)"), start=True, stop=True).then_inc(pe_done, 1)

            def step(s, p, i):
                project_in(s + 1, 1 - p, i, range(G // 2))
                x_proj(s, p)
                project_in(s + 1, 1 - p, i, range(G // 2, G))
                dt_proj(s)

            step(0, 0, 0)
            with t.Fori(0, NCH // 2 - 1) as i:
                for s in (1, 2):
                    step(2 * i + s, s % 2, i + 1)
            x_proj(NCH - 1, 1)
            dt_proj(NCH - 1)

        @block.gpsimd
        def _(pool):
            xn_tiles = d["xn"].rearrange("(i q t p) w -> i q p t w", q=2, t=TPC, p=P)

            def load_rows(i, p):
                pool.dma_start(xs[p][:], xn_tiles[i, p]).then_inc(xs_in[p].sem, 16)

            def pair(i, first=False, last=False):
                for p in range(2):
                    c = 2 * i + p
                    if not (first and p == 0):
                        for j in range(TOPK * TPC):
                            pool.wait_ge(sent[1 - p][j].sem, sent[1 - p][j].at(i, 16 * p))
                        pool.sem_inc(rounds, 1)
                    if not (last and p == 1):
                        load_rows(i + p, 1 - p)
                    nc.gpsimd.tensor_copy(idx[p][:], idx_all[:].rearrange("p c k t -> p (c k t)")[
                        :, bass.ds(c * (TOPK * TPC), TOPK * TPC)]).then_inc(idx_set.sem, 1)
                    pool.wait_ge(xs_in[p].sem, xs_in[p].at(i, 16))
                    pool.wait_ge(idx_set.sem, idx_set.at(c, 1))
                    pool.sem_inc(rounds, 1)
                    for j in range(TOPK * TPC):
                        pool.indirect_dma_start(
                            d["slot_x"], bass.IndirectOffsetOnAxis(idx[p][:, j:j + 1], 0), xs[p][:, j % TPC, :], None,
                        ).then_inc(sent[p][j].sem, 16)

            load_rows(0, 0)
            pool.wait_ge(w2_in, 16)
            nc.gpsimd.tensor_tensor(w2[:], w2[:], mult[:].rearrange("p (n o) -> p n o", o=1)
                                    .to_broadcast([P, E * KD, D]), ALU.mult).then_inc(scaled, 1)
            pool.wait_ge(scaled, 1)
            pool.wait_ge(idx_made, 1)
            pair(0, first=True)
            with pool.Fori(1, NCH // 2 - 1) as i:
                pair(i)
            pair(NCH // 2 - 1, last=True)
            for j in range(TOPK * TPC):
                pool.wait_ge(sent[1][j].sem, sent[1][j].at(NCH // 2, 0))


def scan_phase(nc, ctx, d, block_e, w1, w2):
    ph = Phase(nc, ctx, "sc")
    NP = NS // 2
    NH = 3
    hb = lambda g, k: h[(g * NP + k) % NH]
    turns = [(j % NH) for j in range(G * NP)]
    since = lambda g, k: next(n for n in range(1, 2 * NH) if turns[(g * NP + k - n) % (G * NP)] == turns[g * NP + k])
    sb, bank, sem, count = ph.sb, ph.bank, ph.sem, ph.count
    ident = sb("ident", [P, P])
    A = sb("A", [P, G, NS])
    Dw = sb("Dw", [P, G])
    state = sb("state", [P, G, NS])
    sel = sb("sel", [3 * BPI, BPI, P], BF16)
    bc = sb("bc", [P, NS // 2, 2, 2, CH])
    dt = [sb(f"dt{p}", [P, CH]) for p in range(2)]
    dtx = [sb(f"dtx{p}", [P, CH]) for p in range(2)]
    xc = sb("xc", [P, CH])
    sz = sb("sz", [P, CH])
    dbx = [sb(f"dbx{p}", [P, 2, CH]) for p in range(2)]
    h = [sb(f"h{p}", [P, 2, CH]) for p in range(NH)]
    yo = sb("yo", [P, CH])
    sel_f = yo[0:3 * BPI, 0:BPI * P]
    xg = sb("xg", [P, BPI, D])
    bb1 = sb("bb1", [3 * BPI, 2 * F], BF16)
    bb2 = sb("bb2", [3 * BPI, D], BF16)
    xT = sb("xT", [P, 2, KD, P])
    hid = sb("hid", [P, BPI, 2 * F])

    pA = [bank(f"pA{n}") for n in range(4)]
    pY, pT = bank("pY"), bank("pT")
    pH = [bank(f"pH{q}") for q in range(2)]

    w_in, const_set, reset, rounds = sem("w_in"), sem("const_set"), sem("reset"), sem("rounds")
    in_ld = [count(f"in_ld{p}", 32 * G // 2) for p in range(2)]
    gate_ld = count("gate_ld", 32 * G)
    bc_ld = [count(f"bc_ld{k}", 32) for k in range(NS // 2)]
    xg_ld = count("xg_ld", 16 * G)
    bb1_ld, bb2_ld = (count(n, 16 * BPI * G) for n in ("bb1_ld", "bb2_ld"))
    exp_done, scan_done = count("exp_done", G * NS), count("scan_done", G * NS)
    dbx_done, prod_done, sum_done = (count(n, G * NS // 2) for n in ("dbx_done", "prod_done", "sum_done"))
    saved = count("saved", G * NS // 2)
    skip_done, y_done = count("skip_done", G), count("y_done", G)
    y_st = count("y_st", 16 * G)
    tr_done, tr_out = count("tr_done", 4 * G), count("tr_out", 4 * G)
    f1_done, f1_out = count("f1_done", BPI * G), count("f1_out", BPI * G)
    gelu_done, act_done = count("gelu_done", G), count("act_done", G)
    f2_done, f2_out = count("f2_done", 2 * G), count("f2_out", 2 * G)
    ye_st = [count(f"ye_st{q}", 16 * G) for q in range(2)]

    def chunks(eng, body, between=None):
        body(0, True, first=True)
        with eng.Fori(1, CPB) as c:
            body(c, True)
        if between:
            between()
        with eng.Fori(CPB, MOE_CHUNKS) as c:
            body(c, True)
        for c in range(MOE_CHUNKS, NCH):
            body(c, False)

    with nc.Block() as block:
        @block.sync
        def _(sp):
            ph.credit(sp)

    with nc.Block() as block:
        @block.sync
        def _(sp):
            for dst, name in ((A[:], "A_log"), (ident[:], "ident"), (Dw[:], "D"), (sel_f, "sel")):
                sp.dma_start(dst, d[name]).then_inc(w_in, 16)

            def load_inputs(c, g):
                for dst, name in ((dt, "dt"), (dtx, "dtx")):
                    sp.dma_start(dst[g % 2][:], d[name][c, g]).then_inc(in_ld[g % 2].sem, 16)

            def load_bc(c, k):
                sp.wait_ge(prod_done.sem, prod_done.at(c, k + 1 - NP))
                sp.sem_inc(rounds, 1)
                for n in range(2):
                    row = n * NS + 2 * k
                    src = d["bc"][c, row:row + 2, :].rearrange("(o n) t -> o (n t)", o=1)
                    sp.dma_start(bc[:, k, n].rearrange("p n t -> p (n t)"), src.to_broadcast([P, 2 * CH]))\
                        .then_inc(bc_ld[k].sem, 16)

            def load_blocks(c, g):
                p = g % 2
                sp.wait_ge(tr_done.sem, tr_done.at(c, 4 * g - 2))
                sp.sem_inc(rounds, 1)
                sp.dma_start(xg[:], d["slot_x"].rearrange("(c g b p) w -> c g p b w", g=G, b=BPI, p=P)[c, g])\
                    .then_inc(xg_ld.sem, 16)

            def load_biases(c, g, dst, part, ld):
                for b in range(BPI):
                    e = sp.value_load(block_e[0:1, bass.ds(c * (G * BPI) + (g * BPI + b), 1)], min_val=0, max_val=E - 1)
                    sp.dma_start(dst[3 * b:3 * b + 3, :], d["moe_b"][bass.ds(e, 1)].rearrange("o k n -> (o k) n")[:, part])\
                        .then_inc(ld.sem, 16)

            def load_biases1(c, g):
                sp.wait_ge(f1_done.sem, f1_done.at(c, BPI * g))
                sp.sem_inc(rounds, 1)
                load_biases(c, g, bb1, slice(0, 2 * F), bb1_ld)

            def load_biases2(c, g):
                sp.wait_ge(f2_done.sem, f2_done.at(c, 2 * g))
                sp.sem_inc(rounds, 1)
                load_biases(c, g, bb2, slice(2 * F, 2 * F + D), bb2_ld)

            def store_blocks(c, g, q):
                sp.wait_ge(f2_out.sem, f2_out.at(c, 2 * g + q + 1))
                sp.sem_inc(rounds, 1)
                dst = d["slot_y"].rearrange("(c g q b p) w -> c g q p b w", g=G, q=2, b=2, p=P)
                sp.dma_start(dst[c, g, q], hid[:, 2 * q:2 * q + 2, F:]).then_inc(ye_st[q].sem, 16)

            def chunk(c, moe, moe_next, first=False, last=False):
                for g in range(G):
                    sp.wait_ge(y_done.sem, y_done.at(c, g))
                    sp.sem_inc(rounds, 1)
                    if g:
                        sp.dma_start(d["y"][c, g - 1], yo[:]).then_inc(y_st.sem, 16)
                    elif not first:
                        sp.dma_start(d["y"][c - 1, G - 1], yo[:]).then_inc(y_st.sem, 16)
                    for dst, name in ((xc, "xc"), (sz, "sz")):
                        sp.dma_start(dst[:], d[name][c, g]).then_inc(gate_ld.sem, 16)
                    if g < G - 1:
                        load_inputs(c, g + 1)
                        if moe:
                            load_blocks(c, g + 1)
                            load_biases1(c, g + 1)
                            store_blocks(c, g, 0)
                            load_biases2(c, g + 1)
                            store_blocks(c, g, 1)
                        continue
                    if not last:
                        load_inputs(c + 1, 0)
                        load_bc(c + 1, 0)
                        load_bc(c + 1, 1)
                        if moe_next:
                            load_blocks(c + 1, 0)
                        for k in range(2, NP - 2):
                            load_bc(c + 1, k)
                        if moe_next:
                            load_biases1(c + 1, 0)
                    if moe:
                        store_blocks(c, g, 0)
                    if not last:
                        for k in range(NP - 2, NP):
                            load_bc(c + 1, k)
                        if moe_next:
                            load_biases2(c + 1, 0)
                    if moe:
                        store_blocks(c, g, 1)

            load_inputs(0, 0)
            load_bc(0, 0)
            load_blocks(0, 0)
            load_biases1(0, 0)
            for k in range(1, NP):
                load_bc(0, k)
            load_biases2(0, 0)
            chunk(0, True, True, first=True)
            with sp.Fori(1, MOE_CHUNKS - 1) as c:
                chunk(c, True, True)
            chunk(MOE_CHUNKS - 1, True, False, last=MOE_CHUNKS == NCH)
            for c in range(MOE_CHUNKS, NCH):
                chunk(c, False, False, last=c == NCH - 1)
            sp.wait_ge(y_done.sem, y_done.at(NCH, 0))
            sp.dma_start(d["y"][NCH - 1, G - 1], yo[:]).then_inc(y_st.sem, 16)
            sp.wait_ge(y_st.sem, y_st.at(NCH, 0))
            for s in ye_st:
                sp.wait_ge(s.sem, s.at(MOE_CHUNKS, 0))

        @block.gpsimd
        def _(pool):
            def output(c, g):
                pool.wait_ge(skip_done.sem, skip_done.at(c, g + 1))
                nc.gpsimd.tensor_tensor(yo[:], yo[:], sz[:], ALU.mult).then_inc(y_done.sem, 1)

            def chunk(c, moe, first=False):
                for g in range(G):
                    p = g % 2
                    pool.wait_ge(in_ld[p].sem, in_ld[p].at(c, 32 * (g // 2 + 1)))
                    for k in range(NP):
                        if k == 3 and not (first and g == 0):
                            output(c, g - 1)
                        if moe and k == NP - 1:
                            pool.wait_ge(gelu_done.sem, gelu_done.at(c, g + 1))
                            nc.gpsimd.tensor_tensor(hid[:, :, 0:F], hid[:, :, 0:F], hid[:, :, F:], ALU.mult)\
                                .then_inc(act_done.sem, 1)
                        pool.wait_ge(bc_ld[k].sem, bc_ld[k].at(c, 32))
                        pool.wait_ge(scan_done.sem, scan_done.at(c, NS * g + 2 * k - 2))
                        nc.gpsimd.tensor_tensor(dbx[k % 2][:], dtx[p][:].rearrange("p (o t) -> p o t", o=1)
                                                .to_broadcast([P, 2, CH]), bc[:, k, 0], ALU.mult)\
                            .then_inc(dbx_done.sem, 1)
            chunks(pool, chunk)
            output(NCH - 1, G - 1)

        @block.scalar
        def _(a):
            act = nc.scalar.activation
            a.wait_ge(w_in, 64)
            act(A[:], A[:], ACT.Exp).then_inc(w_in, 1)
            a.wait_ge(w_in, 64 + 2)

            def chunk(c, moe, first=False):
                for g in range(G):
                    p = g % 2

                    def decays(k):
                        for n in (2 * k, 2 * k + 1):
                            a.wait_ge(scan_done.sem, scan_done.at(c, NS * g + n - 3))
                            act(pA[n % 4][:], dt[p][:], ACT.Exp, scale=A[:, g, n:n + 1]).then_inc(exp_done.sem, 1)

                    def save(k):
                        a.wait_ge(scan_done.sem, scan_done.at(c, NS * g + 2 * k + 2))
                        act(state[:, g, 2 * k:2 * k + 2], hb(g, k)[:, :, CH - 1], ACT.Copy).then_inc(saved.sem, 1)

                    def transposed(n, group=g):
                        if n in (0, 3):
                            a.wait_ge(f2_done.sem, f2_done.at(c, 2 * group + (1 if n else 0)))
                        else:
                            a.wait_ge(f1_done.sem, f1_done.at(c, BPI * group + 2 * n))
                        a.wait_ge(tr_done.sem, tr_done.at(c, 4 * group + n + 1))
                        act(xT[:].rearrange("p b k t -> p (b k t)"), pT[:], ACT.Copy).then_inc(tr_out.sem, 1)

                    def out(q, group):
                        a.wait_ge(f2_done.sem, f2_done.at(c, 2 * group + q + 1))
                        act(hid[:, 2 * q:2 * q + 2, F:], pH[q][:].rearrange("p (b w) -> p b w", b=2), ACT.Copy)\
                            .then_inc(f2_out.sem, 1)

                    a.wait_ge(in_ld[p].sem, in_ld[p].at(c, 32 * (g // 2 + 1)))
                    def gelu():
                        a.wait_ge(f1_out.sem, f1_out.at(c, BPI * (g + 1)))
                        act(hid[:, :, F:], hid[:, :, F:], ACT.Gelu).then_inc(gelu_done.sem, 1)

                    decays(0)
                    if not (first and g == 0):
                        h_last = hb((g - 1) % G, NP - 1)
                        a.wait_ge(scan_done.sem, scan_done.at(c, NS * g))
                        act(state[:, (g - 1) % G, NS - 2:NS], h_last[:, :, CH - 1], ACT.Copy).then_inc(saved.sem, 1)
                        before = moe or g == 0
                        if before:
                            out(0, g - 1)
                            transposed(3, g - 1)
                    else:
                        before = False
                    for k in range(1, NP):
                        decays(k)
                        save(k - 1)
                        if k == 1 and before:
                            out(1, g - 1)
                        if moe:
                            if k == 1:
                                transposed(0)
                            elif k == 4:
                                transposed(1)
                            elif k == NP - 2:
                                gelu()
                            elif k == NP - 1:
                                transposed(2)
            chunks(a, chunk)
            a.wait_ge(scan_done.sem, scan_done.at(NCH, 0))
            act(state[:, G - 1, NS - 2:NS], hb(G - 1, NP - 1)[:, :, CH - 1], ACT.Copy).then_inc(saved.sem, 1)

        @block.vector
        def _(v):
            vec = nc.vector
            vec.memset(state[:], 0.0).then_inc(const_set, 1)
            v.wait_ge(w_in, 64)
            vec.tensor_copy(sel[:].rearrange("k b p -> k (b p)"), sel_f).then_inc(const_set, 1)
            v.wait_ge(w_in, 64 + 1)
            vec.tensor_scalar(A[:], A[:], -1.0, None, ALU.mult).then_inc(w_in, 1)
            v.wait_ge(const_set, 2)

            def chunk(c, moe, first=False):
                for g in range(G):
                    p = g % 2

                    def scans(k):
                        v.wait_ge(sum_done.sem, sum_done.at(c, NP * g + k + 1 - since(g, k)))
                        v.wait_ge(dbx_done.sem, dbx_done.at(c, NP * g + k + 1))
                        for j in range(2):
                            n = 2 * k + j
                            v.wait_ge(exp_done.sem, exp_done.at(c, NS * g + n + 1))
                            vec.tensor_tensor_scan(hb(g, k)[:, j, :], pA[n % 4][:], dbx[k % 2][:, j, :],
                                                   state[:, g, n:n + 1], ALU.mult, ALU.add).then_inc(scan_done.sem, 1)

                    def hidden(b):
                        v.wait_ge(tr_done.sem, tr_done.at(c, 4 * g))
                        v.wait_ge(ye_st[b // 2].sem, ye_st[b // 2].at(c, 16 * g))
                        v.wait_ge(f1_done.sem, f1_done.at(c, BPI * g + b + 1))
                        vec.tensor_copy(hid[:, b, :], pH[b % 2][:]).then_inc(f1_out.sem, 1)

                    for k in range(NP):
                        scans(k)
                        if moe and 2 <= k < 2 + BPI:
                            hidden(k - 2)
                        if k == 1 and not (first and g == 0):
                            output(c, g - 1)
                        if k:
                            products(c, g, k - 1)
                        elif not (first and g == 0):
                            products(c if g else c - 1, (g - 1) % G, NP - 1)

            def products(c, g, k):
                v.wait_ge(saved.sem, saved.at(c, NP * g + k + 1))
                v.wait_ge(bc_ld[k].sem, bc_ld[k].at(c, 32))
                vec.tensor_tensor(hb(g, k)[:], hb(g, k)[:], bc[:, k, 1], ALU.mult).then_inc(prod_done.sem, 1)

            def output(c, g):
                v.wait_ge(sum_done.sem, sum_done.at(c, NP * (g + 1)))
                v.wait_ge(gate_ld.sem, gate_ld.at(c, 32 * (g + 1)))
                v.wait_ge(y_st.sem, y_st.at(c, 16 * g))
                vec.scalar_tensor_tensor(yo[:], xc[:], Dw[:, g % G:g % G + 1], pY[:], ALU.mult, ALU.add)\
                    .then_inc(skip_done.sem, 1)

            def new_sequence():
                v.wait_ge(saved.sem, saved.at(CPB, 0))
                vec.memset(state[:], 0.0).then_inc(reset, 1)
                v.wait_ge(reset, 1)

            chunks(v, chunk, between=new_sequence)
            products(NCH - 1, G - 1, NP - 1)
            output(NCH - 1, G - 1)

        @block.tensor
        def _(t):
            mm = nc.tensor.matmul
            t.wait_ge(w_in, 64)
            t.wait_ge(const_set, 2)

            def chunk(c, moe, first=False):
                for g in range(G):
                    p = g % 2

                    def sums(k):
                        if k == 0:
                            t.wait_ge(skip_done.sem, skip_done.at(c, g))
                        t.wait_ge(prod_done.sem, prod_done.at(c, NP * g + k + 1))
                        for j in range(2):
                            ins = mm(pY[:], ident[:], hb(g, k)[:, j, :], start=(k + j == 0),
                                     stop=(2 * k + j == NS - 1))
                        ins.then_inc(sum_done.sem, 1)

                    def turn(n):
                        t.wait_ge(tr_out.sem, tr_out.at(c, 4 * g + n))
                        if n == 0:
                            t.wait_ge(xg_ld.sem, xg_ld.at(c, 16 * (g + 1)))
                        if n == 2:
                            t.wait_ge(act_done.sem, act_done.at(c, g + 1))
                        src = xg if n < 2 else hid
                        for b in range(2):
                            for k in range(KD):
                                at = (KD * b + k) * P
                                ins = nc.tensor.transpose(pT[:, at:at + P],
                                                          src[:, 2 * (n % 2) + b, k * P:(k + 1) * P], ident[:])
                        ins.then_inc(tr_done.sem, 1)

                    def first(b):
                        if b % 2 == 0:
                            t.wait_ge(tr_out.sem, tr_out.at(c, 4 * g + b // 2 + 1))
                        if b < 2:
                            t.wait_ge(f2_out.sem, f2_out.at(c, 2 * g - 1 + b))
                        else:
                            t.wait_ge(f1_out.sem, f1_out.at(c, BPI * g + b - 1))
                        for k in range(KD):
                            mm(pH[b % 2][:], xT[:, b % 2, k, :], w1[:, bass.ds(e[b] * KD + k, 1), :]
                               .rearrange("p o n -> p (o n)"), start=(k == 0), stop=False)
                        if b == 0:
                            t.wait_ge(bb1_ld.sem, bb1_ld.at(c, 16 * BPI * (g + 1)))
                        mm(pH[b % 2][:], sel[:, b, :], bb1[:], start=False, stop=True)\
                            .then_inc(f1_done.sem, 1)

                    def second(q):
                        t.wait_ge(tr_out.sem, tr_out.at(c, 4 * g + 2 + q + 1))
                        t.wait_ge(f1_out.sem, f1_out.at(c, BPI * g + 3 + q))
                        for j in range(2):
                            dst = pH[q][:, j * D:(j + 1) * D]
                            for k in range(KD):
                                mm(dst, xT[:, j, k, :], w2[:, bass.ds(e[2 * q + j] * KD + k, 1), :]
                                   .rearrange("p o n -> p (o n)"), start=(k == 0), stop=False)
                            if q + j == 0:
                                t.wait_ge(bb2_ld.sem, bb2_ld.at(c, 16 * BPI * (g + 1)))
                            ins = mm(dst, sel[:, 2 * q + j, :], bb2[:], start=False, stop=True)
                        ins.then_inc(f2_done.sem, 1)

                    if not moe:
                        for k in range(NP):
                            sums(k)
                        continue
                    turn(0)
                    e = [t.value_load(block_e[0:1, bass.ds(c * (G * BPI) + (g * BPI + b), 1)], min_val=0,
                                      max_val=E - 1) for b in range(BPI)]
                    first(0)
                    sums(0)
                    first(1)
                    turn(1)
                    sums(1)
                    first(2)
                    sums(2)
                    first(3)
                    sums(3)
                    sums(4)
                    sums(5)
                    turn(2)
                    second(0)
                    turn(3)
                    sums(6)
                    second(1)
                    sums(7)
            chunks(t, chunk)

def tail_phase(nc, ctx, d, wts, idx_all):
    ph = Phase(nc, ctx, "tl")
    sb, bank, sem, count = ph.sb, ph.bank, ph.sem, ph.count
    wo = sb("wo", [P, G, D])
    wf1 = sb("wf1", [P, KD, DF])
    wf2 = sb("wf2", [P, KF, D])
    ident = sb("ident", [P, P])
    bf1 = sb("bf1", [P, KF])
    ln2 = sb("ln2", [P, 2, KD])
    brow = [sb(f"brow{n}", [P, D]) for n in range(2)]
    eps = sb("eps", [P, 1])
    fence = sb("fence", [P, 2])

    y = [sb(f"y{p}", [P, G, CH]) for p in range(2)]
    xn = [sb(f"xn{p}", [P, TPC, D]) for p in range(2)]
    ys = [sb(f"ys{p}", [P, TPC, D]) for p in range(2)]
    x = [sb(f"x{p}", [P, TPC, D]) for p in range(2)]
    idx = [sb(f"idx{p}", [P, TOPK * TPC], U32) for p in range(2)]
    rows = [sb(f"rows{p}", [P, TOPK, TPC, D]) for p in range(2)]
    x1 = [sb(f"res{p}", [P, TPC, D]) for p in range(2)]
    xh = sb("xh", [P, TPC, D])
    xhT = sb("xhT", [P, KD, CH])
    stats = sb("stats", [P, TPC, 6])
    mv = sb("mv", [P, TPC, 2])
    sd = sb("sd", [P, TPC])
    rs = sb("rs", [P, TPC])
    ff = sb("ff", [P, KF, CH])
    acc = sb("acc", [P, TPC, D])
    out = [sb(f"out{p}", [P, TPC, D]) for p in range(2)]

    pO = [bank(f"pO{q}") for q in range(2)]
    pT = [bank(f"pT{k}") for k in range(KD)]
    pF = [bank(f"pF{n}") for n in range(2)]
    pR = [bank(f"pR{q}") for q in range(2)]

    w_in, wo_in, rounds = sem("w_in"), sem("wo_in"), sem("rounds")
    ld, more = ([count(f"{name}{p}", 32, start=0) for p in range(2)] for name in ("ld", "more"))
    got = [count(f"got{p}", 16 * TOPK * TPC, start=0) for p in range(2)]
    idx_set = count("idx_set", 1)
    o_done, x1_done = count("o_done", 2), count("x1_done", 2)
    dve = count("dve", NORM)
    sd_ready, xh_done = count("sd_ready", 1), count("xh_done", TPC)
    tr_done, tr_out = count("tr_done", KD), count("tr_out", KD)
    f1_done, f1_out = count("f1_done", KF), count("f1_out", KF)
    r_done = count("r_done", 2)
    acc_step = count("acc_step", 3 + TOPK)
    out_done = count("out_done", 2)
    out_st = [count(f"out_st{p}", 16) for p in range(2)]
    pair = lambda ap, q: ap[:, 2 * q:2 * q + 2, :]

    names = (("ident", ident), ("ln2", ln2), ("ffn_b1", bf1), ("ffn_w1", wf1), ("ffn_w2", wf2))
    NW = 16 * (len(names) + 2)
    with nc.Block() as block:
        @block.sync
        def _(sp):
            ph.credit(sp)

        @block.vector
        def _(v):
            nc.vector.memset(fence[:], 0.0)
            nc.vector.memset(eps[:], EPS)

    tiles = lambda name: d[name].rearrange("(i q t p) w -> i q p t w", q=2, t=TPC, p=P)
    with nc.Block() as block:
        @block.sync
        def _(sp):
            sp.dma_start(wo[:], d["out_proj_w"]).then_inc(wo_in, 16)
            for n, name in enumerate(("ffn_b2", "s_fc2_b")):
                sp.dma_start(brow[n][:], d[name].to_broadcast([P, D])).then_inc(w_in, 16)
            for name, dst in names:
                sp.dma_start(dst[:], d[name]).then_inc(w_in, 16)
            with sp.Fori(0, NCH // 2) as i:
                for p in range(2):
                    sp.wait_ge(out_done.sem, out_done.at(2 * i + p, 2))
                    sp.dma_start(tiles("out")[i, p], out[p][:]).then_inc(out_st[p].sem, 16)
            for p in range(2):
                sp.wait_ge(out_st[p].sem, out_st[p].at(NCH // 2, 0))

        @block.gpsimd
        def _(pool):
            with pool.Fori(0, NCH // 2) as i:
                for p in range(2):
                    c = 2 * i + p
                    pool.wait_ge(x1_done.sem, x1_done.at(c, 2, back=2))
                    pool.sem_inc(rounds, 1)
                    for dst, src in ((y, d["y"].rearrange("(i q) g p t -> i q p g t", q=2)[i, p]),
                                     (xn, tiles("xn")[i, p])):
                        pool.dma_start(dst[p][:], src).then_inc(ld[p].sem, 16)
                    pool.wait_ge(acc_step.sem, acc_step.at(c, 3 + TOPK, back=2))
                    pool.sem_inc(rounds, 1)
                    for dst, src in ((ys, tiles("ys")[i, p]), (x, tiles("x")[i, p])):
                        pool.dma_start(dst[p][:], src).then_inc(more[p].sem, 16)
                    nc.gpsimd.tensor_copy(idx[p][:], idx_all[:].rearrange("p c k t -> p (c k t)")[
                        :, bass.ds(c * (TOPK * TPC), TOPK * TPC)]).then_inc(idx_set.sem, 1)
                    pool.wait_ge(idx_set.sem, idx_set.at(c, 1))
                    pool.sem_inc(rounds, 1)
                    for k in range(TOPK):
                        for j in range(TPC):
                            n = k * TPC + j
                            pool.indirect_dma_start(rows[p][:, k, j, :], None, d["slot_y"],
                                                    bass.IndirectOffsetOnAxis(idx[p][:, n:n + 1], 0))\
                                .then_inc(got[p].sem, 16)

        @block.vector
        def _(v):
            vec = nc.vector

            def residual(i, p):
                c = 2 * i + p
                n = [0]
                v.wait_ge(ld[p].sem, ld[p].at(i, 32))
                for q in range(2):
                    v.wait_ge(o_done.sem, o_done.at(c, q + 1))
                    vec.tensor_tensor(pair(x1[p], q), pair(xn[p], q), pO[q][:].rearrange("p (t w) -> p t w", t=2),
                                      ALU.add).then_inc(x1_done.sem, 1)
                v.wait_ge(x1_done.sem, x1_done.at(c, 2))
                v.wait_ge(tr_done.sem, tr_done.at(c, KD, back=1))
                norm_steps(nc, v, dve, c, n, x1[p], xh, stats, mv, sd, rs, fence, sd_ready, 0, xh_done)
                assert n[0] == NORM

            def total(i, p):
                c = 2 * i + p
                v.wait_ge(more[p].sem, more[p].at(i, 32))
                v.wait_ge(out_done.sem, out_done.at(c, 0))
                terms = [x[p][:], ys[p][:], brow[0][:].rearrange("p (o w) -> p o w", o=1).to_broadcast([P, TPC, D])]
                for n, term in enumerate(terms):
                    vec.tensor_tensor(acc[:], acc[:] if n else x1[p][:], term, ALU.add).then_inc(acc_step.sem, 1)
                    v.wait_ge(acc_step.sem, acc_step.at(c, n + 1))
                v.wait_ge(got[p].sem, got[p].at(i, got[p].per))
                for k in range(TOPK):
                    for j in range(TPC):
                        ins = vec.scalar_tensor_tensor(acc[:, j, :], rows[p][:, k, j, :],
                                                       wts[:, k, bass.ds(c * TPC + j, 1)], acc[:, j, :],
                                                       ALU.mult, ALU.add)
                    ins.then_inc(acc_step.sem, 1)
                    v.wait_ge(acc_step.sem, acc_step.at(c, k + 4))
                v.wait_ge(out_st[p].sem, out_st[p].at(i, 16, back=1))
                for q in range(2):
                    v.wait_ge(r_done.sem, r_done.at(c, q + 1))
                    vec.tensor_tensor(pair(out[p], q), pair(acc, q), pR[q][:].rearrange("p (t w) -> p t w", t=2),
                                      ALU.add).then_inc(out_done.sem, 1)

            def two(i, last=False):
                for p in range(2):
                    if not (last and p):
                        residual(i + p, 1 - p)
                    total(i, p)

            residual(0, 0)
            v.wait_ge(w_in, NW)
            vec.tensor_tensor(brow[0][:], brow[0][:], brow[1][:], ALU.add).then_inc(w_in, 1)
            v.wait_ge(w_in, NW + 1)
            with v.Fori(0, NCH // 2 - 1) as i:
                two(i)
            two(NCH // 2 - 1, last=True)

        @block.scalar
        def _(a):
            act = nc.scalar.activation

            def root(c):
                a.wait_ge(dve.sem, dve.at(c, 2 * TPC))
                act(sd[:], mv[:, :, 1], ACT.Sqrt, bias=eps[:, 0:1]).then_inc(sd_ready.sem, 1)

            def chunk(c, last=False):
                a.wait_ge(f1_done.sem, f1_done.at(c, KF, back=1))
                for k in range(KD):
                    a.wait_ge(tr_done.sem, tr_done.at(c, k + 1))
                    act(xhT[:, k, :], pT[k][:], ACT.Identity, bias=ln2[:, 1, k:k + 1],
                        scale=ln2[:, 0, k:k + 1]).then_inc(tr_out.sem, 1)
                a.wait_ge(r_done.sem, r_done.at(c, 2, back=1))
                for k in range(KF):
                    if k == 2 and not last:
                        root(c + 1)
                    a.wait_ge(f1_done.sem, f1_done.at(c, k + 1))
                    act(ff[:, k, :], pF[k % 2][:], ACT.Gelu_apprx_tanh, bias=bf1[:, k:k + 1]).then_inc(f1_out.sem, 1)

            root(0)
            a.wait_ge(w_in, NW)
            with a.Fori(0, NCH - 1) as c:
                chunk(c)
            chunk(NCH - 1, last=True)

        @block.tensor
        def _(t):
            mm = nc.tensor.matmul

            def out_proj(i, p):
                c = 2 * i + p
                t.wait_ge(ld[p].sem, ld[p].at(i, 32))
                for q in range(2):
                    t.wait_ge(x1_done.sem, x1_done.at(c, q + 1, back=1))
                    for j in range(2):
                        for g in range(G):
                            ins = mm(pO[q][:, j * D:(j + 1) * D], y[p][:, g, (2 * q + j) * P:(2 * q + j + 1) * P],
                                     wo[:, g, :], start=(g == 0), stop=(g == G - 1))
                    ins.then_inc(o_done.sem, 1)

            def chunk(i, p, last=False):
                c = 2 * i + p
                t.wait_ge(xh_done.sem, xh_done.at(c, TPC))
                for k in range(KD):
                    t.wait_ge(tr_out.sem, tr_out.at(c, k + 1, back=1))
                    for j in range(TPC):
                        ins = nc.tensor.transpose(pT[k][:, j * P:(j + 1) * P], xh[:, j, k * P:(k + 1) * P],
                                                  ident[:])
                    ins.then_inc(tr_done.sem, 1)
                if not last:
                    out_proj(i + p, 1 - p)
                t.wait_ge(tr_out.sem, tr_out.at(c, KD))
                for k in range(KF):
                    t.wait_ge(f1_out.sem, f1_out.at(c, k - 1))
                    for kk in range(KD):
                        ins = mm(pF[k % 2][:], wf1[:, kk, k * P:(k + 1) * P], xhT[:, kk, :],
                                 start=(kk == 0), stop=(kk == KD - 1))
                    ins.then_inc(f1_done.sem, 1)
                t.wait_ge(f1_out.sem, f1_out.at(c, KF))
                for q in range(2):
                    t.wait_ge(out_done.sem, out_done.at(c, q + 1, back=1))
                    for j in range(2):
                        dst, col = pR[q][:, j * D:(j + 1) * D], (2 * q + j) * P
                        for k in range(KF):
                            ins = mm(dst, ff[:, k, col:col + P], wf2[:, k, :], start=(k == 0), stop=(k == KF - 1))
                    ins.then_inc(r_done.sem, 1)

            t.wait_ge(wo_in, 16)
            out_proj(0, 0)
            t.wait_ge(w_in, NW)
            with t.Fori(0, NCH // 2 - 1) as i:
                for p in range(2):
                    chunk(i, p)
            chunk(NCH // 2 - 1, 0)
            chunk(NCH // 2 - 1, 1, last=True)


SCRATCH = {
    "xn": (T, D), "xnT": (NCH, P, KD, CH), "xhT": (NCH, P, KD, CH), "sz": (NCH, G, P, CH), "xc": (NCH, G, P, CH),
    "bc": (NCH, 2 * NS, CH), "dt": (NCH, G, P, CH), "dtx": (NCH, G, P, CH),
    "ys": (T, D), "slot_x": (NSLOT, D), "slot_y": (NSLOT, D), "y": (NCH, G, P, CH),
}
DEBUG = False


def build(nc, d):
    for name, shape in SCRATCH.items():
        d[name] = nc.dram_tensor(f"{name}_dram", shape, F32, kind="ExternalOutput" if DEBUG else "Internal").ap()
    d["moe_b"] = nc.dram_tensor("moe_b_dram", (E, 3, 2 * F + D), BF16, kind="Internal").ap()
    with ExitStack() as ctx:
        def sb(name, shape, dt=F32):
            return ctx.enter_context(nc.sbuf_tensor(name, shape, dt))

        wts = sb("wts", [P, TOPK, NT])
        slotf = sb("slotf", [P, TOPK, NT])
        block_e = sb("block_e", [1, NBLK], I32)
        idx_all = sb("idx_all", [P, NCH, TOPK, TPC], U32)
        scores = ExitStack()
        logits = scores.enter_context(nc.sbuf_tensor("logits", [P, NT, EP], F32, side="right"))
        with ExitStack() as experts:
            w1 = experts.enter_context(nc.sbuf_tensor("w1", [P, E * KD, 2 * F], F32))
            w2 = experts.enter_context(nc.sbuf_tensor("w2", [P, E * KD, D], F32))
            with ExitStack() as head:
                consts = [(head.enter_context(nc.sbuf_tensor(f"hw_{name}", shape, F32)), name) for name, shape in (
                    ("in_proj_w", [P, KD, 2 * DI]), ("x_proj_w", [P, G, XP]), ("dt_proj_w", [RK, DI]),
                    ("conv_w", [P, G, CONV]), ("inner_bias", [P, 2, G]), ("tri", [P, P]), ("ones", [P, P]),
                    ("rev", [P, NT, EP]), ("geglu_mult", [P, E * KD]))]
                with ExitStack() as inner:
                    gate_phase(nc, inner, d, logits, consts)
                with ExitStack() as inner:
                    head_phase(nc, inner, d, [t for t, _ in consts], logits, wts, block_e, slotf, idx_all, w1, w2)
            scores.close()
            with ExitStack() as inner:
                scan_phase(nc, inner, d, block_e, w1, w2)
        with ExitStack() as inner:
            tail_phase(nc, inner, d, wts, idx_all)


def arrange(inputs):
    a = {k: np.asarray(v) for k, v in inputs.items()}
    m, f = (lambda n: a["L0_attn_" + n]), (lambda n: a["L0_ffn_" + n])
    rows = lambda w: w.reshape(-1, P, w.shape[-1]).transpose(1, 0, 2)
    cols = lambda v: v.reshape(-1, P).T
    out = {
        "x": m("x").reshape(T, D),
        "in_proj_w": rows(m("in_proj_w")), "x_proj_w": rows(m("x_proj_w")), "dt_proj_w": m("dt_proj_w"),
        "gate_w": rows(f("gate_w").T), "conv_w": m("conv_w").reshape(G, P, CONV).transpose(1, 0, 2),
        "ln1": np.stack([cols(m("ln1_g")), cols(m("ln1_b"))], 1),
        "inner_bias": np.stack([cols(m("conv_b")), cols(m("dt_proj_b"))], 1),
        "ident": np.eye(P, dtype=np.float32),
        "tri": np.triu(np.ones((P, P), np.float32), 1), "ones": np.ones((P, P), np.float32),
        "rev": np.broadcast_to(np.float32(EP) - np.arange(EP, dtype=np.float32), (P, NT, EP)),
        "blk": np.broadcast_to(np.arange(NBLK, dtype=np.float32)[:, None], (1, NBLK, EP)),
        "sel": np.kron(np.eye(BPI, dtype=np.float32), np.ones((3, P), np.float32)),
        "fc1_w": f("fc1_w").reshape(E, 2 * F, KD, P).transpose(3, 0, 2, 1).reshape(P, E * KD, 2 * F),
        "fc2_w": f("fc2_w").reshape(E, D, F // P, P).transpose(3, 0, 2, 1).reshape(P, E * KD, D),
        "fc1_b": f("fc1_b"), "fc2_b": f("fc2_b"),
        "geglu_mult": f("geglu_mult").reshape(E * KD, P).T,
        "out_proj_w": rows(m("out_proj_w")), "ffn_w1": rows(m("ffn_w1")), "ffn_w2": rows(m("ffn_w2")),
        "s_fc1_w": rows(f("s_fc1_w").T), "s_fc2_w": rows(f("s_fc2_w").T), "s_mult": cols(f("s_geglu_mult")),
        "ffn_b1": cols(m("ffn_b1")), "s_fc1_b": cols(f("s_fc1_b")),
        "ffn_b2": m("ffn_b2").reshape(1, D), "s_fc2_b": f("s_fc2_b").reshape(1, D),
        "ln2": np.stack([cols(m("ln2_g")), cols(m("ln2_b"))], 1),
        "A_log": m("A_log").reshape(G, P, NS).transpose(1, 0, 2), "D": cols(m("D")),
    }
    return {k: np.ascontiguousarray(v) for k, v in out.items()}


def kernel(**inputs):
    import concourse.bacc as bacc
    from concourse.bass_utils import run_bass_kernel_spmd

    nc = bacc.Bacc("TRN2", target_bir_lowering=False, num_devices=1)
    arrays = arrange(inputs)
    d = {n: nc.dram_tensor(n + "_in", a.shape, mybir.dt.from_np(a.dtype), kind="ExternalInput").ap()
         for n, a in arrays.items()}
    d["out"] = nc.dram_tensor("out", (T, D), F32, kind="ExternalOutput").ap()
    build(nc, d)
    r = run_bass_kernel_spmd(nc, [{n + "_in": a for n, a in arrays.items()}], core_ids=[0])
    return r.results[0]["out"].reshape(B, L, D)
```
